# Optimizing a Trainium2 kernel written in Bass

```python
import numpy as np
import jax
import jax.numpy as jnp

def _softmax(x, axis=-1):
    return jax.nn.softmax(x, axis=axis)
def _gelu(x):
    return jax.nn.gelu(x, approximate=True)
def _silu(x):
    return jax.nn.silu(x)
def _sigmoid(x):
    return jax.nn.sigmoid(x)
def _layernorm(x, axis=-1, eps=1e-5):
    m = jnp.mean(x, axis=axis, keepdims=True)
    v = jnp.var(x, axis=axis, keepdims=True)
    return (x - m) / jnp.sqrt(v + eps)
def _scatter_add(tgt, idx, src, axis=0):
    return tgt.at[idx].add(src)
def _segment_sum(src, seg, n):
    return jax.ops.segment_sum(src, seg, n)

kernel_name = 'mk_conv_preact_d4_conv_nchw256_cc99a4'

def setup_inputs(seed: int = 0):
    np.random.seed(seed)
    _w = jnp.asarray
    def _rec_inputs():
        import jax
        import jax.numpy as jnp
        _gk = jax.random.key(seed)
        x = -0.0002928 + 1 * jax.random.normal(jax.random.fold_in(_gk, 1), (4, 256, 64, 64), jnp.float32)
        return x
    x = _rec_inputs()
    def _L0_conv_setup():
        import jax, jax.numpy as jnp
        import numpy as np
        K = 3
        STRIDE = 1
        PAD = 1

        def _dcn(x, w_off, b_off, dcn_weight):
            k, s, p = (K, STRIDE, PAD)
            N, C, H, W = x.shape
            outC = dcn_weight.shape[0]
            KK = k * k
            om = jax.lax.conv_general_dilated(x, w_off, (s, s), [(p, p), (p, p)], dimension_numbers=('NCHW', 'OIHW', 'NCHW')) + b_off[None, :, None, None]
            offset = om[:, :2 * KK]
            mask = jax.nn.sigmoid(om[:, 2 * KK:])
            oH = (H + 2 * p - (k - 1)) // s
            oW = (W + 2 * p - (k - 1)) // s
            px = jnp.pad(x, ((0, 0), (0, 0), (p, p + 1), (p, p + 1)))
            px = jnp.transpose(px, (0, 2, 3, 1))
            offset = jnp.transpose(offset, (0, 2, 3, 1)).reshape(N, oH, oW, KK, 2)
            mask = jnp.transpose(mask, (0, 2, 3, 1))
            base_y = jnp.arange(oH, dtype=jnp.float32) * s + p
            base_x = jnp.arange(oW, dtype=jnp.float32) * s + p
            half = (k - 1) // 2
            inner_y = jnp.repeat(jnp.arange(k, dtype=jnp.float32) - half, k)
            inner_x = jnp.tile(jnp.arange(k, dtype=jnp.float32) - half, k)
            pos_y = base_y[None, :, None, None] + inner_y[None, None, None, :] + offset[..., 0]
            pos_x = base_x[None, None, :, None] + inner_x[None, None, None, :] + offset[..., 1]
            pos_y = jnp.clip(pos_y, 0.0, H + 2 * p - 1.0)
            pos_x = jnp.clip(pos_x, 0.0, W + 2 * p - 1.0)
            y1 = jnp.floor(pos_y)
            x1 = jnp.floor(pos_x)
            y1i = y1.astype(jnp.int32)
            x1i = x1.astype(jnp.int32)
            nidx = jnp.arange(N)[:, None, None, None]
            v1 = px[nidx, y1i, x1i]
            v2 = px[nidx, y1i, x1i + 1]
            v3 = px[nidx, y1i + 1, x1i]
            v4 = px[nidx, y1i + 1, x1i + 1]
            lh = (pos_y - y1)[..., None]
            lw = (pos_x - x1)[..., None]
            hh = 1.0 - lh
            hw = 1.0 - lw
            value = hh * hw * v1 + hh * lw * v2 + lh * hw * v3 + lh * lw * v4
            value = value * mask[..., None]
            w = dcn_weight.reshape(outC, C, KK)
            out = jnp.einsum('nhwkc,ock->nohw', value, w)
            return out
        key = jax.random.key(seed)
        k1, k2, k3 = jax.random.split(key, 3)
        N, C, H, W = (4, 256, 64, 64)
        outC = 256
        x = jax.random.normal(k1, (N, C, H, W), dtype=jnp.float32)
        conv_offset_w = jax.random.normal(k2, (3 * K * K, C, K, K), dtype=jnp.float32) * 0.01
        conv_offset_b = jnp.zeros((3 * K * K,), dtype=jnp.float32)
        fan = C * K * K + outC * K * K
        dcn_weight = jax.random.normal(k3, (outC, C, K, K), dtype=jnp.float32) * np.float32(np.sqrt(2.0 / fan))
        return {'x': x, 'conv_offset_w': conv_offset_w, 'conv_offset_b': conv_offset_b, 'dcn_weight': dcn_weight}
    _L0_conv_all = _L0_conv_setup()
    _L0_conv_in = {k: v for k, v in _L0_conv_all.items() if k in ('conv_offset_w', 'conv_offset_b', 'dcn_weight', )}
    del _L0_conv_all

    def _L1_conv_setup():
        import jax, jax.numpy as jnp
        import numpy as np
        B, C, H, W = (16, 256, 64, 64)
        HEADS, DIM_HEAD = (8, 64)
        HIDDEN = HEADS * DIM_HEAD
        SCALE = DIM_HEAD ** (-0.5)
        EPS = 1e-12

        def rms_norm(x, g):
            n = jnp.sqrt(jnp.sum(x * x, axis=1, keepdims=True))
            return x / jnp.maximum(n, EPS) * g * x.shape[1] ** 0.5
        key = jax.random.key(seed)
        ks = jax.random.split(key, 5)
        x = jax.random.normal(ks[0], (B, C, H, W), dtype=jnp.float32)
        g_norm = jnp.ones((1, C, 1, 1), dtype=jnp.float32)
        w_qkv = jax.random.normal(ks[1], (3 * HIDDEN, C), dtype=jnp.float32) * C ** (-0.5)
        w_out = jax.random.normal(ks[2], (C, HIDDEN), dtype=jnp.float32) * HIDDEN ** (-0.5)
        b_out = jax.random.normal(ks[3], (C,), dtype=jnp.float32) * 0.01
        g_out = jnp.ones((1, C, 1, 1), dtype=jnp.float32)
        return {'x': x, 'g_norm': g_norm, 'w_qkv': w_qkv, 'w_out': w_out, 'b_out': b_out, 'g_out': g_out}
    _L1_conv_all = _L1_conv_setup()
    _L1_conv_in = {k: v for k, v in _L1_conv_all.items() if k in ('g_norm', 'w_qkv', 'w_out', 'b_out', 'g_out', )}
    del _L1_conv_all

    def _L2_conv_setup():
        import jax, jax.numpy as jnp
        import numpy as np
        from jax import lax
        BN_EPS = 0.001
        K = 7
        GROUPS = 16
        GC = 16

        def _conv1x1(x, w):
            return jnp.einsum('bchw,oc->bohw', x, w)

        def _bn(x, gamma, beta, mean, var):
            scale = (gamma / jnp.sqrt(var + BN_EPS))[None, :, None, None]
            shift = (beta - mean * gamma / jnp.sqrt(var + BN_EPS))[None, :, None, None]
            return x * scale + shift

        def _aconc(x, p1, p2, beta):
            p1 = p1[None, :, None, None]
            p2 = p2[None, :, None, None]
            beta = beta[None, :, None, None]
            d = (p1 - p2) * x
            return d * jax.nn.sigmoid(beta * d) + p2 * x
        key = jax.random.key(seed)
        ks = jax.random.split(key, 16)
        f = jnp.float32
        c1, mid, w2o = (256, 64, K * K * GROUPS)
        return {'x': jax.random.normal(ks[0], (4, c1, 56, 56), f), 'w1': jax.random.normal(ks[1], (mid, c1), f) * 0.05, 'bn1_gamma': jax.random.uniform(ks[2], (mid,), f, 0.5, 1.5), 'bn1_beta': jax.random.normal(ks[3], (mid,), f) * 0.1, 'bn1_mean': jax.random.normal(ks[4], (mid,), f) * 0.1, 'bn1_var': jax.random.uniform(ks[5], (mid,), f, 0.5, 1.5), 'acon_p1': jax.random.normal(ks[6], (mid,), f), 'acon_p2': jax.random.normal(ks[7], (mid,), f), 'acon_beta': jnp.ones((mid,), f), 'w2': jax.random.normal(ks[8], (w2o, mid), f) * 0.05, 'bn2_gamma': jax.random.uniform(ks[9], (w2o,), f, 0.5, 1.5), 'bn2_beta': jax.random.normal(ks[10], (w2o,), f) * 0.1, 'bn2_mean': jax.random.normal(ks[11], (w2o,), f) * 0.1, 'bn2_var': jax.random.uniform(ks[12], (w2o,), f, 0.5, 1.5)}
    _L2_conv_all = _L2_conv_setup()
    _L2_conv_in = {k: v for k, v in _L2_conv_all.items() if k in ('w1', 'bn1_gamma', 'bn1_beta', 'bn1_mean', 'bn1_var', 'acon_p1', 'acon_p2', 'acon_beta', 'w2', 'bn2_gamma', 'bn2_beta', 'bn2_mean', 'bn2_var', )}
    del _L2_conv_all

    def _L3_conv_setup():
        import jax, jax.numpy as jnp
        import numpy as np
        from jax import lax
        B, C, H, W = (8, 256, 128, 128)
        KS = 4
        key = jax.random.key(seed)
        x = jax.random.normal(key, (B, C, H, W), dtype=jnp.float32)
        k1 = jnp.array([1.0, 3.0, 3.0, 1.0], dtype=jnp.float32)
        k2 = jnp.outer(k1, k1)
        k2 = k2 / k2.sum() * 4.0
        filt = jnp.broadcast_to(k2[None, None, :, :], (C, 1, KS, KS)).astype(jnp.float32)
        return {'x': x, 'filt': filt}
    _L3_conv_all = _L3_conv_setup()
    _L3_conv_in = {k: v for k, v in _L3_conv_all.items() if k in ('filt', )}
    del _L3_conv_all

    return {
        "x": x,
        "L0_conv_conv_offset_w": _L0_conv_in["conv_offset_w"],
        "L0_conv_conv_offset_b": _L0_conv_in["conv_offset_b"],
        "L0_conv_dcn_weight": _L0_conv_in["dcn_weight"],
        "L1_conv_g_norm": _L1_conv_in["g_norm"],
        "L1_conv_w_qkv": _L1_conv_in["w_qkv"],
        "L1_conv_w_out": _L1_conv_in["w_out"],
        "L1_conv_b_out": _L1_conv_in["b_out"],
        "L1_conv_g_out": _L1_conv_in["g_out"],
        "L2_conv_w1": _L2_conv_in["w1"],
        "L2_conv_bn1_gamma": _L2_conv_in["bn1_gamma"],
        "L2_conv_bn1_beta": _L2_conv_in["bn1_beta"],
        "L2_conv_bn1_mean": _L2_conv_in["bn1_mean"],
        "L2_conv_bn1_var": _L2_conv_in["bn1_var"],
        "L2_conv_acon_p1": _L2_conv_in["acon_p1"],
        "L2_conv_acon_p2": _L2_conv_in["acon_p2"],
        "L2_conv_acon_beta": _L2_conv_in["acon_beta"],
        "L2_conv_w2": _L2_conv_in["w2"],
        "L2_conv_bn2_gamma": _L2_conv_in["bn2_gamma"],
        "L2_conv_bn2_beta": _L2_conv_in["bn2_beta"],
        "L2_conv_bn2_mean": _L2_conv_in["bn2_mean"],
        "L2_conv_bn2_var": _L2_conv_in["bn2_var"],
        "L3_conv_filt": _L3_conv_in["filt"],
    }

def reference(x, L0_conv_conv_offset_w, L0_conv_conv_offset_b, L0_conv_dcn_weight, L1_conv_g_norm, L1_conv_w_qkv, L1_conv_w_out, L1_conv_b_out, L1_conv_g_out, L2_conv_w1, L2_conv_bn1_gamma, L2_conv_bn1_beta, L2_conv_bn1_mean, L2_conv_bn1_var, L2_conv_acon_p1, L2_conv_acon_p2, L2_conv_acon_beta, L2_conv_w2, L2_conv_bn2_gamma, L2_conv_bn2_beta, L2_conv_bn2_mean, L2_conv_bn2_var, L3_conv_filt):
    import jax
    import jax.numpy as jnp
    def _L0_conv_ref(x, conv_offset_w, conv_offset_b, dcn_weight):
        import jax, jax.numpy as jnp
        import numpy as np
        K = 3
        STRIDE = 1
        PAD = 1

        def _dcn(x, w_off, b_off, dcn_weight):
            k, s, p = (K, STRIDE, PAD)
            N, C, H, W = x.shape
            outC = dcn_weight.shape[0]
            KK = k * k
            om = jax.lax.conv_general_dilated(x, w_off, (s, s), [(p, p), (p, p)], dimension_numbers=('NCHW', 'OIHW', 'NCHW')) + b_off[None, :, None, None]
            offset = om[:, :2 * KK]
            mask = jax.nn.sigmoid(om[:, 2 * KK:])
            oH = (H + 2 * p - (k - 1)) // s
            oW = (W + 2 * p - (k - 1)) // s
            px = jnp.pad(x, ((0, 0), (0, 0), (p, p + 1), (p, p + 1)))
            px = jnp.transpose(px, (0, 2, 3, 1))
            offset = jnp.transpose(offset, (0, 2, 3, 1)).reshape(N, oH, oW, KK, 2)
            mask = jnp.transpose(mask, (0, 2, 3, 1))
            base_y = jnp.arange(oH, dtype=jnp.float32) * s + p
            base_x = jnp.arange(oW, dtype=jnp.float32) * s + p
            half = (k - 1) // 2
            inner_y = jnp.repeat(jnp.arange(k, dtype=jnp.float32) - half, k)
            inner_x = jnp.tile(jnp.arange(k, dtype=jnp.float32) - half, k)
            pos_y = base_y[None, :, None, None] + inner_y[None, None, None, :] + offset[..., 0]
            pos_x = base_x[None, None, :, None] + inner_x[None, None, None, :] + offset[..., 1]
            pos_y = jnp.clip(pos_y, 0.0, H + 2 * p - 1.0)
            pos_x = jnp.clip(pos_x, 0.0, W + 2 * p - 1.0)
            y1 = jnp.floor(pos_y)
            x1 = jnp.floor(pos_x)
            y1i = y1.astype(jnp.int32)
            x1i = x1.astype(jnp.int32)
            nidx = jnp.arange(N)[:, None, None, None]
            v1 = px[nidx, y1i, x1i]
            v2 = px[nidx, y1i, x1i + 1]
            v3 = px[nidx, y1i + 1, x1i]
            v4 = px[nidx, y1i + 1, x1i + 1]
            lh = (pos_y - y1)[..., None]
            lw = (pos_x - x1)[..., None]
            hh = 1.0 - lh
            hw = 1.0 - lw
            value = hh * hw * v1 + hh * lw * v2 + lh * hw * v3 + lh * lw * v4
            value = value * mask[..., None]
            w = dcn_weight.reshape(outC, C, KK)
            out = jnp.einsum('nhwkc,ock->nohw', value, w)
            return out
        return _dcn(x, conv_offset_w, conv_offset_b, dcn_weight)

    def _L1_conv_ref(x, g_norm, w_qkv, w_out, b_out, g_out):
        import jax, jax.numpy as jnp
        import numpy as np
        B, C, H, W = (16, 256, 64, 64)
        HEADS, DIM_HEAD = (8, 64)
        HIDDEN = HEADS * DIM_HEAD
        SCALE = DIM_HEAD ** (-0.5)
        EPS = 1e-12

        def rms_norm(x, g):
            n = jnp.sqrt(jnp.sum(x * x, axis=1, keepdims=True))
            return x / jnp.maximum(n, EPS) * g * x.shape[1] ** 0.5
        b, c, h, w = x.shape
        xn = rms_norm(x, g_norm)
        qkv = jnp.einsum('bchw,oc->bohw', xn, w_qkv)
        q, k, v = jnp.split(qkv, 3, axis=1)

        def to_heads(t):
            return t.reshape(b, HEADS, DIM_HEAD, h * w)
        q, k, v = (to_heads(q), to_heads(k), to_heads(v))
        q = jax.nn.softmax(q, axis=-2) * SCALE
        k = jax.nn.softmax(k, axis=-1)
        context = jnp.einsum('bhdn,bhen->bhde', k, v)
        out = jnp.einsum('bhde,bhdn->bhen', context, q)
        out = out.reshape(b, HIDDEN, h, w)
        out = jnp.einsum('bchw,oc->bohw', out, w_out) + b_out[None, :, None, None]
        return rms_norm(out, g_out)

    def _L2_conv_ref(x, w1, bn1_gamma, bn1_beta, bn1_mean, bn1_var, acon_p1, acon_p2, acon_beta, w2, bn2_gamma, bn2_beta, bn2_mean, bn2_var):
        import jax, jax.numpy as jnp
        import numpy as np
        from jax import lax
        BN_EPS = 0.001
        K = 7
        GROUPS = 16
        GC = 16

        def _conv1x1(x, w):
            return jnp.einsum('bchw,oc->bohw', x, w)

        def _bn(x, gamma, beta, mean, var):
            scale = (gamma / jnp.sqrt(var + BN_EPS))[None, :, None, None]
            shift = (beta - mean * gamma / jnp.sqrt(var + BN_EPS))[None, :, None, None]
            return x * scale + shift

        def _aconc(x, p1, p2, beta):
            p1 = p1[None, :, None, None]
            p2 = p2[None, :, None, None]
            beta = beta[None, :, None, None]
            d = (p1 - p2) * x
            return d * jax.nn.sigmoid(beta * d) + p2 * x
        b, c, H, W = x.shape
        y = _aconc(_bn(_conv1x1(x, w1), bn1_gamma, bn1_beta, bn1_mean, bn1_var), acon_p1, acon_p2, acon_beta)
        weight = _bn(_conv1x1(y, w2), bn2_gamma, bn2_beta, bn2_mean, bn2_var)
        h, w = (weight.shape[2], weight.shape[3])
        weight = weight.reshape(b, GROUPS, 1, K * K, h, w)
        pad = (K - 1) // 2
        patches = lax.conv_general_dilated_patches(x, (K, K), (1, 1), [(pad, pad), (pad, pad)], dimension_numbers=('NCHW', 'OIHW', 'NCHW'))
        patches = patches.reshape(b, GROUPS, GC, K * K, h, w)
        out = (weight * patches).sum(axis=3)
        return out.reshape(b, c, h, w)

    def _L3_conv_ref(x, filt):
        import jax, jax.numpy as jnp
        import numpy as np
        from jax import lax
        B, C, H, W = (8, 256, 128, 128)
        KS = 4
        k = filt.shape[-1]
        c = x.shape[1]
        pad = k - 2
        p0 = (pad + 1) // 2
        p1 = pad // 2
        return lax.conv_general_dilated(x, filt, window_strides=(2, 2), padding=((p0, p1 + 1), (p0, p1 + 1)), lhs_dilation=(2, 2), dimension_numbers=('NCHW', 'OIHW', 'NCHW'), feature_group_count=c)

    def _gn(v, G=32, eps=1e-5):
        B_, C_, H_, W_ = v.shape
        g = v.reshape(B_, G, C_ // G, H_, W_)
        m = jnp.mean(g, axis=(2, 3, 4), keepdims=True)
        s = jnp.var(g, axis=(2, 3, 4), keepdims=True)
        return ((g - m) / jnp.sqrt(s + eps)).reshape(v.shape)

    def _ln_c(v, eps=1e-6):
        m = jnp.mean(v, axis=1, keepdims=True)
        s = jnp.var(v, axis=1, keepdims=True)
        return (v - m) / jnp.sqrt(s + eps)

    def _ln_t(v, eps=1e-5):
        m = jnp.mean(v, axis=-1, keepdims=True)
        s = jnp.var(v, axis=-1, keepdims=True)
        return (v - m) / jnp.sqrt(s + eps)

    def _to_tokens(v):
        B_, C_, H_, W_ = v.shape
        return v.reshape(B_, C_, H_ * W_).transpose(0, 2, 1)
    def _from_tokens(t, like):
        B_, C_, H_, W_ = like.shape
        return t.transpose(0, 2, 1).reshape(B_, C_, H_, W_)

    x = x + _L0_conv_ref(_gn(x), L0_conv_conv_offset_w, L0_conv_conv_offset_b, L0_conv_dcn_weight)
    x = x + _L1_conv_ref(_gn(x), L1_conv_g_norm, L1_conv_w_qkv, L1_conv_w_out, L1_conv_b_out, L1_conv_g_out)
    x = x + _L2_conv_ref(_gn(x), L2_conv_w1, L2_conv_bn1_gamma, L2_conv_bn1_beta, L2_conv_bn1_mean, L2_conv_bn1_var, L2_conv_acon_p1, L2_conv_acon_p2, L2_conv_acon_beta, L2_conv_w2, L2_conv_bn2_gamma, L2_conv_bn2_beta, L2_conv_bn2_mean, L2_conv_bn2_var)
    x = x + _L3_conv_ref(_gn(x), L3_conv_filt)
    return x


_drawn_inputs = setup_inputs


def setup_inputs(seed=0):
    import zlib

    import numpy as np

    out = dict(_drawn_inputs(seed))
    spreads = {'L0_conv_conv_offset_b': (0.0, 0.1),
     'L1_conv_g_norm': (1.0, 0.2),
     'L1_conv_g_out': (1.0, 0.2),
     'L2_conv_acon_beta': (1.0, 0.2)}
    factors = {}
    for name, (base, spread) in spreads.items():
        noise = np.random.default_rng([zlib.crc32(name.encode()), seed]).standard_normal(out[name].shape)
        drawn = base * np.exp(spread * noise) if base else spread * noise
        out[name] = jnp.asarray(drawn.astype(out[name].dtype))
    for name, factor in factors.items():
        out[name] = (out[name] * factor).astype(out[name].dtype)
    return out
```

```python
from contextlib import ExitStack

import concourse.bass as bass
from concourse import mybir

ALU = mybir.AluOpType
ACT = mybir.ActivationFunctionType
AX_X = mybir.AxisListType.X
F32 = mybir.dt.float32
I32 = mybir.dt.int32
U32 = mybir.dt.uint32

P = 128
IMAGES = 4
C = 256
CH = C // P
HW = 64
PIX = HW * HW
TILE_ROWS = P // HW
TILES = PIX // P
GROUP = 4
GPIX = GROUP * P
GROUPS = TILES // GROUP
GN_CH = 8
GN_EPS = 1e-5

KK = 9
PADW = HW + 3
POS = PADW * PADW
POS_TILES = -(-POS // (GROUP * P)) * GROUP
POS_PAD = POS_TILES * P
QUAD = (0, 1, PADW, PADW + 1)
QBASE = PADW + 1
QROWS = POS_PAD + QBASE
STEPS = KK * GROUP

HEADS, DH = 8, 64
HID = HEADS * DH
PAIRS = HID // P
RMS_EPS = 1e-12

MID = 64
K7 = 7
TAPS = K7 * K7
G2 = 16
GC = C // G2
BN_EPS = 1e-3
BY, BX = 2, 8
WY, WX = BY + K7 - 1, BX + K7 - 1
WIN = WY * WX
BPIX = BY * BX
PAD2 = HW + K7 - 1
LEAD = 2 * WX
FLAT = LEAD + WIN
HALF_ROWS = HW // 2
BLOCKS = (HALF_ROWS // BY) * (HW // BX)
BCOLS = HW // BX


class Chain:

    def __init__(self, eng, sem, base=0):
        self.eng, self.sem, self.base, self.n = eng, sem, base, 0

    def value(self):
        return self.base + self.n

    def add(self, ins):
        self.n += 1
        ins.then_inc(self.sem, 1)

    def link(self, ins):
        self.add(ins)
        self.eng.wait_ge(self.sem, self.value())


class Alloc:
    def __init__(self, nc, ctx, tag):
        self.nc, self.ctx, self.tag = nc, ctx, tag

    def sb(self, name, shape, dt=F32):
        return self.ctx.enter_context(self.nc.sbuf_tensor(self.tag + name, shape, dt))

    def ps(self, name, shape):
        return self.ctx.enter_context(self.nc.psum_tensor(self.tag + name, shape, F32))

    def sem(self, name):
        return self.ctx.enter_context(self.nc.semaphore(self.tag + name))


def group_average_matrix(nc, pool, chain, avg):
    chain.link(nc.gpsimd.memset(avg[:], 1.0 / GN_CH))
    view = avg[:].rearrange("p (g c) -> p g c", c=GN_CH)
    chain.link(nc.gpsimd.affine_select(out=view, in_=view, compare_op=ALU.is_ge, fill=0.0, base=0,
                                       pattern=[[-GN_CH, P // GN_CH], [0, GN_CH]], channel_multiplier=1))
    chain.link(nc.gpsimd.affine_select(out=view, in_=view, compare_op=ALU.is_ge, fill=0.0, base=GN_CH - 1,
                                       pattern=[[GN_CH, P // GN_CH], [0, GN_CH]], channel_multiplier=-1))


def identity_matrix(nc, pool, chain, ident):
    chain.link(nc.gpsimd.memset(ident[:], 0.0))
    chain.link(nc.gpsimd.affine_select(out=ident[:], in_=ident[:], compare_op=ALU.not_equal, fill=1.0, base=0,
                                       pattern=[[-1, P]], channel_multiplier=1))




class GroupNorm:

    def __init__(self, a):
        self.stats = a.sb("gn_stats", [P, CH, GROUPS, 6])
        self.mv = a.sb("gn_mv", [P, CH, 2])
        self.mom = a.sb("gn_mom", [P, CH, 2])
        self.gm = a.sb("gn_gm", [P, CH, 2])
        self.var = a.sb("gn_var", [P, CH])
        self.std = a.sb("gn_std", [P, CH])
        self.scale = a.sb("gn_scale", [P, CH])
        self.shift = a.sb("gn_shift", [P, CH])
        self.passed = a.sem("gn_passed")
        self.moments = a.sem("gn_moments")
        self.averaged = a.sem("gn_averaged")
        self.variance = a.sem("gn_variance")
        self.root = a.sem("gn_root")
        self.ready = a.sem("gn_ready")

    def dve(self, nc, dve, chain, n, x, ps, lax=False):
        for h in range(CH):
            for g in range(GROUPS):
                chain.add(nc.vector.bn_stats(self.stats[:, h, g, :], x[:, h, g * GPIX:(g + 1) * GPIX]))
        dve.wait_ge(chain.sem, chain.value())
        dve.sem_inc(self.passed, 1)
        for h in range(CH):
            chain.add(nc.vector.bn_aggr(self.mv[:, h, :], self.stats[:, h, :, :].rearrange("p g s -> p (g s)")))
        dve.wait_ge(chain.sem, chain.value())
        self.dve_rest(nc, dve, chain, n, ps)

    def dve_rest(self, nc, dve, chain, n, ps):
        chain.link(nc.vector.tensor_tensor(self.mom[:, :, 1], self.mv[:, :, 0], self.mv[:, :, 0], ALU.mult))
        nc.vector.tensor_tensor(self.mom[:, :, 1], self.mom[:, :, 1], self.mv[:, :, 1], ALU.add).then_inc(self.moments, 1)
        nc.vector.tensor_copy(self.mom[:, :, 0], self.mv[:, :, 0]).then_inc(self.moments, 1)
        dve.wait_ge(self.averaged, n + 1)
        chain.link(nc.vector.tensor_copy(self.gm[:].rearrange("p h s -> p (h s)"), ps))
        chain.link(nc.vector.tensor_tensor(self.var[:], self.gm[:, :, 0], self.gm[:, :, 0], ALU.mult))
        chain.link(nc.vector.tensor_tensor(self.var[:], self.gm[:, :, 1], self.var[:], ALU.subtract))
        nc.vector.tensor_scalar(self.var[:], self.var[:], GN_EPS, None, ALU.add).then_inc(self.variance, 1)
        dve.wait_ge(self.root, n + 1)
        chain.link(nc.vector.reciprocal(self.scale[:], self.std[:]))
        chain.link(nc.vector.tensor_tensor(self.shift[:], self.gm[:, :, 0], self.scale[:], ALU.mult))
        nc.vector.tensor_scalar(self.shift[:], self.shift[:], -1.0, None, ALU.mult).then_inc(self.ready, 1)
        dve.wait_ge(self.ready, n + 1)

    def pe(self, nc, pe, n, avg, ps):
        pe.wait_ge(self.moments, 2 * (n + 1))
        nc.tensor.matmul(ps, avg[:], self.mom[:].rearrange("p h s -> p (h s)"), start=True, stop=True).then_inc(self.averaged, 1)

    def act(self, nc, act, n):
        act.wait_ge(self.variance, n + 1)
        nc.scalar.activation(self.std[:], self.var[:], ACT.Sqrt).then_inc(self.root, 1)


def stage_offsets(nc, D, avg, ident, all_idx, all_wt):
    with ExitStack() as ctx:
        a = Alloc(nc, ctx, "o_")
        x = a.sb("x", [P, CH, PIX])
        xp = a.sb("xp", [P, CH, POS_PAD])
        w_off = a.sb("w_off", [P, CH, KK, 3 * KK])
        b_off = a.sb("b_off", [3 * KK, 1])
        quad = a.sb("quad", [P, 2, GROUP, C])
        om_c = a.sb("om_c", [3 * KK, 2, GPIX])
        om = a.sb("om", [P, TILES, 3 * KK])
        mask = a.sb("mask", [P, TILES, KK])
        grid = a.sb("grid", [P, 2, TILES * KK])
        pos = a.sb("pos", [P, 2, TILES * KK])
        pos_i = a.sb("pos_i", [P, 2, TILES * KK], I32)
        low = a.sb("low", [P, 2, TILES * KK])
        frac = a.sb("frac", [P, 2, TILES * KK])
        rest = a.sb("rest", [P, 2, TILES * KK])
        over = a.sb("over", [P, 2, TILES * KK])
        row = a.sb("row", [P, TILES * KK])
        base = a.sb("base", [P, 1])
        zero = a.sb("zero", [QBASE, C])
        gn = GroupNorm(a)
        tp = a.ps("tp", [P, 2, 2, 512])
        cv = a.ps("cv", [P, 2, 512])
        ot = a.ps("ot", [P, 512])
        gp = a.ps("gp", [P, 512])
        w_loaded = a.sem("w_loaded")
        x_loaded = a.sem("x_loaded")
        const = a.sem("const")
        chain_sem = a.sem("chain")
        normalised = a.sem("normalised")
        transposed = a.sem("transposed")
        tp_free = a.sem("tp_free")
        quad_stored = [a.sem(f"quad_stored{b}") for b in range(2)]
        conv_done = a.sem("conv_done")
        om_c_ready = a.sem("om_c_ready")
        om_t = a.sem("om_t")
        om_ready = a.sem("om_ready")
        mask_ready = a.sem("mask_ready")
        passed = a.sem("passed")
        filled = a.sem("filled")
        BATCH = POS_TILES // GROUP
        DVE_STEPS = CH * GROUPS + CH + 6 + 12 + 5

        with nc.Block() as block:
            @block.sync
            def _(sp):
                sp.dma_start(w_off[:], D["w_off"]).then_inc(w_loaded, 16)
                sp.dma_start(b_off[:], D["b_off"]).then_inc(w_loaded, 16)
                sp.wait_ge(const, 7)
                with sp.Fori(0, IMAGES) as n:
                    for corner, off in enumerate(QUAD):
                        for first, rows in ((0, QBASE - off), (QROWS - off, off)):
                            if rows:
                                sp.dma_start(D["table"][bass.ds(n * QROWS + first, rows), corner * C:(corner + 1) * C],
                                             zero[0:rows]).then_inc(filled, 16)
                    sp.wait_ge(normalised, CH * n)
                    sp.dma_start(x[:], D["x"][n].rearrange("(h p) q -> p h q", p=P)).then_inc(x_loaded, 16)
                    for b in range(BATCH):
                        sp.wait_ge(tp_free, 2 * BATCH * n + 2 * (b + 1))
                        for corner, off in enumerate(QUAD):
                            first = QBASE - off + b * GPIX
                            dst = D["table"][bass.ds(n * QROWS + first, GPIX), corner * C:(corner + 1) * C]
                            sp.dma_start(dst.rearrange("(t p) c -> p t c", p=P), quad[:, b % 2]).then_inc(quad_stored[b % 2], 16)
                sp.wait_ge(filled, 16 * 6 * IMAGES)
                sp.wait_ge(quad_stored[0], 64 * IMAGES * -(-BATCH // 2))
                sp.wait_ge(quad_stored[1], 64 * IMAGES * (BATCH // 2))

            @block.gpsimd
            def _(pool):
                chain = Chain(pool, const)
                chain.link(nc.gpsimd.memset(xp[:], 0.0))
                for half in range(TILE_ROWS):
                    part = slice(half * HW, (half + 1) * HW)
                    for axis in range(2):
                        by = [[2 * GROUP, GROUPS], [1, 3], [0, 3], [2, GROUP]]
                        bx = [[0, GROUPS], [0, 3], [1, 3], [0, GROUP]]
                        chain.link(nc.gpsimd.iota(grid[part, axis, :].rearrange("p (g a b t) -> p g a b t", g=GROUPS, a=3, b=3),
                                       by if axis == 0 else bx, base=half if axis == 0 else 0,
                                       channel_multiplier=0 if axis == 0 else 1,
                                       allow_small_or_imprecise_dtypes=True))
                chain.link(nc.gpsimd.memset(base[:], float(QBASE)))
                chain.link(nc.gpsimd.memset(zero[:], 0.0))

            @block.vector
            def _(dve):
                dve.wait_ge(const, 7)
                with dve.Fori(0, IMAGES) as n:
                    chain = Chain(dve, chain_sem, n * DVE_STEPS)
                    dve.wait_ge(x_loaded, 16 * (n + 1))
                    gn.dve(nc, dve, chain, n, x, gp[:, 0:2 * CH])
                    dve.wait_ge(transposed, 2 * BATCH * n)
                    dve.wait_ge(conv_done, GROUPS * n)
                    inner = xp[:, 0, PADW + 1:PADW + 1 + HW * PADW].rearrange("p (r c) -> p r c", c=PADW)[:, :, 0:HW]
                    nc.vector.tensor_scalar(inner, x[:, 0].rearrange("p (r c) -> p r c", c=HW), gn.scale[:, 0:1],
                                            gn.shift[:, 0:1], ALU.mult, ALU.add).then_inc(normalised, 1)
                    for g in range(GROUPS):
                        dve.wait_ge(om_t, GROUPS * n + g + 1)
                        view = ot[:, (g % 2) * 128:(g % 2 + 1) * 128].rearrange("p (t m) -> p t m", t=GROUP)
                        nc.vector.tensor_copy(om[:, g * GROUP:(g + 1) * GROUP, :], view[:, :, 0:3 * KK]).then_inc(om_ready, 1)
                    dve.wait_ge(om_ready, GROUPS * (n + 1))
                    for axis in range(2):
                        for g in range(GROUPS):
                            sl = slice(g * STEPS, (g + 1) * STEPS)
                            off = om[:, g * GROUP:(g + 1) * GROUP, axis * KK:(axis + 1) * KK].rearrange("p t k -> p k t")
                            ins = nc.vector.tensor_tensor(pos[:, axis, sl].rearrange("p (k t) -> p k t", t=GROUP),
                                                          grid[:, axis, sl].rearrange("p (k t) -> p k t", t=GROUP), off, ALU.add)
                    chain.link(ins)
                    chain.link(nc.vector.tensor_scalar(pos[:], pos[:], 0.0, HW + 1.0, ALU.max, ALU.min))
                    chain.link(nc.vector.tensor_copy(pos_i[:], pos[:]))
                    chain.link(nc.vector.tensor_copy(low[:], pos_i[:]))
                    chain.link(nc.vector.tensor_tensor(over[:], low[:], pos[:], ALU.is_gt))
                    chain.link(nc.vector.tensor_tensor(low[:], low[:], over[:], ALU.subtract))
                    chain.link(nc.vector.tensor_tensor(frac[:], pos[:], low[:], ALU.subtract))
                    chain.link(nc.vector.tensor_scalar(rest[:], frac[:], -1.0, 1.0, ALU.mult, ALU.add))
                    chain.link(nc.vector.scalar_tensor_tensor(row[:], low[:, 0], float(PADW), low[:, 1], ALU.mult, ALU.add))
                    chain.link(nc.vector.tensor_scalar(row[:], row[:], base[:, 0:1], None, ALU.add))
                    chain.link(nc.vector.tensor_copy(all_idx[:, n, :], row[:]))
                    chain.link(nc.vector.tensor_scalar(base[:], base[:], float(QROWS), None, ALU.add))
                    dve.wait_ge(mask_ready, n + 1)
                    for g in range(GROUPS):
                        sl = slice(g * STEPS, (g + 1) * STEPS)
                        m = mask[:, g * GROUP:(g + 1) * GROUP, :].rearrange("p t k -> p k t")
                        for src in (frac, rest):
                            v = src[:, 0, sl].rearrange("p (k t) -> p k t", t=GROUP)
                            ins = nc.vector.tensor_tensor(v, v, m, ALU.mult)
                    chain.link(ins)
                    for corner, (wy, wx) in enumerate(((rest, rest), (rest, frac), (frac, rest), (frac, frac))):
                        chain.link(nc.vector.tensor_tensor(all_wt[:, n, corner, :], wy[:, 0], wx[:, 1], ALU.mult))
                    assert chain.n == DVE_STEPS, chain.n

            @block.scalar
            def _(act):
                act.wait_ge(w_loaded, 32)
                with act.Fori(0, IMAGES) as n:
                    gn.act(nc, act, n)
                    act.wait_ge(gn.ready, n + 1)
                    act.wait_ge(transposed, 2 * BATCH * n)
                    act.wait_ge(conv_done, GROUPS * n)
                    inner = xp[:, 1, PADW + 1:PADW + 1 + HW * PADW].rearrange("p (r c) -> p r c", c=PADW)[:, :, 0:HW]
                    nc.scalar.activation(inner, x[:, 1].rearrange("p (r c) -> p r c", c=HW), ACT.Identity,
                                         bias=gn.shift[:, 1:2], scale=gn.scale[:, 1:2]).then_inc(normalised, 1)

                    def offsets(g):
                        act.wait_ge(conv_done, GROUPS * n + g + 1)
                        if g >= 2:
                            act.wait_ge(om_t, GROUPS * n + g - 1)
                        nc.scalar.activation(om_c[:, g % 2, :], cv[0:3 * KK, g % 2, :], ACT.Identity, bias=b_off[:]).then_inc(om_c_ready, 1)

                    for b in range(BATCH):
                        even, odd = -(-BATCH // 2), BATCH // 2
                        act.wait_ge(quad_stored[b % 2], (n * (even, odd)[b % 2] + b // 2) * 64)
                        for half in range(2):
                            act.wait_ge(transposed, 2 * BATCH * n + 2 * b + half + 1)
                            nc.scalar.activation(quad[:, b % 2, 2 * half:2 * half + 2, :],
                                                 tp[:, half, :, 0:C], ACT.Copy).then_inc(tp_free, 1)
                        if b < GROUPS:
                            offsets(b)
                    act.wait_ge(om_ready, GROUPS * (n + 1))
                    nc.scalar.activation(mask[:], om[:, :, 2 * KK:3 * KK], ACT.Sigmoid).then_inc(mask_ready, 1)

            @block.tensor
            def _(pe):
                pe.wait_ge(w_loaded, 32)
                with pe.Fori(0, IMAGES) as n:
                    gn.pe(nc, pe, n, avg, gp[:, 0:2 * CH])
                    pe.wait_ge(normalised, CH * (n + 1))

                    def conv(g):
                        if g >= 2:
                            pe.wait_ge(om_c_ready, GROUPS * n + g - 1)
                        for tap in range(KK):
                            ky, kx = divmod(tap, 3)
                            for h in range(CH):
                                at = (g * GPIX // HW + ky) * PADW + kx
                                rows = xp[:, h, at:at + 8 * PADW].rearrange("p (r c) -> p r c", c=PADW)[:, :, 0:HW]
                                mm = nc.tensor.matmul(cv[0:3 * KK, g % 2, :], w_off[:, h, tap, :], rows,
                                                      start=(tap == 0 and h == 0), stop=(tap == KK - 1 and h == CH - 1))
                        mm.then_inc(conv_done, 1)

                    def turn(g):
                        pe.wait_ge(om_c_ready, GROUPS * n + g + 1)
                        pe.wait_ge(om_ready, GROUPS * n + g)
                        pe.sem_inc(passed, 1)
                        for t in range(GROUP):
                            col = (g % 2) * 128 + t * 32
                            mm = nc.tensor.transpose(ot[:, col:col + 3 * KK], om_c[:, g % 2, t * P:(t + 1) * P], ident[0:3 * KK, 0:3 * KK])
                        mm.then_inc(om_t, 1)

                    for b in range(BATCH):
                        for half in range(2):
                            pe.wait_ge(tp_free, (2 * BATCH * n + 2 * b + half - 1) if b else 2 * BATCH * n)
                            for t in range(2):
                                for h in range(CH):
                                    at = ((2 * b + half) * 2 + t) * P
                                    mm = nc.tensor.transpose(tp[:, half, t, h * P:(h + 1) * P], xp[:, h, at:at + P], ident[:])
                            mm.then_inc(transposed, 1)
                        if b < GROUPS:
                            conv(b)
                        if 1 <= b < GROUPS + 1:
                            turn(b - 1)


def stage_deform(nc, D, ident, all_idx, all_wt):
    SLOTS = 6
    with ExitStack() as ctx:
        a = Alloc(nc, ctx, "d_")
        w = a.sb("w", [P, CH, KK, C])
        ring = a.sb("ring", [P, SLOTS, 4 * C])
        idx = a.sb("idx", [P, STEPS], U32)
        wt = a.sb("wt", [P, 2, 4, STEPS])
        val = a.sb("val", [P, 4, C])
        val_c = a.sb("val_c", [P, 2, CH, GPIX])
        xres = a.sb("xres", [P, 2, CH, GPIX])
        tp = a.ps("tp", [P, 2, CH, GPIX])
        acc = a.ps("acc", [P, 2, CH, GPIX])
        w_loaded = a.sem("w_loaded")
        x_loaded = [a.sem(f"x_loaded{b}") for b in range(2)]
        gathered = [a.sem(f"gathered{s}") for s in range(SLOTS)]
        idx_ready = a.sem("idx_ready")
        passed = a.sem("passed")
        wt_ready = a.sem("wt_ready")
        first_ready = a.sem("first_ready")
        part = a.sem("part")
        value_ready = a.sem("value_ready")
        val_free = a.sem("val_free")
        val_c_ready = a.sem("val_c_ready")
        tap_done = a.sem("tap_done")
        stored = a.sem("stored")
        added = a.sem("added")
        RUNS = IMAGES * GROUPS // 2

        def dram(t, n, g):
            return t[n].rearrange("(h p) q -> p h q", p=P)[:, :, g * GPIX:(g + 1) * GPIX]

        with nc.Block() as block:
            @block.sync
            def _(sp):
                sp.dma_start(w[:], D["w_dcn"]).then_inc(w_loaded, 16)
                with sp.Fori(0, IMAGES) as n:
                    with sp.Fori(0, GROUPS // 2) as gg:
                        for b in range(2):
                            i = (n * (GROUPS // 2) + gg) * 2 + b
                            if True:
                                sp.wait_ge(stored, (n * (GROUPS // 2) + gg) * 32)
                            src = D["x"][n].rearrange("(h p) q -> p h q", p=P)[:, :, bass.ds((gg * 2 + b) * GPIX, GPIX)]
                            sp.dma_start(xres[:, b], src).then_inc(x_loaded[b], 16)
                        for b in range(2):
                            i = (n * (GROUPS // 2) + gg) * 2 + b
                            sp.wait_ge(added, CH * (i + 1))
                            dst = D["x1"][n].rearrange("(h p) q -> p h q", p=P)[:, :, bass.ds((gg * 2 + b) * GPIX, GPIX)]
                            sp.dma_start(dst, xres[:, b]).then_inc(stored, 16)
                sp.wait_ge(stored, 16 * IMAGES * GROUPS)

            @block.gpsimd
            def _(pool):
                with pool.Fori(0, IMAGES) as n:
                    with pool.Fori(0, GROUPS) as g:
                        i = n * GROUPS + g
                        for s in range(SLOTS):
                            pool.wait_ge(gathered[s], i * (16 * STEPS // SLOTS))
                        nc.gpsimd.tensor_copy(idx[:], all_idx[:, n, bass.ds(g * STEPS, STEPS)]).then_inc(idx_ready, 1)
                        pool.wait_ge(idx_ready, i + 1)
                        for s in range(STEPS):
                            pool.wait_ge(value_ready, (i * STEPS + s - SLOTS + 1) if s >= SLOTS else i * STEPS)
                            pool.sem_inc(passed, 1)
                            pool.indirect_dma_start(out=ring[:, s % SLOTS, :], out_offset=None, in_=D["table"],
                                                    in_offset=bass.IndirectOffsetOnAxis(ap=idx[:, s:s + 1], axis=0)
                                                    ).then_inc(gathered[s % SLOTS], 16)

            @block.scalar
            def _(act):
                with act.Fori(0, IMAGES) as n:
                    with act.Fori(0, GROUPS // 2) as gg:
                        for b in range(2):
                            i = (n * (GROUPS // 2) + gg) * 2 + b
                            act.wait_ge(wt_ready, i + 1)
                            for tap in range(KK + 1):
                                if tap < KK:
                                    for t in range(GROUP):
                                        s = tap * GROUP + t
                                        act.wait_ge(gathered[s % SLOTS], (i * (STEPS // SLOTS) + s // SLOTS + 1) * 16)
                                        act.wait_ge(val_free, (i * STEPS + s - 3) if s > 3 else i * STEPS)
                                        nc.scalar.activation(val[:, s % 4, :], ring[:, s % SLOTS, 0:C], ACT.Copy,
                                                             scale=wt[:, b, 0, s:s + 1]).then_inc(first_ready, 1)
                                if tap:
                                    k = tap - 1
                                    act.wait_ge(val_free, i * STEPS + (k + 1) * GROUP)
                                    act.wait_ge(tap_done, (i * KK + k - 1) if k > 1 else i * KK)
                                    nc.scalar.activation(val_c[:, (b * KK + k) % 2, :, :], tp[:, (b * KK + k) % 2, :, :], ACT.Copy).then_inc(val_c_ready, 1)

            @block.vector
            def _(dve):
                with dve.Fori(0, IMAGES) as n:
                    with dve.Fori(0, GROUPS // 2) as gg:
                        for b in range(2):
                            i = (n * (GROUPS // 2) + gg) * 2 + b
                            nc.vector.tensor_copy(wt[:, b], all_wt[:, n, :, bass.ds((gg * 2 + b) * STEPS, STEPS)]).then_inc(wt_ready, 1)
                            dve.wait_ge(wt_ready, i + 1)
                            for pair in range(STEPS // 2):
                                for corner in range(1, 4):
                                    for j in range(2):
                                        s = 2 * pair + j
                                        if corner == 1:
                                            dve.wait_ge(first_ready, i * STEPS + s + 1)
                                        else:
                                            dve.wait_ge(part, i * STEPS * 2 + pair * 4 + (corner - 2) * 2 + j + 1)
                                        ins = nc.vector.scalar_tensor_tensor(
                                            val[:, s % 4, :], ring[:, s % SLOTS, corner * C:(corner + 1) * C],
                                            wt[:, b, corner, s:s + 1], val[:, s % 4, :], ALU.mult, ALU.add)
                                        ins.then_inc(part if corner < 3 else value_ready, 1)
                                if pair == 4 or pair == 1:
                                    pass
                            dve.wait_ge(tap_done, KK * (i + 1))
                            dve.wait_ge(x_loaded[b], (n * (GROUPS // 2) + gg + 1) * 16)
                            for h in range(CH):
                                nc.vector.tensor_tensor(xres[:, b, h, :], xres[:, b, h, :], acc[:, b, h, :], ALU.add).then_inc(added, 1)

            @block.tensor
            def _(pe):
                pe.wait_ge(w_loaded, 16)
                with pe.Fori(0, IMAGES) as n:
                    with pe.Fori(0, GROUPS // 2) as gg:
                        for b in range(2):
                            i = (n * (GROUPS // 2) + gg) * 2 + b
                            pe.wait_ge(added, (n * (GROUPS // 2) + gg) * 4)
                            for tap in range(KK + 1):
                                if tap < KK:
                                    pe.wait_ge(val_c_ready, (i * KK + tap - 1) if tap > 1 else i * KK)
                                    for t in range(GROUP):
                                        s = tap * GROUP + t
                                        pe.wait_ge(value_ready, i * STEPS + s + 1)
                                        for h in range(CH):
                                            mm = nc.tensor.transpose(tp[:, (b * KK + tap) % 2, h, t * P:(t + 1) * P],
                                                                     val[:, s % 4, h * P:(h + 1) * P], ident[:])
                                        mm.then_inc(val_free, 1)
                                if tap:
                                    k = tap - 1
                                    pe.wait_ge(val_c_ready, i * KK + k + 1)
                                    for o in range(CH):
                                        for h in range(CH):
                                            mm = nc.tensor.matmul(acc[:, b, o, :], w[:, h, k, o * P:(o + 1) * P], val_c[:, (b * KK + k) % 2, h, :],
                                                                  start=(k == 0 and h == 0), stop=(k == KK - 1 and h == CH - 1),
                                                                  skip_group_check=True)
                                    mm.then_inc(tap_done, 1)


def stage_attention(nc, D, avg, ident):
    with ExitStack() as ctx:
        a = Alloc(nc, ctx, "a_")
        x = a.sb("x", [P, CH, PIX])
        keys = a.sb("keys", [P, TILES, HID])
        outs = keys[:].rearrange("p t d -> p (t d)")[:, 0:TILES * C].rearrange("p (t c) -> p t c", c=C)
        xs = a.sb("xs", [P, 2, CH, GPIX])
        w = a.sb("w", [P, CH, 3, HID])
        w_out = a.sb("w_out", [P, PAIRS, C])
        g_in = a.sb("g_in", [P, CH])
        g_out = a.sb("g_out", [P, CH])
        b_out = a.sb("b_out", [P, C])
        ones = a.sb("ones", [P, 1])
        zeros = a.sb("zeros", [P, HID])
        rinv = a.sb("rinv", [P, TILES])
        kmax = a.sb("kmax", [P, HID])
        mx = a.sb("mx", [P, PAIRS])
        mxb = a.sb("mxb", [P, PAIRS, P])
        kb = a.sb("kb", [P, HID])
        e = a.sb("e", [P, 2, HID])
        v = a.sb("v", [P, 2, HID])
        esum = a.sb("esum", [P, HID])
        rs = a.sb("rs", [P, PAIRS])
        cT = a.sb("cT", [P, PAIRS, P])
        mix = a.sb("mix", [P, PAIRS, C])
        q = a.sb("q", [P, 2, HID])
        qm = a.sb("qm", [P, 2, HEADS])
        qs = a.sb("qs", [P, 2, HEADS])
        qT = a.sb("qT", [P, 2, HID])
        sq = a.sb("sq", [P, C])
        osum = a.sb("osum", [P, TILES])
        oinv = a.sb("oinv", [P, TILES])
        y = a.sb("y", [P, 2, C])
        xo = a.sb("xo", [P, 2, CH, GPIX])
        gn = GroupNorm(a)
        proj = a.ps("proj", [P, 2, HID])
        small = a.ps("small", [P, 512])
        ctxp = a.ps("ctxp", [P, PAIRS, P])
        qtp = a.ps("qtp", [P, 2, HID])
        op = a.ps("op", [P, 2, 512])
        sems = {}
        for s in ("w_loaded x_loaded const chain w_ready sq_ready norms_done norms_var norms_root rinv_ready xs_ready "
                  "proj_done k_read kmax_done kmax_clear kmax_turned mx_ready mx_spread kb_ready diff_ready "
                  "e_ready esum_done esum_clear v_read ctx_cleared ctx_used ctx_sum rs_ready cT_ready mix_done mix_ready "
                  "qmax q_read q_exp q_sum q_norm q_turned qT_ready out_done out_ready out_sq oroot oinv_ready y_ready "
                  "y_turned added passed").split():
            sems[s] = a.sem(s)
        S = type("Sems", (), sems)
        stored = [a.sem(f"stored{b}") for b in range(2)]
        U = 2 * GROUP
        RUNS = GROUPS // 2
        CHAIN = CH * GROUPS + CH + 6 + 5

        with nc.Block() as block:
            @block.sync
            def _(sp):
                for dst, src in ((w, "w_qkv"), (w_out, "w_out"), (g_in, "g_in"), (g_out, "g_out"), (b_out, "b_out")):
                    sp.dma_start(dst[:], D[src]).then_inc(S.w_loaded, 16)
                with sp.Fori(0, IMAGES) as n:
                    sp.wait_ge(S.added, CH * GROUPS * n)
                    sp.dma_start(x[:], D["x1"][n].rearrange("(h p) q -> p h q", p=P)).then_inc(S.x_loaded, 16)
                    with sp.Fori(0, RUNS) as r:
                        for b in range(2):
                            sp.wait_ge(S.added, CH * (GROUPS * n + 2 * r + b + 1))
                            dst = D["x2"][n].rearrange("(h p) q -> p h q", p=P)[:, :, bass.ds((2 * r + b) * GPIX, GPIX)]
                            sp.dma_start(dst, xo[:, b]).then_inc(stored[b], 16)
                for b in range(2):
                    sp.wait_ge(stored[b], 16 * IMAGES * RUNS)

            @block.gpsimd
            def _(pool):
                chain = Chain(pool, S.const)
                chain.link(nc.gpsimd.memset(ones[:], 1.0))
                chain.link(nc.gpsimd.memset(zeros[:], 0.0))
                chain.link(nc.gpsimd.memset(cT[:], 0.0))
                with pool.Fori(0, IMAGES) as n:
                    pool.wait_ge(S.ctx_sum, n)
                    pool.sem_inc(S.passed, 1)
                    nc.gpsimd.memset(esum[:], 0.0).then_inc(S.esum_clear, 1)
                    pool.wait_ge(S.kb_ready, n + 1)
                    pool.sem_inc(S.passed, 1)
                    with pool.Fori(0, RUNS) as r:
                        for c in range(U + 1):
                            i = n * TILES + r * U + c
                            if c < U:
                                pool.wait_ge(S.ctx_used, n * TILES + r * U + max(c - 1, 0))
                                nc.gpsimd.tensor_tensor(e[:, c % 2, :], keys[:, bass.ds(r * U + c, 1), :].rearrange("p t d -> p (t d)"),
                                                        kb[:], ALU.subtract).then_inc(S.diff_ready, 1)
                            if c:
                                pool.wait_ge(S.e_ready, n * TILES + r * U + c)
                                pool.wait_ge(S.esum_done, n * TILES + r * U + c - 1)
                                if c == 1:
                                    pool.wait_ge(S.esum_clear, n + 1)
                                nc.gpsimd.tensor_tensor(esum[:], esum[:], e[:, (c - 1) % 2, :], ALU.add).then_inc(S.esum_done, 1)

            @block.scalar
            def _(act):
                def normalise(n, r, b, which, func, done):
                    if which == 0:
                        act.wait_ge(S.norms_done, n * GROUPS + 2 * r + max(b - 1, 0))
                        act.wait_ge(S.proj_done, n * 3 * TILES)
                    else:
                        act.wait_ge(S.norms_done, (n + 1) * GROUPS)
                        act.wait_ge(S.proj_done, (n * 3 + which - 1) * TILES + r * U)
                    act.sem_inc(S.passed, 1)
                    for h in range(CH):
                        nc.scalar.activation(xs[:, b, h, :], x[:, h, bass.ds((2 * r + b) * GPIX, GPIX)], func,
                                             bias=gn.shift[:, h:h + 1], scale=gn.scale[:, h:h + 1]).then_inc(done, 1)

                def spaced(n, r, what, start):
                    normalise(n, r, 0, what, ACT.Identity, S.xs_ready)
                    normalise(n, r, 1, what, ACT.Identity, S.xs_ready)

                with act.Fori(0, IMAGES) as n:
                    gn.act(nc, act, n)
                    act.wait_ge(gn.ready, n + 1)
                    act.sem_inc(S.passed, 1)
                    with act.Fori(0, RUNS) as r:
                        for b in range(2):
                            normalise(n, r, b, 0, ACT.Square, S.sq_ready)
                    act.wait_ge(S.norms_var, n + 1)
                    nc.scalar.activation(rinv[:], small[:, 32:32 + TILES], ACT.Sqrt).then_inc(S.norms_root, 1)
                    act.wait_ge(S.rinv_ready, n + 1)
                    act.sem_inc(S.passed, 1)
                    with act.Fori(0, RUNS) as r:
                        spaced(n, r, 1, 0)
                        for c in range(U):
                            act.wait_ge(S.proj_done, n * 3 * TILES + r * U + c + 1)
                            act.sem_inc(S.passed, 1)
                            nc.scalar.activation(keys[:, bass.ds(r * U + c, 1), :].rearrange("p t d -> p (t d)"), proj[:, c % 2, :], ACT.Copy,
                                                 scale=rinv[:, bass.ds(r * U + c, 1)]).then_inc(S.k_read, 1)
                    with act.Fori(0, RUNS) as r:
                        spaced(n, r, 2, 0)
                        for c in range(U):
                            act.wait_ge(S.diff_ready, n * TILES + r * U + c + 1)
                            nc.scalar.activation(e[:, c % 2, :], e[:, c % 2, :], ACT.Exp).then_inc(S.e_ready, 1)
                            act.wait_ge(S.proj_done, (n * 3 + 1) * TILES + r * U + c + 1)
                            act.wait_ge(S.ctx_used, n * TILES + r * U + max(c - 1, 0))
                            act.sem_inc(S.passed, 1)
                            nc.scalar.activation(v[:, c % 2, :], proj[:, c % 2, :], ACT.Copy,
                                                 scale=rinv[:, bass.ds(r * U + c, 1)]).then_inc(S.v_read, 1)
                    with act.Fori(0, RUNS) as r:
                        spaced(n, r, 3, 0)
                        for c in range(U + 3):
                            if c < U:
                                act.wait_ge(S.q_read, n * TILES + r * U + c + 1)
                                act.sem_inc(S.passed, 1)
                                nc.scalar.activation(q[:, c % 2, :], q[:, c % 2, :], ACT.Exp,
                                                     scale=rinv[:, bass.ds(r * U + c, 1)]).then_inc(S.q_exp, 1)
                            if 1 <= c < U + 1:
                                j = c - 1
                                act.wait_ge(S.q_turned, n * TILES + r * U + j + 1)
                                act.wait_ge(S.out_done, n * TILES + r * U + max(j - 1, 0))
                                nc.scalar.activation(qT[:, j % 2, :], qtp[:, j % 2, :], ACT.Copy).then_inc(S.qT_ready, 1)
                            if c >= 3:
                                j = c - 3
                                act.wait_ge(S.out_ready, n * TILES + r * U + j + 1)
                                act.wait_ge(S.out_sq, n * TILES + r * U + j)
                                act.sem_inc(S.passed, 1)
                                nc.scalar.activation(sq[:], outs[:, bass.ds(r * U + j, 1), :].rearrange("p t c -> p (t c)"), ACT.Square,
                                                     accum_out=osum[:, bass.ds(r * U + j, 1)]).then_inc(S.out_sq, 1)
                    act.wait_ge(S.out_sq, (n + 1) * TILES)
                    nc.scalar.activation(oinv[:], osum[:], ACT.Sqrt).then_inc(S.oroot, 1)

            @block.vector
            def _(dve):
                dve.wait_ge(S.w_loaded, 16 * 5)
                dve.wait_ge(S.const, 3)
                for h in range(CH):
                    nc.vector.tensor_scalar(w[:, h].rearrange("p a b -> p (a b)"), w[:, h].rearrange("p a b -> p (a b)"),
                                            g_in[:, h:h + 1], float(C) ** 0.5, ALU.mult, ALU.mult).then_inc(S.w_ready, 1)
                with dve.Fori(0, IMAGES) as n:
                    chain = Chain(dve, S.chain, n * CHAIN)
                    dve.wait_ge(S.x_loaded, 16 * (n + 1))
                    gn.dve(nc, dve, chain, n, x, small[:, 0:2 * CH])
                    dve.wait_ge(S.norms_done, GROUPS * (n + 1))
                    nc.vector.memset(kmax[:], -3.0e38).then_inc(S.norms_var, 1)
                    dve.wait_ge(S.norms_root, n + 1)
                    chain.link(nc.vector.tensor_scalar(rinv[:], rinv[:], RMS_EPS, None, ALU.max))
                    nc.vector.reciprocal(rinv[:], rinv[:]).then_inc(S.rinv_ready, 1)
                    dve.wait_ge(S.rinv_ready, n + 1)
                    dve.sem_inc(S.passed, 1)
                    with dve.Fori(0, RUNS) as r:
                        for c in range(U):
                            dve.wait_ge(S.k_read, n * TILES + r * U + c + 1)
                            dve.wait_ge(S.kmax_done, n * TILES + r * U + c)
                            dve.sem_inc(S.passed, 1)
                            nc.vector.tensor_tensor(kmax[:], kmax[:], keys[:, bass.ds(r * U + c, 1), :].rearrange("p t d -> p (t d)"),
                                                    ALU.max).then_inc(S.kmax_done, 1)
                    dve.wait_ge(S.kmax_turned, n + 1)
                    chain.link(nc.vector.tensor_reduce(mx[:], op[:, 0, :].rearrange("p (j q) -> p j q", q=P), AX_X, ALU.max))
                    nc.vector.tensor_copy(mxb[:], mx[:].unsqueeze(2).to_broadcast([P, PAIRS, P])).then_inc(S.mx_ready, 1)
                    dve.wait_ge(S.mx_spread, n + 1)
                    nc.vector.tensor_copy(kb[:], op[:, 1, :]).then_inc(S.kb_ready, 1)
                    dve.wait_ge(S.ctx_sum, n + 1)
                    for lo in (0, DH):
                        s = slice(lo, lo + DH)
                        nc.vector.tensor_copy(cT[s, :, s], ctxp[s, :, s]).then_inc(S.cT_ready, 1)
                    chain.link(nc.vector.reciprocal(rs[:], small[:, 64:64 + PAIRS]))
                    nc.vector.tensor_scalar(rs[:], rs[:], float(DH) ** -0.5, None, ALU.mult).then_inc(S.rs_ready, 1)
                    dve.wait_ge(S.rs_ready, n + 1)
                    dve.wait_ge(S.mix_done, n + 1)
                    for j in range(PAIRS):
                        nc.vector.tensor_scalar(mix[:, j, :], qtp[:, j // 2, (j % 2) * C:(j % 2 + 1) * C], rs[:, j:j + 1], None,
                                                ALU.mult).then_inc(S.mix_ready, 1)
                    with dve.Fori(0, RUNS) as r:
                        for c in range(U + 3):
                            if c < U:
                                dve.wait_ge(S.proj_done, (n * 3 + 2) * TILES + r * U + c + 1)
                                heads = proj[:, c % 2, :].rearrange("p (h d) -> p h d", d=DH)
                                nc.vector.tensor_reduce(qm[:, c % 2, :], heads, AX_X, ALU.max).then_inc(S.qmax, 1)
                                dve.wait_ge(S.qmax, n * TILES + r * U + c + 1)
                                dve.wait_ge(S.q_turned, n * TILES + r * U + max(c - 1, 0))
                                nc.vector.tensor_tensor(q[:, c % 2, :].rearrange("p (h d) -> p h d", d=DH), heads,
                                                        qm[:, c % 2, :].unsqueeze(2).to_broadcast([P, HEADS, DH]),
                                                        ALU.subtract).then_inc(S.q_read, 1)
                            if 1 <= c < U + 1:
                                j = c - 1
                                qj = q[:, j % 2, :].rearrange("p (h d) -> p h d", d=DH)
                                dve.wait_ge(S.q_exp, n * TILES + r * U + j + 1)
                                nc.vector.tensor_reduce(qs[:, j % 2, :], qj, AX_X, ALU.add).then_inc(S.q_sum, 1)
                                dve.wait_ge(S.q_sum, 2 * (n * TILES + r * U + j) + 1)
                                nc.vector.reciprocal(qs[:, j % 2, :], qs[:, j % 2, :]).then_inc(S.q_sum, 1)
                                dve.wait_ge(S.q_sum, 2 * (n * TILES + r * U + j) + 2)
                                nc.vector.tensor_tensor(qj, qj, qs[:, j % 2, :].unsqueeze(2).to_broadcast([P, HEADS, DH]),
                                                        ALU.mult).then_inc(S.q_norm, 1)
                            if c >= 3:
                                j = c - 3
                                dve.wait_ge(S.out_done, n * TILES + r * U + j + 1)
                                dve.sem_inc(S.passed, 1)
                                nc.vector.tensor_tensor(outs[:, bass.ds(r * U + j, 1), :].rearrange("p t c -> p (t c)"), op[:, j % 2, 0:C],
                                                        b_out[:], ALU.add).then_inc(S.out_ready, 1)
                    dve.wait_ge(S.oroot, n + 1)
                    chain.link(nc.vector.tensor_scalar(oinv[:], oinv[:], RMS_EPS, None, ALU.max))
                    chain.link(nc.vector.reciprocal(oinv[:], oinv[:]))
                    nc.vector.tensor_scalar(oinv[:], oinv[:], float(C) ** 0.5, None, ALU.mult).then_inc(S.oinv_ready, 1)
                    dve.wait_ge(S.oinv_ready, n + 1)
                    dve.sem_inc(S.passed, 1)
                    with dve.Fori(0, RUNS) as r:
                        for b in range(2):
                            for t in range(GROUP):
                                c = b * GROUP + t
                                dve.wait_ge(S.y_turned, n * TILES + r * U + max(c - 1, 0))
                                dve.sem_inc(S.passed, 1)
                                nc.vector.tensor_scalar(y[:, c % 2, :], outs[:, bass.ds(r * U + c, 1), :].rearrange("p t c -> p (t c)"),
                                                        oinv[:, bass.ds(r * U + c, 1)], None, ALU.mult).then_inc(S.y_ready, 1)
                            dve.wait_ge(S.y_turned, n * TILES + r * U + (b + 1) * GROUP)
                            dve.wait_ge(stored[b], 16 * (RUNS * n + r))
                            dve.sem_inc(S.passed, 1)
                            for h in range(CH):
                                nc.vector.scalar_tensor_tensor(xo[:, b, h, :], proj[:, h, :], g_out[:, h:h + 1],
                                                               x[:, h, bass.ds((2 * r + b) * GPIX, GPIX)], ALU.mult, ALU.add).then_inc(S.added, 1)
                    assert chain.n == CHAIN, chain.n

            @block.tensor
            def _(pe):
                pe.wait_ge(S.w_ready, CH)
                pe.wait_ge(S.const, 3)

                def project(n, r, c, which, read):
                    if c % GROUP == 0:
                        pe.wait_ge(S.xs_ready, CH * ((n * 3 + which) * GROUPS + 2 * r + c // GROUP + 1))
                    pe.wait_ge(read, n * TILES + r * U + max(c - 1, 0))
                    for h in range(CH):
                        mm = nc.tensor.matmul(proj[:, c % 2, :], xs[:, c // GROUP, h, (c % GROUP) * P:(c % GROUP + 1) * P],
                                              w[:, h, (1, 2, 0)[which], :], start=(h == 0), stop=(h == CH - 1))
                    mm.then_inc(S.proj_done, 1)

                with pe.Fori(0, IMAGES) as n:
                    gn.pe(nc, pe, n, avg, small[:, 0:2 * CH])
                    pe.wait_ge(gn.variance, n + 1)
                    pe.sem_inc(S.passed, 1)
                    with pe.Fori(0, RUNS) as r:
                        for b in range(2):
                            pe.wait_ge(S.sq_ready, CH * (n * GROUPS + 2 * r + b + 1))
                            for t in range(GROUP):
                                for h in range(CH):
                                    mm = nc.tensor.matmul(small[:, bass.ds(32 + r * U + b * GROUP + t, 1)], xs[:, b, h, t * P:(t + 1) * P],
                                                          ones[:], start=(h == 0), stop=(h == CH - 1))
                            mm.then_inc(S.norms_done, 1)
                    pe.wait_ge(S.added, CH * GROUPS * n)
                    pe.sem_inc(S.passed, 1)
                    with pe.Fori(0, RUNS) as r:
                        for c in range(U):
                            project(n, r, c, 0, S.k_read)
                    pe.wait_ge(S.kmax_done, TILES * (n + 1))
                    for j in range(PAIRS):
                        mm = nc.tensor.transpose(op[:, 0, j * P:(j + 1) * P], kmax[:, j * P:(j + 1) * P], ident[:])
                    mm.then_inc(S.kmax_turned, 1)
                    pe.wait_ge(S.mx_ready, n + 1)
                    for j in range(PAIRS):
                        mm = nc.tensor.matmul(op[:, 1, j * P:(j + 1) * P], mxb[:, j, :], ident[:], start=True, stop=True)
                    mm.then_inc(S.mx_spread, 1)
                    pe.wait_ge(S.cT_ready, 2 * n)
                    nc.tensor.matmul(ctxp[:].rearrange("p j d -> p (j d)"), zeros[:, 0:P], zeros[:], start=True, stop=False,
                                     skip_group_check=True)
                    pe.wait_ge(S.k_read, TILES * (n + 1))
                    pe.sem_inc(S.passed, 1)
                    with pe.Fori(0, RUNS) as r:
                        for c in range(U + 1):
                            if c < U:
                                project(n, r, c, 1, S.v_read)
                            if c:
                                k = c - 1
                                pe.wait_ge(S.e_ready, n * TILES + r * U + k + 1)
                                pe.wait_ge(S.v_read, n * TILES + r * U + k + 1)
                                pe.wait_ge(S.esum_done, n * TILES + r * U + k + 1)
                                for j in range(PAIRS):
                                    s = slice(j * P, (j + 1) * P)
                                    mm = nc.tensor.matmul(ctxp[:, j, :], v[:, k % 2, s], e[:, k % 2, s], start=False, stop=False,
                                                          skip_group_check=True)
                                mm.then_inc(S.ctx_used, 1)
                    pe.wait_ge(S.esum_done, TILES * (n + 1))
                    for j in range(PAIRS):
                        mm = nc.tensor.matmul(small[:, 64 + j:65 + j], esum[:, j * P:(j + 1) * P], ones[:], start=True, stop=True)
                    mm.then_inc(S.ctx_sum, 1)
                    pe.wait_ge(S.cT_ready, 2 * (n + 1))
                    for j in range(PAIRS):
                        mm = nc.tensor.matmul(qtp[:, j // 2, (j % 2) * C:(j % 2 + 1) * C], cT[:, j, :], w_out[:, j, :], start=True, stop=True)
                    mm.then_inc(S.mix_done, 1)
                    pe.wait_ge(S.mix_ready, PAIRS * (n + 1))
                    pe.wait_ge(S.v_read, TILES * (n + 1))
                    pe.sem_inc(S.passed, 1)
                    with pe.Fori(0, RUNS) as r:
                        for c in range(U + 2):
                            if c < U:
                                project(n, r, c, 2, S.q_read)
                            if 1 <= c < U + 1:
                                j = c - 1
                                pe.wait_ge(S.q_norm, n * TILES + r * U + j + 1)
                                pe.wait_ge(S.qT_ready, n * TILES + r * U + max(j - 1, 0))
                                for p in range(PAIRS):
                                    mm = nc.tensor.transpose(qtp[:, j % 2, p * P:(p + 1) * P], q[:, j % 2, p * P:(p + 1) * P], ident[:])
                                mm.then_inc(S.q_turned, 1)
                            if c >= 2:
                                j = c - 2
                                pe.wait_ge(S.qT_ready, n * TILES + r * U + j + 1)
                                pe.wait_ge(S.out_ready, n * TILES + r * U + max(j - 1, 0))
                                for p in range(PAIRS):
                                    mm = nc.tensor.matmul(op[:, j % 2, 0:C], qT[:, j % 2, p * P:(p + 1) * P], mix[:, p, :],
                                                          start=(p == 0), stop=(p == PAIRS - 1))
                                mm.then_inc(S.out_done, 1)
                    with pe.Fori(0, RUNS) as r:
                        for b in range(2):
                            pe.wait_ge(S.added, CH * (GROUPS * n + 2 * r + b))
                            for t in range(GROUP):
                                c = b * GROUP + t
                                pe.wait_ge(S.y_ready, n * TILES + r * U + c + 1)
                                for h in range(CH):
                                    mm = nc.tensor.transpose(proj[:, h, t * P:(t + 1) * P], y[:, c % 2, h * P:(h + 1) * P], ident[:])
                                mm.then_inc(S.y_turned, 1)


def stage_involution_filters(nc, D, filt):
    with ExitStack() as ctx:
        a = Alloc(nc, ctx, "f_")
        w2 = a.sb("w2", [MID + 1, G2 * TAPS])
        bn = a.sb("bn", [MID + 1, 4, G2 * TAPS])
        loaded = a.sem("loaded")
        chain_sem = a.sem("chain")
        root = a.sem("root")
        with nc.Block() as block:
            @block.sync
            def _(sp):
                sp.dma_start(w2[0:MID], D["w2"]).then_inc(loaded, 16)
                sp.dma_start(bn[:], D["bn2"]).then_inc(loaded, 16)

            @block.scalar
            def _(act):
                act.wait_ge(chain_sem, 2)
                nc.scalar.activation(bn[:, 3], bn[:, 3], ACT.Sqrt).then_inc(root, 1)

            @block.vector
            def _(dve):
                chain = Chain(dve, chain_sem)
                dve.wait_ge(loaded, 32)
                chain.add(nc.vector.memset(filt[:], 0.0))
                chain.add(nc.vector.tensor_scalar(bn[:, 3], bn[:, 3], BN_EPS, None, ALU.add))
                dve.wait_ge(root, 1)
                chain.link(nc.vector.reciprocal(bn[:, 3], bn[:, 3]))
                chain.link(nc.vector.tensor_tensor(bn[:, 0], bn[:, 0], bn[:, 3], ALU.mult))
                chain.link(nc.vector.tensor_tensor(w2[0:MID], w2[0:MID], bn[0:MID, 0], ALU.mult))
                chain.link(nc.vector.tensor_tensor(bn[:, 2], bn[:, 2], bn[:, 0], ALU.mult))
                chain.link(nc.vector.tensor_tensor(w2[MID:MID + 1], bn[MID:MID + 1, 1], bn[MID:MID + 1, 2], ALU.subtract))
                for g in range(G2):
                    chain.add(nc.vector.tensor_copy(filt[:, g, LEAD:LEAD + K7 * WX].rearrange("p (a b) -> p a b", b=WX)[:, :, 0:K7],
                                                    w2[:, g * TAPS:(g + 1) * TAPS].rearrange("p (a b) -> p a b", b=K7)))


def stage_involution(nc, D, avg, ident, filt):
    GH = G2 // CH
    CHUNKS = 4
    CB = BLOCKS // CHUNKS
    with ExitStack() as ctx:
        a = Alloc(nc, ctx, "i_")
        x = a.sb("x", [P, CH, PIX])
        y = a.sb("y", [MID + 1, BPIX, 2 * BLOCKS])
        y_half = a.sb("y_half", [MID + 1, BPIX, BLOCKS])
        kern = a.sb("kern", [WIN, GH, BPIX, BLOCKS])
        win = a.sb("win", [WIN, 2, CB, P])
        xs = a.sb("xs", [P, 2, CH, GPIX])
        turned = a.sb("turned", [P, 2, GROUP, C])
        w1 = a.sb("w1", [P, CH, MID])
        bn1 = a.sb("bn1", [MID, 7])
        co = a.sb("co", [MID, 8])
        d = a.sb("d", [MID, 2, GPIX])
        sg = a.sb("sg", [MID, 2, GPIX])
        u = a.sb("u", [MID, 2, GPIX])
        own = a.sb("own", [P, GH, BPIX])
        masked = a.sb("masked", [P, 2, 4 * GH * BPIX])
        inv = a.sb("inv", [P, BLOCKS, BPIX])
        zero = kern[0:PAD2 + 1].rearrange("p g q b -> p (g q b)")[:, 0:(K7 - 1) * C]
        gn = GroupNorm(a)
        small = a.ps("small", [P, 512])
        yp = a.ps("yp", [P, 512])
        tp = a.ps("tp", [P, 2, 2, C])
        kp = a.ps("kp", [P, 2, 4 * BLOCKS])
        sp_ = a.ps("sum", [P, 2, 4 * GH * BPIX])
        sems = {}
        for s in ("root1 half_ready w_loaded x_loaded const chain xs_ready yp_done d_ready sg_ready u_ready m_ready y_ready turn_done turn_read "
                  "filled kern_done kern_read sum_done sum_read reduced added stored passed").split():
            sems[s] = a.sem(s)
        S = type("Sems", (), sems)
        patched = [a.sem(f"patched{b}") for b in range(2)]
        win_loaded = [a.sem(f"win_loaded{b}") for b in range(2)]
        RUNS = GROUPS // 2
        COEF = 10
        CHAIN = CH * GROUPS + CH + 6
        BANKS = GH * BPIX // 4
        patch = D["patch"]
        EDGE = 3 * PAD2 + 3

        with nc.Block() as block:
            @block.sync
            def _(sp):
                sp.dma_start(w1[:], D["w1"]).then_inc(S.w_loaded, 16)
                sp.dma_start(bn1[:], D["bn1"]).then_inc(S.w_loaded, 16)
                sp.wait_ge(S.const, 2)
                with sp.Fori(0, IMAGES) as n:
                    z3 = zero[:, 0:3 * C]
                    for first in (0, PAD2 * PAD2 - EDGE):
                        sp.dma_start(patch[n, bass.ds(first, EDGE), :].rearrange("(p q) c -> p (q c)", q=3), z3[0:EDGE // 3]).then_inc(S.filled, 16)
                    gaps = patch[n, bass.ds(EDGE, (HW - 1) * PAD2), :].rearrange("(r q) c -> r q c", q=PAD2)[:, HW:PAD2, :]
                    sp.dma_start(gaps, zero[0:HW - 1, :].rearrange("p (q c) -> p q c", c=C)).then_inc(S.filled, 16)
                sp.wait_ge(S.filled, 16 * 3 * IMAGES)
                with sp.Fori(0, IMAGES) as n:
                    sp.wait_ge(S.stored, 16 * 4 * n)
                    sp.dma_start(x[:], D["x2"][n].rearrange("(h p) q -> p h q", p=P)).then_inc(S.x_loaded, 16)
                    with sp.Fori(0, RUNS) as r:
                        for b in range(2):
                            sp.wait_ge(S.turn_read, 2 * (GROUPS * n + 2 * r + b + 1))
                            for half in range(2):
                                rows = patch[n, bass.ds((3 + (2 * r + b) * 8) * PAD2, 8 * PAD2), :]
                                dst = rows.rearrange("(t o q) c -> q t o c", o=2, q=PAD2)[3:3 + HW, :, half, :]
                                sp.dma_start(dst, turned[half * HW:(half + 1) * HW, b]).then_inc(patched[b], 16)
                    for b in range(2):
                        sp.wait_ge(patched[b], 32 * RUNS * (n + 1))
                    sp.sem_inc(S.passed, 1)
                    with sp.Fori(0, 2) as hf:
                        for h in range(CH):
                            unit = (n * 2 + hf) * CH + h
                            for q in range(CHUNKS):
                                sp.wait_ge(S.sum_done, unit * BANKS + max(q - 1, 0) * BANKS // CHUNKS)
                                for wy in range(WY):
                                    for by in range(CB // BCOLS):
                                        row = (hf * HALF_ROWS + q * (HALF_ROWS // CHUNKS) + by * BY + wy) * PAD2
                                        at = patch[n, bass.ds(row, 1), h * P:(h + 1) * P]
                                        src = bass.AP(at.tensor, at.offset, [[C, WX], [BX * C, BCOLS], [1, P]])
                                        dst = win[wy * WX:(wy + 1) * WX, q % 2, by * BCOLS:(by + 1) * BCOLS, :]
                                        sp.dma_start(dst, src).then_inc(win_loaded[q % 2], 16)
                            sp.wait_ge(S.added, 2 * (unit + 1))
                            dst = D["x3"][n].rearrange("(h p) q -> p h q", p=P)[:, h, bass.ds(hf * (PIX // 2), PIX // 2)]
                            sp.dma_start(dst, x[:, h, bass.ds(hf * (PIX // 2), PIX // 2)]).then_inc(S.stored, 16)
                sp.wait_ge(S.stored, 16 * 4 * IMAGES)

            @block.gpsimd
            def _(pool):
                chain = Chain(pool, S.const)
                chain.link(nc.gpsimd.memset(zero, 0.0))
                chain.link(nc.gpsimd.memset(y[MID:MID + 1], 1.0))
                chain.link(nc.gpsimd.memset(own[:], 1.0))
                chain.link(nc.gpsimd.affine_select(out=own[:], in_=own[:], compare_op=ALU.is_ge, fill=0.0, base=0,
                                                   pattern=[[-GC, GH], [0, BPIX]], channel_multiplier=1))
                chain.link(nc.gpsimd.affine_select(out=own[:], in_=own[:], compare_op=ALU.is_ge, fill=0.0, base=GC - 1,
                                                   pattern=[[GC, GH], [0, BPIX]], channel_multiplier=-1))
                with pool.Fori(0, IMAGES) as n:
                    pool.wait_ge(S.y_ready, BY * GROUPS * (n + 1))
                    pool.sem_inc(S.passed, 1)
                    with pool.Fori(0, 2) as hf:
                        pool.wait_ge(S.kern_done, (n * 2 + hf) * CH * BANKS)
                        pool.sem_inc(S.passed, 1)
                        nc.gpsimd.tensor_copy(y_half[:], y[:, :, bass.ds(hf * BLOCKS, BLOCKS)]).then_inc(S.half_ready, 1)
                        for h in range(CH):
                            unit = (n * 2 + hf) * CH + h
                            pool.wait_ge(S.reduced, (unit + 1) * BANKS)
                            pool.sem_inc(S.passed, 1)
                            half = x[:, h, bass.ds(hf * (PIX // 2), PIX // 2)].rearrange("p (by ry bx rx) -> p by ry bx rx", ry=BY, bx=BCOLS, rx=BX)
                            for ry in range(BY):
                                src = inv[:].rearrange("p (by bx) (ry rx) -> p by bx ry rx", bx=BCOLS, ry=BY)[:, :, :, ry, :]
                                dst = half[:, :, ry, :, :]
                                nc.gpsimd.tensor_tensor(dst, dst, src, ALU.add).then_inc(S.added, 1)

            @block.scalar
            def _(act):
                act.wait_ge(S.chain, 1)
                nc.scalar.activation(co[:, 4:5], co[:, 5:6], ACT.Sqrt).then_inc(S.root1, 1)
                act.wait_ge(S.chain, COEF)
                with act.Fori(0, IMAGES) as n:
                    gn.act(nc, act, n)
                    act.wait_ge(gn.ready, n + 1)
                    act.sem_inc(S.passed, 1)
                    with act.Fori(0, RUNS) as r:
                        for b in range(2):
                            act.wait_ge(S.turn_done, 2 * (GROUPS * n + 2 * r))
                            act.wait_ge(S.yp_done, GROUPS * n + 2 * r)
                            act.sem_inc(S.passed, 1)
                            for h in range(CH):
                                nc.scalar.activation(xs[:, b, h, :], x[:, h, bass.ds((2 * r + b) * GPIX, GPIX)], ACT.Identity,
                                                     bias=gn.shift[:, h:h + 1], scale=gn.scale[:, h:h + 1]).then_inc(S.xs_ready, 1)
                        for b in range(2):
                            act.wait_ge(S.yp_done, GROUPS * n + 2 * r + b + 1)
                            act.wait_ge(S.m_ready, GROUPS * n + 2 * r)
                            act.wait_ge(S.u_ready, GROUPS * n + 2 * r + b)
                            nc.scalar.activation(d[:, b, :], yp[0:MID], ACT.Identity, bias=co[:, 1:2], scale=co[:, 0:1]).then_inc(S.d_ready, 1)
                            act.wait_ge(S.d_ready, GROUPS * n + 2 * r + b + 1)
                            act.sem_inc(S.passed, 1)
                            nc.scalar.activation(sg[:, b, :], d[:, b, :], ACT.Sigmoid, scale=bn1[:, 6:7]).then_inc(S.sg_ready, 1)
                    act.sem_inc(S.passed, 1)
                    with act.Fori(0, 2) as hf:
                        for h in range(CH):
                            unit = (n * 2 + hf) * CH + h
                            act.wait_ge(S.sum_done, unit * BANKS)
                            for k in range(BANKS):
                                act.wait_ge(S.kern_done, unit * BANKS + k + 1)
                                g, at = divmod(4 * k, BPIX)
                                nc.scalar.activation(kern[:, g, at:at + 4, :].rearrange("p a b -> p (a b)"), kp[0:WIN, k % 2, :],
                                                     ACT.Copy).then_inc(S.kern_read, 1)

            @block.vector
            def _(dve):
                chain = Chain(dve, S.chain)
                dve.wait_ge(S.w_loaded, 32)
                dve.wait_ge(S.const, 5)
                gamma, beta, mean, var, p1, p2 = (bn1[:, k:k + 1] for k in range(6))
                s, t, dp = (co[:, k:k + 1] for k in (4, 5, 6))
                chain.link(nc.vector.tensor_scalar(t, var, BN_EPS, None, ALU.add))
                dve.wait_ge(S.root1, 1)
                chain.link(nc.vector.reciprocal(s, s))
                chain.link(nc.vector.tensor_tensor(s, s, gamma, ALU.mult))
                chain.link(nc.vector.tensor_tensor(t, mean, s, ALU.mult))
                chain.link(nc.vector.tensor_tensor(t, beta, t, ALU.subtract))
                chain.link(nc.vector.tensor_tensor(dp, p1, p2, ALU.subtract))
                chain.link(nc.vector.tensor_tensor(co[:, 0:1], dp, s, ALU.mult))
                chain.link(nc.vector.tensor_tensor(co[:, 1:2], dp, t, ALU.mult))
                chain.link(nc.vector.tensor_tensor(co[:, 2:3], p2, s, ALU.mult))
                chain.link(nc.vector.tensor_tensor(co[:, 3:4], p2, t, ALU.mult))
                assert chain.n == COEF
                with dve.Fori(0, IMAGES) as n:
                    chain = Chain(dve, S.chain, n * CHAIN + COEF)
                    dve.wait_ge(S.x_loaded, 16 * (n + 1))
                    gn.dve(nc, dve, chain, n, x, small[:, 0:2 * CH])
                    assert chain.n == CHAIN, chain.n
                    dve.sem_inc(S.passed, 1)
                    with dve.Fori(0, RUNS) as r:
                        for b in range(2):
                            i = GROUPS * n + 2 * r + b
                            for half in range(2):
                                dve.wait_ge(S.turn_done, 2 * i + half + 1)
                                dve.wait_ge(patched[b], 32 * (RUNS * n + r))
                                nc.vector.tensor_copy(turned[:, b, 2 * half:2 * half + 2, :], tp[:, half]).then_inc(S.turn_read, 1)
                            dve.wait_ge(S.d_ready, i + 1)
                            nc.vector.tensor_scalar(u[:, b, :], yp[0:MID], co[:, 2:3], co[:, 3:4], ALU.mult, ALU.add).then_inc(S.u_ready, 1)
                            dve.wait_ge(S.sg_ready, i + 1)
                            nc.vector.tensor_tensor(d[:, b, :], d[:, b, :], sg[:, b, :], ALU.mult).then_inc(S.m_ready, 1)
                            dve.wait_ge(S.m_ready, i + 1)
                            dve.wait_ge(S.u_ready, i + 1)
                            dve.wait_ge(S.half_ready, 2 * n)
                            dve.sem_inc(S.passed, 1)
                            for ry in range(BY):
                                def rows(v):
                                    return v[:, b, :].rearrange("p (by ry bx rx) -> p by ry bx rx", ry=BY, bx=BCOLS, rx=BX)[:, :, ry]
                                per = GPIX // BPIX
                                dst = y[0:MID, ry * BX:(ry + 1) * BX, bass.ds((2 * r + b) * per, per)].rearrange("p rx (by bx) -> p by bx rx", bx=BCOLS)
                                nc.vector.tensor_tensor(dst, rows(d), rows(u), ALU.add).then_inc(S.y_ready, 1)
                    dve.sem_inc(S.passed, 1)
                    with dve.Fori(0, 2) as hf:
                        for h in range(CH):
                            unit = (n * 2 + hf) * CH + h
                            mask = own[:].rearrange("p g q -> p (g q)").unsqueeze(1).to_broadcast([P, 4, GH * BPIX])
                            for k in range(BANKS + 1):
                                if k < BANKS:
                                    dve.wait_ge(S.reduced, unit * BANKS + max(k - 1, 0))
                                    dve.wait_ge(S.sum_done, unit * BANKS + k + 1)
                                    nc.vector.tensor_tensor(masked[:, k % 2, :].rearrange("p (a b) -> p a b", a=4),
                                                            sp_[:, k % 2, :].rearrange("p (a b) -> p a b", a=4), mask,
                                                            ALU.mult).then_inc(S.sum_read, 1)
                                if k:
                                    j = k - 1
                                    if j == 0:
                                        dve.wait_ge(S.added, 2 * unit)
                                    dve.wait_ge(S.sum_read, unit * BANKS + j + 1)
                                    nc.vector.tensor_reduce(inv[:, 4 * j:4 * j + 4, :],
                                                            masked[:, j % 2, :].rearrange("p (a g q) -> p a q g", a=4, g=GH),
                                                            AX_X, ALU.add).then_inc(S.reduced, 1)

            @block.tensor
            def _(pe):
                pe.wait_ge(S.w_loaded, 32)
                with pe.Fori(0, IMAGES) as n:
                    gn.pe(nc, pe, n, avg, small[:, 0:2 * CH])
                    pe.sem_inc(S.passed, 1)
                    with pe.Fori(0, RUNS) as r:
                        for b in range(2):
                            i = GROUPS * n + 2 * r + b
                            pe.wait_ge(S.xs_ready, CH * (i + 1))
                            pe.wait_ge(S.u_ready, i)
                            for h in range(CH):
                                mm = nc.tensor.matmul(yp[0:MID], w1[:, h, :], xs[:, b, h, :], start=(h == 0), stop=(h == CH - 1))
                            mm.then_inc(S.yp_done, 1)
                            for half in range(2):
                                pe.wait_ge(S.turn_read, 2 * i + max(half - 1, 0))
                                for t in range(2):
                                    for h in range(CH):
                                        s = (2 * half + t) * P
                                        mm = nc.tensor.transpose(tp[:, half, t, h * P:(h + 1) * P], xs[:, b, h, s:s + P], ident[:])
                                mm.then_inc(S.turn_done, 1)
                    with pe.Fori(0, 2) as hf:
                        pe.wait_ge(S.half_ready, n * 2 + hf + 1)
                        for h in range(CH):
                            unit = (n * 2 + hf) * CH + h
                            for k in range(BANKS):
                                pe.wait_ge(S.kern_read, unit * BANKS + max(k - 1, 0))
                                for j in range(4):
                                    g, at = divmod(4 * k + j, BPIX)
                                    ry, rx = divmod(at, BX)
                                    mm = nc.tensor.matmul(kp[0:WIN, k % 2, j * BLOCKS:(j + 1) * BLOCKS],
                                                          filt[:, h * GH + g, LEAD - ry * WX - rx:FLAT - ry * WX - rx],
                                                          y_half[:, at, :], start=True, stop=True)
                                mm.then_inc(S.kern_done, 1)
                            pe.wait_ge(S.kern_read, (unit + 1) * BANKS)
                            for k in range(BANKS):
                                q, first = divmod(4 * k, CB)
                                if first == 0:
                                    pe.wait_ge(win_loaded[q % 2], (unit * (CHUNKS // 2) + q // 2 + 1) * 16 * WY * (CB // BCOLS))
                                pe.wait_ge(S.sum_read, unit * BANKS + max(k - 1, 0))
                                for j in range(4):
                                    mm = nc.tensor.matmul(sp_[:, k % 2, j * GH * BPIX:(j + 1) * GH * BPIX], win[:, q % 2, first + j, :],
                                                          kern[:, :, :, 4 * k + j].rearrange("p g q -> p (g q)"), start=True, stop=True)
                                mm.then_inc(S.sum_done, 1)


def stage_filter(nc, D, avg):
    with ExitStack() as ctx:
        a = Alloc(nc, ctx, "u_")
        W1 = HW + 1
        x = a.sb("x", [P, CH, PIX])
        xn = a.sb("xn", [P, CH, W1 * W1])
        f = a.sb("f", [P, CH, 16])
        gn = GroupNorm(a)
        small = a.ps("small", [P, 512])
        loaded = a.sem("loaded")
        x_loaded = a.sem("x_loaded")
        chain_sem = a.sem("chain")
        const = a.sem("const")
        normalised = a.sem("normalised")
        done = a.sem("done")
        stored = a.sem("stored")
        CHAIN = CH * GROUPS + CH + 6 + 6

        with nc.Block() as block:
            @block.sync
            def _(sp):
                sp.dma_start(f[:], D["filt"]).then_inc(loaded, 16)
                with sp.Fori(0, IMAGES) as n:
                    sp.wait_ge(stored, 16 * n)
                    sp.dma_start(x[:], D["x3"][n].rearrange("(h p) q -> p h q", p=P)).then_inc(x_loaded, 16)
                    sp.wait_ge(done, CH * (n + 1))
                    sp.dma_start(D["out"][n].rearrange("(h p) q -> p h q", p=P), x[:]).then_inc(stored, 16)
                sp.wait_ge(stored, 16 * IMAGES)

            @block.gpsimd
            def _(pool):
                nc.gpsimd.memset(xn[:], 0.0).then_inc(const, 1)

            @block.scalar
            def _(act):
                act.wait_ge(const, 1)
                with act.Fori(0, IMAGES) as n:
                    gn.act(nc, act, n)
                    act.wait_ge(gn.ready, n + 1)
                    for h in range(CH):
                        nc.scalar.activation(xn[:, h].rearrange("p (r c) -> p r c", c=W1)[:, 0:HW, 0:HW],
                                             x[:, h].rearrange("p (r c) -> p r c", c=HW), ACT.Identity,
                                             bias=gn.shift[:, h:h + 1], scale=gn.scale[:, h:h + 1]).then_inc(normalised, 1)

            @block.vector
            def _(dve):
                dve.wait_ge(loaded, 16)
                with dve.Fori(0, IMAGES) as n:
                    chain = Chain(dve, chain_sem, n * CHAIN)
                    dve.wait_ge(x_loaded, 16 * (n + 1))
                    gn.dve(nc, dve, chain, n, x, small[:, 0:2 * CH])
                    dve.wait_ge(normalised, CH * (n + 1))
                    taps = [(0, 0), (0, 1), (1, 0), (1, 1)]
                    for dy, dx in taps:
                        for h in range(CH):
                            at = 4 * (2 * dy + 1) + 2 * dx + 1
                            xh = x[:, h].rearrange("p (r c) -> p r c", c=HW)
                            src = xn[:, h].rearrange("p (r c) -> p r c", c=W1)[:, dy:dy + HW, dx:dx + HW]
                            ins = nc.vector.scalar_tensor_tensor(xh, src, f[:, h, at:at + 1], xh, ALU.mult, ALU.add)
                            if (dy, dx) == taps[-1]:
                                ins.then_inc(done, 1)
                            else:
                                chain.add(ins)
                        if (dy, dx) != taps[-1]:
                            dve.wait_ge(chain_sem, chain.value())
                    assert chain.n == CHAIN, chain.n

            @block.tensor
            def _(pe):
                with pe.Fori(0, IMAGES) as n:
                    gn.pe(nc, pe, n, avg, small[:, 0:2 * CH])


def build_program(nc, D, stages=("0", "1", "2", "3")):
    with ExitStack() as ctx:
        a = Alloc(nc, ctx, "g_")
        avg = a.sb("avg", [P, P])
        ident = a.sb("ident", [P, P])
        const = a.sem("const")
        with nc.Block() as block:
            @block.gpsimd
            def _(pool):
                chain = Chain(pool, const)
                group_average_matrix(nc, pool, chain, avg)
                identity_matrix(nc, pool, chain, ident)
        if "0" in stages:
            with ExitStack() as ctx0:
                a0 = Alloc(nc, ctx0, "l0_")
                all_idx = a0.sb("idx", [P, IMAGES, TILES * KK], I32)
                all_wt = a0.sb("wt", [P, IMAGES, 4, TILES * KK])
                stage_offsets(nc, D, avg, ident, all_idx, all_wt)
                stage_deform(nc, D, ident, all_idx[:].bitcast(U32), all_wt)
        if "1" in stages:
            stage_attention(nc, D, avg, ident)
        if "2" in stages:
            with ExitStack() as ctx2:
                filt = Alloc(nc, ctx2, "l2_").sb("filt", [MID + 1, G2, FLAT])
                stage_involution_filters(nc, D, filt)
                stage_involution(nc, D, avg, ident, filt)
        if "3" in stages:
            stage_filter(nc, D, avg)


def layouts(inp):
    import numpy as np

    def put(a):
        return np.ascontiguousarray(a)

    out = {"x": put(inp["x"].reshape(IMAGES, C, PIX))}
    w = inp["L0_conv_conv_offset_w"].reshape(3 * KK, CH, P, KK)
    b = inp["L0_conv_conv_offset_b"]
    w = np.concatenate([w[0:2 * KK:2], w[1:2 * KK:2], w[2 * KK:]])
    b = np.concatenate([b[0:2 * KK:2], b[1:2 * KK:2], b[2 * KK:]])
    out["w_off"] = put(w.transpose(2, 1, 3, 0))
    out["b_off"] = put(b.reshape(3 * KK, 1))
    out["w_dcn"] = put(inp["L0_conv_dcn_weight"].reshape(C, CH, P, KK).transpose(2, 1, 3, 0))

    def by_partition(v):
        return put(v.reshape(CH, P).T)

    w = inp["L1_conv_w_qkv"].reshape(3, HID, CH, P)
    out["w_qkv"] = put(w.transpose(3, 2, 0, 1))
    out["w_out"] = put(inp["L1_conv_w_out"].reshape(C, PAIRS, P).transpose(2, 1, 0))
    out["g_in"] = by_partition(inp["L1_conv_g_norm"])
    out["g_out"] = by_partition(inp["L1_conv_g_out"])
    out["b_out"] = put(np.broadcast_to(inp["L1_conv_b_out"], (P, C)))

    out["w1"] = put(inp["L2_conv_w1"].reshape(MID, CH, P).transpose(2, 1, 0))
    names = ("bn1_gamma", "bn1_beta", "bn1_mean", "bn1_var", "acon_p1", "acon_p2", "acon_beta")
    out["bn1"] = put(np.stack([inp["L2_conv_" + k] for k in names], axis=1))
    out["w2"] = put(inp["L2_conv_w2"].T)
    bn2 = np.stack([inp["L2_conv_bn2_" + k] for k in ("gamma", "beta", "mean", "var")])
    out["bn2"] = put(np.broadcast_to(bn2, (MID + 1,) + bn2.shape))
    out["filt"] = put(inp["L3_conv_filt"].reshape(CH, P, 16).transpose(1, 0, 2))
    return out


SCRATCH = {
    "table": (IMAGES * QROWS, 4 * C),
    "x1": (IMAGES, C, PIX),
    "x2": (IMAGES, C, PIX),
    "patch": (IMAGES, PAD2 * PAD2, C),
    "x3": (IMAGES, C, PIX),
}


def kernel(**inputs):
    import numpy as np
    from concourse import bacc
    from concourse.bass_utils import run_bass_kernel_spmd

    nc = bacc.Bacc("TRN2", target_bir_lowering=False, num_devices=1)
    arrays = layouts(inputs)
    D = {k: nc.dram_tensor("in_" + k, v.shape, F32, kind="ExternalInput").ap() for k, v in arrays.items()}
    for k, shape in SCRATCH.items():
        D[k] = nc.dram_tensor(k, shape, F32, kind="Internal").ap()
    D["out"] = nc.dram_tensor("out", (IMAGES, C, PIX), F32, kind="ExternalOutput").ap()
    build_program(nc, D)
    r = run_bass_kernel_spmd(nc, [{"in_" + k: v for k, v in arrays.items()}], core_ids=[0])
    return r.results[0]["out"].reshape(IMAGES, C, HW, HW)
```

```python
from contextlib import ExitStack

import concourse.bass as bass
from concourse import mybir

ALU = mybir.AluOpType
ACT = mybir.ActivationFunctionType
AX_X = mybir.AxisListType.X
F32 = mybir.dt.float32
I32 = mybir.dt.int32
BF16 = mybir.dt.bfloat16
U32 = mybir.dt.uint32

P = 128
IMAGES = 4
C = 256
CH = C // P
HW = 64
PIX = HW * HW
TILE_ROWS = P // HW
TILES = PIX // P
GROUP = 4
GPIX = GROUP * P
GROUPS = TILES // GROUP
GN_CH = 8
GN_EPS = 1e-5

KK = 9
PADW = HW + 3
POS = PADW * PADW
POS_TILES = -(-POS // (GROUP * P)) * GROUP
POS_PAD = POS_TILES * P
QUAD = (0, 1, PADW, PADW + 1)
QBASE = PADW + 1
QROWS = POS_PAD + QBASE
STEPS = KK * GROUP
OM = 32

HEADS, DH = 8, 64
HID = HEADS * DH
PAIRS = HID // P
RMS_EPS = 1e-12

MID = 64
K7 = 7
TAPS = K7 * K7
G2 = 16
GC = C // G2
BN_EPS = 1e-3
BY, BX = 2, 8
WY, WX = BY + K7 - 1, BX + K7 - 1
WIN = WY * WX
BPIX = BY * BX
PAD2 = HW + K7 - 1
LEAD = 2 * WX
FLAT = LEAD + WIN
HALF_ROWS = HW // 2
BLOCKS = (HALF_ROWS // BY) * (HW // BX)
BCOLS = HW // BX


class Chain:

    def __init__(self, eng, sem, base=0):
        self.eng, self.sem, self.base, self.n = eng, sem, base, 0

    def value(self):
        return self.base + self.n

    def add(self, ins):
        self.n += 1
        ins.then_inc(self.sem, 1)

    def link(self, ins):
        self.add(ins)
        self.eng.wait_ge(self.sem, self.value())


class Alloc:
    def __init__(self, nc, ctx, tag):
        self.nc, self.ctx, self.tag = nc, ctx, tag

    def sb(self, name, shape, dt=F32):
        return self.ctx.enter_context(self.nc.sbuf_tensor(self.tag + name, shape, dt))

    def ps(self, name, shape):
        return self.ctx.enter_context(self.nc.psum_tensor(self.tag + name, shape, F32))

    def sem(self, name):
        return self.ctx.enter_context(self.nc.semaphore(self.tag + name))


def group_average_matrix(nc, pool, chain, avg):
    chain.link(nc.gpsimd.memset(avg[:], 1.0 / GN_CH))
    view = avg[:].rearrange("p (g c) -> p g c", c=GN_CH)
    chain.link(nc.gpsimd.affine_select(out=view, in_=view, compare_op=ALU.is_ge, fill=0.0, base=0,
                                       pattern=[[-GN_CH, P // GN_CH], [0, GN_CH]], channel_multiplier=1))
    chain.link(nc.gpsimd.affine_select(out=view, in_=view, compare_op=ALU.is_ge, fill=0.0, base=GN_CH - 1,
                                       pattern=[[GN_CH, P // GN_CH], [0, GN_CH]], channel_multiplier=-1))


def identity_matrix(nc, pool, chain, ident):
    chain.link(nc.gpsimd.memset(ident[:], 0.0))
    chain.link(nc.gpsimd.affine_select(out=ident[:], in_=ident[:], compare_op=ALU.not_equal, fill=1.0, base=0,
                                       pattern=[[-1, P]], channel_multiplier=1))




class GroupNorm:

    def __init__(self, a):
        self.stats = a.sb("gn_stats", [P, CH, GROUPS, 6])
        self.mv = a.sb("gn_mv", [P, CH, 2])
        self.mom = a.sb("gn_mom", [P, CH, 2])
        self.gm = a.sb("gn_gm", [P, CH, 2])
        self.var = a.sb("gn_var", [P, CH])
        self.std = a.sb("gn_std", [P, CH])
        self.scale = a.sb("gn_scale", [P, CH])
        self.shift = a.sb("gn_shift", [P, CH])
        self.passed = a.sem("gn_passed")
        self.moments = a.sem("gn_moments")
        self.averaged = a.sem("gn_averaged")
        self.variance = a.sem("gn_variance")
        self.root = a.sem("gn_root")
        self.ready = a.sem("gn_ready")

    def dve(self, nc, dve, chain, n, x, ps, lax=False):
        for h in range(CH):
            for g in range(GROUPS):
                chain.add(nc.vector.bn_stats(self.stats[:, h, g, :], x[:, h, g * GPIX:(g + 1) * GPIX]))
        dve.wait_ge(chain.sem, chain.value())
        dve.sem_inc(self.passed, 1)
        for h in range(CH):
            chain.add(nc.vector.bn_aggr(self.mv[:, h, :], self.stats[:, h, :, :].rearrange("p g s -> p (g s)")))
        dve.wait_ge(chain.sem, chain.value())
        self.dve_rest(nc, dve, chain, n, ps)

    def dve_rest(self, nc, dve, chain, n, ps):
        chain.link(nc.vector.tensor_tensor(self.mom[:, :, 1], self.mv[:, :, 0], self.mv[:, :, 0], ALU.mult))
        nc.vector.tensor_tensor(self.mom[:, :, 1], self.mom[:, :, 1], self.mv[:, :, 1], ALU.add).then_inc(self.moments, 1)
        nc.vector.tensor_copy(self.mom[:, :, 0], self.mv[:, :, 0]).then_inc(self.moments, 1)
        dve.wait_ge(self.averaged, n + 1)
        chain.link(nc.vector.tensor_copy(self.gm[:].rearrange("p h s -> p (h s)"), ps))
        chain.link(nc.vector.tensor_tensor(self.var[:], self.gm[:, :, 0], self.gm[:, :, 0], ALU.mult))
        chain.link(nc.vector.tensor_tensor(self.var[:], self.gm[:, :, 1], self.var[:], ALU.subtract))
        nc.vector.tensor_scalar(self.var[:], self.var[:], GN_EPS, None, ALU.add).then_inc(self.variance, 1)
        dve.wait_ge(self.root, n + 1)
        chain.link(nc.vector.reciprocal(self.scale[:], self.std[:]))
        chain.link(nc.vector.tensor_tensor(self.shift[:], self.gm[:, :, 0], self.scale[:], ALU.mult))
        nc.vector.tensor_scalar(self.shift[:], self.shift[:], -1.0, None, ALU.mult).then_inc(self.ready, 1)
        dve.wait_ge(self.ready, n + 1)

    def pe(self, nc, pe, n, avg, ps):
        pe.wait_ge(self.moments, 2 * (n + 1))
        nc.tensor.matmul(ps, avg[:], self.mom[:].rearrange("p h s -> p (h s)"), start=True, stop=True).then_inc(self.averaged, 1)

    def act(self, nc, act, n):
        act.wait_ge(self.variance, n + 1)
        nc.scalar.activation(self.std[:], self.var[:], ACT.Sqrt).then_inc(self.root, 1)


def stage_offsets(nc, D, avg, ident, all_idx, all_wt):
    with ExitStack() as ctx:
        a = Alloc(nc, ctx, "o_")
        x = a.sb("x", [P, CH, PIX])
        xp = a.sb("xp", [P, CH, POS_PAD])
        w_off = a.sb("w_off", [P, CH, KK, OM])
        b_off = a.sb("b_off", [P, 1])
        quad = a.sb("quad", [P, 2, GROUP, C])
        om_c = a.sb("om_c", [P, 2, GPIX])
        om = a.sb("om", [P, TILES, 3 * KK])
        mask = a.sb("mask", [P, TILES, KK])
        grid = a.sb("grid", [P, 2, TILES * KK])
        pos = a.sb("pos", [P, 2, TILES * KK])
        pos_i = a.sb("pos_i", [P, 2, TILES * KK], I32)
        low = a.sb("low", [P, 2, TILES * KK])
        frac = a.sb("frac", [P, 2, TILES * KK])
        rest = a.sb("rest", [P, 2, TILES * KK])
        over = a.sb("over", [P, 2, TILES * KK])
        row = a.sb("row", [P, TILES * KK])
        base = a.sb("base", [P, 1])
        zero = a.sb("zero", [QBASE, C])
        gn = GroupNorm(a)
        tp = a.ps("tp", [P, 2, 2, 512])
        cv = a.ps("cv", [P, 2, 512])
        ot = a.ps("ot", [P, GROUP, P])
        gp = a.ps("gp", [P, 512])
        w_loaded = a.sem("w_loaded")
        x_loaded = a.sem("x_loaded")
        const = a.sem("const")
        chain_sem = a.sem("chain")
        normalised = a.sem("normalised")
        transposed = a.sem("transposed")
        tp_free = a.sem("tp_free")
        quad_stored = [a.sem(f"quad_stored{b}") for b in range(2)]
        conv_done = a.sem("conv_done")
        om_c_ready = a.sem("om_c_ready")
        om_t = a.sem("om_t")
        om_ready = a.sem("om_ready")
        mask_ready = a.sem("mask_ready")
        passed = a.sem("passed")
        filled = a.sem("filled")
        BATCH = POS_TILES // GROUP
        SETS = GROUPS // 4
        AFTER = (1, 4)
        DVE_STEPS = CH * GROUPS + CH + 6 + 12 + 5

        with nc.Block() as block:
            @block.sync
            def _(sp):
                sp.dma_start(w_off[:], D["w_off"]).then_inc(w_loaded, 16)
                sp.dma_start(b_off[:], D["b_off"]).then_inc(w_loaded, 16)
                sp.wait_ge(const, 7)
                with sp.Fori(0, IMAGES) as n:
                    for corner, off in enumerate(QUAD):
                        for first, rows in ((0, QBASE - off), (QROWS - off, off)):
                            if rows:
                                sp.dma_start(D["table"][bass.ds(n * QROWS + first, rows), corner * C:(corner + 1) * C],
                                             zero[0:rows]).then_inc(filled, 16)
                    sp.wait_ge(normalised, CH * n)
                    sp.dma_start(x[:], D["x"][n].rearrange("(h p) q -> p h q", p=P)).then_inc(x_loaded, 16)
                    for b in range(BATCH):
                        sp.wait_ge(tp_free, 2 * BATCH * n + 2 * (b + 1))
                        for corner, off in enumerate(QUAD):
                            first = QBASE - off + b * GPIX
                            dst = D["table"][bass.ds(n * QROWS + first, GPIX), corner * C:(corner + 1) * C]
                            sp.dma_start(dst.rearrange("(t p) c -> p t c", p=P), quad[:, b % 2]).then_inc(quad_stored[b % 2], 16)
                sp.wait_ge(filled, 16 * 6 * IMAGES)
                sp.wait_ge(quad_stored[0], 64 * IMAGES * -(-BATCH // 2))
                sp.wait_ge(quad_stored[1], 64 * IMAGES * (BATCH // 2))

            @block.gpsimd
            def _(pool):
                chain = Chain(pool, const)
                chain.link(nc.gpsimd.memset(xp[:], 0.0))
                for half in range(TILE_ROWS):
                    part = slice(half * HW, (half + 1) * HW)
                    for axis in range(2):
                        by = [[2 * GROUP, GROUPS], [1, 3], [0, 3], [2, GROUP]]
                        bx = [[0, GROUPS], [0, 3], [1, 3], [0, GROUP]]
                        chain.link(nc.gpsimd.iota(grid[part, axis, :].rearrange("p (g a b t) -> p g a b t", g=GROUPS, a=3, b=3),
                                       by if axis == 0 else bx, base=half if axis == 0 else 0,
                                       channel_multiplier=0 if axis == 0 else 1,
                                       allow_small_or_imprecise_dtypes=True))
                chain.link(nc.gpsimd.memset(base[:], float(QBASE)))
                chain.link(nc.gpsimd.memset(zero[:], 0.0))

            @block.vector
            def _(dve):
                dve.wait_ge(const, 7)
                with dve.Fori(0, IMAGES) as n:
                    chain = Chain(dve, chain_sem, n * DVE_STEPS)
                    dve.wait_ge(x_loaded, 16 * (n + 1))
                    gn.dve(nc, dve, chain, n, x, gp[:, 0:2 * CH])
                    dve.wait_ge(transposed, 2 * BATCH * n)
                    dve.wait_ge(conv_done, SETS * n)
                    inner = xp[:, 0, PADW + 1:PADW + 1 + HW * PADW].rearrange("p (r c) -> p r c", c=PADW)[:, :, 0:HW]
                    nc.vector.tensor_scalar(inner, x[:, 0].rearrange("p (r c) -> p r c", c=HW), gn.scale[:, 0:1],
                                            gn.shift[:, 0:1], ALU.mult, ALU.add).then_inc(normalised, 1)
                    for s in range(SETS):
                        dve.wait_ge(om_t, SETS * n + s + 1)
                        src = ot[:].rearrange("p t (g m) -> p g t m", m=OM)[:, :, :, 0:3 * KK]
                        dst = om[:, s * 4 * GROUP:(s + 1) * 4 * GROUP, :].rearrange("p (g t) m -> p g t m", t=GROUP)
                        nc.vector.tensor_copy(dst, src).then_inc(om_ready, 1)
                    dve.wait_ge(om_ready, SETS * (n + 1))
                    for axis in range(2):
                        for g in range(GROUPS):
                            sl = slice(g * STEPS, (g + 1) * STEPS)
                            off = om[:, g * GROUP:(g + 1) * GROUP, axis * KK:(axis + 1) * KK].rearrange("p t k -> p k t")
                            ins = nc.vector.tensor_tensor(pos[:, axis, sl].rearrange("p (k t) -> p k t", t=GROUP),
                                                          grid[:, axis, sl].rearrange("p (k t) -> p k t", t=GROUP), off, ALU.add)
                    chain.link(ins)
                    chain.link(nc.vector.tensor_scalar(pos[:], pos[:], 0.0, HW + 1.0, ALU.max, ALU.min))
                    chain.link(nc.vector.tensor_copy(pos_i[:], pos[:]))
                    chain.link(nc.vector.tensor_copy(low[:], pos_i[:]))
                    chain.link(nc.vector.tensor_tensor(over[:], low[:], pos[:], ALU.is_gt))
                    chain.link(nc.vector.tensor_tensor(low[:], low[:], over[:], ALU.subtract))
                    chain.link(nc.vector.tensor_tensor(frac[:], pos[:], low[:], ALU.subtract))
                    chain.link(nc.vector.tensor_scalar(rest[:], frac[:], -1.0, 1.0, ALU.mult, ALU.add))
                    chain.link(nc.vector.scalar_tensor_tensor(row[:], low[:, 0], float(PADW), low[:, 1], ALU.mult, ALU.add))
                    chain.link(nc.vector.tensor_scalar(row[:], row[:], base[:, 0:1], None, ALU.add))
                    chain.link(nc.vector.tensor_copy(all_idx[:, n, :], row[:]))
                    chain.link(nc.vector.tensor_scalar(base[:], base[:], float(QROWS), None, ALU.add))
                    dve.wait_ge(mask_ready, n + 1)
                    for g in range(GROUPS):
                        sl = slice(g * STEPS, (g + 1) * STEPS)
                        m = mask[:, g * GROUP:(g + 1) * GROUP, :].rearrange("p t k -> p k t")
                        for src in (frac, rest):
                            v = src[:, 0, sl].rearrange("p (k t) -> p k t", t=GROUP)
                            ins = nc.vector.tensor_tensor(v, v, m, ALU.mult)
                    chain.link(ins)
                    for corner, (wy, wx) in enumerate(((rest, rest), (rest, frac), (frac, rest), (frac, frac))):
                        chain.link(nc.vector.tensor_tensor(all_wt[:, n, corner, :], wy[:, 0], wx[:, 1], ALU.mult))
                    assert chain.n == DVE_STEPS, chain.n

            @block.scalar
            def _(act):
                act.wait_ge(w_loaded, 32)
                with act.Fori(0, IMAGES) as n:
                    gn.act(nc, act, n)
                    act.wait_ge(gn.ready, n + 1)
                    act.wait_ge(transposed, 2 * BATCH * n)
                    act.wait_ge(conv_done, SETS * n)
                    inner = xp[:, 1, PADW + 1:PADW + 1 + HW * PADW].rearrange("p (r c) -> p r c", c=PADW)[:, :, 0:HW]
                    nc.scalar.activation(inner, x[:, 1].rearrange("p (r c) -> p r c", c=HW), ACT.Identity,
                                         bias=gn.shift[:, 1:2], scale=gn.scale[:, 1:2]).then_inc(normalised, 1)

                    def offsets(s):
                        act.wait_ge(conv_done, SETS * n + s + 1)
                        act.wait_ge(om_t, SETS * n)
                        nc.scalar.activation(om_c[:, s, :], cv[:, s, :], ACT.Identity, bias=b_off[:]).then_inc(om_c_ready, 1)

                    for b in range(BATCH):
                        even, odd = -(-BATCH // 2), BATCH // 2
                        act.wait_ge(quad_stored[b % 2], (n * (even, odd)[b % 2] + b // 2) * 64)
                        for half in range(2):
                            act.wait_ge(transposed, 2 * BATCH * n + 2 * b + half + 1)
                            nc.scalar.activation(quad[:, b % 2, 2 * half:2 * half + 2, :],
                                                 tp[:, half, :, 0:C], ACT.Copy).then_inc(tp_free, 1)
                        if b in AFTER:
                            offsets(AFTER.index(b))
                    act.wait_ge(om_ready, SETS * (n + 1))
                    nc.scalar.activation(mask[:], om[:, :, 2 * KK:3 * KK], ACT.Sigmoid).then_inc(mask_ready, 1)

            @block.tensor
            def _(pe):
                pe.wait_ge(w_loaded, 32)
                with pe.Fori(0, IMAGES) as n:
                    gn.pe(nc, pe, n, avg, gp[:, 0:2 * CH])
                    pe.wait_ge(normalised, CH * (n + 1))

                    def conv(s):
                        pe.wait_ge(om_c_ready, SETS * n)
                        for tap in range(KK):
                            ky, kx = divmod(tap, 3)
                            for h in range(CH):
                                for j in range(4):
                                    at = ((4 * s + j) * GPIX // HW + ky) * PADW + kx
                                    rows = xp[:, h, at:at + 8 * PADW].rearrange("p (r c) -> p r c", c=PADW)[:, :, 0:HW]
                                    mm = nc.tensor.matmul(cv[j * OM:(j + 1) * OM, s, :], w_off[:, h, tap, :], rows,
                                                          start=(tap == 0 and h == 0), stop=(tap == KK - 1 and h == CH - 1),
                                                          skip_group_check=True)
                        mm.then_inc(conv_done, 1)

                    def turn(s):
                        pe.wait_ge(om_c_ready, SETS * n + s + 1)
                        pe.wait_ge(om_ready, SETS * n + s)
                        pe.sem_inc(passed, 1)
                        for t in range(GROUP):
                            mm = nc.tensor.transpose(ot[:, t, :], om_c[:, s, t * P:(t + 1) * P], ident[:])
                        mm.then_inc(om_t, 1)

                    for b in range(BATCH):
                        for half in range(2):
                            pe.wait_ge(tp_free, (2 * BATCH * n + 2 * b + half - 1) if b else 2 * BATCH * n)
                            for t in range(2):
                                for h in range(CH):
                                    at = ((2 * b + half) * 2 + t) * P
                                    mm = nc.tensor.transpose(tp[:, half, t, h * P:(h + 1) * P], xp[:, h, at:at + P], ident[:])
                            mm.then_inc(transposed, 1)
                        if b in AFTER:
                            conv(AFTER.index(b))
                        if b - 2 in AFTER:
                            turn(AFTER.index(b - 2))


def stage_deform(nc, D, ident, all_idx, all_wt):
    SLOTS = 6
    with ExitStack() as ctx:
        a = Alloc(nc, ctx, "d_")
        w = a.sb("w", [P, CH, KK, C])
        ring = a.sb("ring", [P, SLOTS, 4 * C])
        idx = a.sb("idx", [P, STEPS], U32)
        wt = a.sb("wt", [P, 2, 4, STEPS])
        val = a.sb("val", [P, 4, C])
        val_c = a.sb("val_c", [P, 2, CH, GPIX])
        xres = a.sb("xres", [P, 2, CH, GPIX])
        tp = a.ps("tp", [P, 2, CH, GPIX])
        acc = a.ps("acc", [P, 2, CH, GPIX])
        w_loaded = a.sem("w_loaded")
        x_loaded = [a.sem(f"x_loaded{b}") for b in range(2)]
        gathered = [a.sem(f"gathered{s}") for s in range(SLOTS)]
        idx_ready = a.sem("idx_ready")
        passed = a.sem("passed")
        wt_ready = a.sem("wt_ready")
        first_ready = a.sem("first_ready")
        part = a.sem("part")
        value_ready = a.sem("value_ready")
        val_free = a.sem("val_free")
        val_c_ready = a.sem("val_c_ready")
        tap_done = a.sem("tap_done")
        stored = a.sem("stored")
        added = a.sem("added")
        RUNS = IMAGES * GROUPS // 2

        def dram(t, n, g):
            return t[n].rearrange("(h p) q -> p h q", p=P)[:, :, g * GPIX:(g + 1) * GPIX]

        with nc.Block() as block:
            @block.sync
            def _(sp):
                sp.dma_start(w[:], D["w_dcn"]).then_inc(w_loaded, 16)
                with sp.Fori(0, IMAGES) as n:
                    with sp.Fori(0, GROUPS // 2) as gg:
                        for b in range(2):
                            i = (n * (GROUPS // 2) + gg) * 2 + b
                            if True:
                                sp.wait_ge(stored, (n * (GROUPS // 2) + gg) * 32)
                            src = D["x"][n].rearrange("(h p) q -> p h q", p=P)[:, :, bass.ds((gg * 2 + b) * GPIX, GPIX)]
                            sp.dma_start(xres[:, b], src).then_inc(x_loaded[b], 16)
                        for b in range(2):
                            i = (n * (GROUPS // 2) + gg) * 2 + b
                            sp.wait_ge(added, CH * (i + 1))
                            dst = D["x1"][n].rearrange("(h p) q -> p h q", p=P)[:, :, bass.ds((gg * 2 + b) * GPIX, GPIX)]
                            sp.dma_start(dst, xres[:, b]).then_inc(stored, 16)
                sp.wait_ge(stored, 16 * IMAGES * GROUPS)

            @block.gpsimd
            def _(pool):
                with pool.Fori(0, IMAGES) as n:
                    with pool.Fori(0, GROUPS) as g:
                        i = n * GROUPS + g
                        for s in range(SLOTS):
                            pool.wait_ge(gathered[s], i * (16 * STEPS // SLOTS))
                        nc.gpsimd.tensor_copy(idx[:], all_idx[:, n, bass.ds(g * STEPS, STEPS)]).then_inc(idx_ready, 1)
                        pool.wait_ge(idx_ready, i + 1)
                        for s in range(STEPS):
                            pool.wait_ge(value_ready, (i * STEPS + s - SLOTS + 1) if s >= SLOTS else i * STEPS)
                            pool.sem_inc(passed, 1)
                            pool.indirect_dma_start(out=ring[:, s % SLOTS, :], out_offset=None, in_=D["table"],
                                                    in_offset=bass.IndirectOffsetOnAxis(ap=idx[:, s:s + 1], axis=0)
                                                    ).then_inc(gathered[s % SLOTS], 16)

            @block.scalar
            def _(act):
                with act.Fori(0, IMAGES) as n:
                    with act.Fori(0, GROUPS // 2) as gg:
                        for b in range(2):
                            i = (n * (GROUPS // 2) + gg) * 2 + b
                            act.wait_ge(wt_ready, i + 1)
                            for tap in range(KK + 1):
                                if tap < KK:
                                    for t in range(GROUP):
                                        s = tap * GROUP + t
                                        act.wait_ge(gathered[s % SLOTS], (i * (STEPS // SLOTS) + s // SLOTS + 1) * 16)
                                        act.wait_ge(val_free, (i * STEPS + s - 3) if s > 3 else i * STEPS)
                                        nc.scalar.activation(val[:, s % 4, :], ring[:, s % SLOTS, 0:C], ACT.Copy,
                                                             scale=wt[:, b, 0, s:s + 1]).then_inc(first_ready, 1)
                                if tap:
                                    k = tap - 1
                                    act.wait_ge(val_free, i * STEPS + (k + 1) * GROUP)
                                    act.wait_ge(tap_done, (i * KK + k - 1) if k > 1 else i * KK)
                                    nc.scalar.activation(val_c[:, (b * KK + k) % 2, :, :], tp[:, (b * KK + k) % 2, :, :], ACT.Copy).then_inc(val_c_ready, 1)

            @block.vector
            def _(dve):
                with dve.Fori(0, IMAGES) as n:
                    with dve.Fori(0, GROUPS // 2) as gg:
                        for b in range(2):
                            i = (n * (GROUPS // 2) + gg) * 2 + b
                            nc.vector.tensor_copy(wt[:, b], all_wt[:, n, :, bass.ds((gg * 2 + b) * STEPS, STEPS)]).then_inc(wt_ready, 1)
                            dve.wait_ge(wt_ready, i + 1)
                            for pair in range(STEPS // 2):
                                for corner in range(1, 4):
                                    for j in range(2):
                                        s = 2 * pair + j
                                        if corner == 1:
                                            dve.wait_ge(first_ready, i * STEPS + s + 1)
                                        else:
                                            dve.wait_ge(part, i * STEPS * 2 + pair * 4 + (corner - 2) * 2 + j + 1)
                                        ins = nc.vector.scalar_tensor_tensor(
                                            val[:, s % 4, :], ring[:, s % SLOTS, corner * C:(corner + 1) * C],
                                            wt[:, b, corner, s:s + 1], val[:, s % 4, :], ALU.mult, ALU.add)
                                        ins.then_inc(part if corner < 3 else value_ready, 1)
                                if pair == 4 or pair == 1:
                                    pass
                            dve.wait_ge(tap_done, KK * (i + 1))
                            dve.wait_ge(x_loaded[b], (n * (GROUPS // 2) + gg + 1) * 16)
                            for h in range(CH):
                                nc.vector.tensor_tensor(xres[:, b, h, :], xres[:, b, h, :], acc[:, b, h, :], ALU.add).then_inc(added, 1)

            @block.tensor
            def _(pe):
                pe.wait_ge(w_loaded, 16)
                with pe.Fori(0, IMAGES) as n:
                    with pe.Fori(0, GROUPS // 2) as gg:
                        for b in range(2):
                            i = (n * (GROUPS // 2) + gg) * 2 + b
                            pe.wait_ge(added, (n * (GROUPS // 2) + gg) * 4)
                            for tap in range(KK + 1):
                                if tap < KK:
                                    pe.wait_ge(val_c_ready, (i * KK + tap - 1) if tap > 1 else i * KK)
                                    for t in range(GROUP):
                                        s = tap * GROUP + t
                                        pe.wait_ge(value_ready, i * STEPS + s + 1)
                                        for h in range(CH):
                                            mm = nc.tensor.transpose(tp[:, (b * KK + tap) % 2, h, t * P:(t + 1) * P],
                                                                     val[:, s % 4, h * P:(h + 1) * P], ident[:])
                                        mm.then_inc(val_free, 1)
                                if tap:
                                    k = tap - 1
                                    pe.wait_ge(val_c_ready, i * KK + k + 1)
                                    for o in range(CH):
                                        for h in range(CH):
                                            mm = nc.tensor.matmul(acc[:, b, o, :], w[:, h, k, o * P:(o + 1) * P], val_c[:, (b * KK + k) % 2, h, :],
                                                                  start=(k == 0 and h == 0), stop=(k == KK - 1 and h == CH - 1),
                                                                  skip_group_check=True)
                                    mm.then_inc(tap_done, 1)


def stage_attention(nc, D, avg, ident):
    with ExitStack() as ctx:
        a = Alloc(nc, ctx, "a_")
        x = a.sb("x", [P, CH, PIX])
        xT = a.sb("xT", [P, TILES, C])
        keys = a.sb("keys", [P, TILES, HID])
        outs = keys[:].rearrange("p t d -> p (t d)")[:, 0:TILES * C].rearrange("p (t c) -> p t c", c=C)
        w = a.sb("w", [P, CH, 3, HID])
        w_out = a.sb("w_out", [P, PAIRS, C])
        g_in = a.sb("g_in", [P, CH])
        g_out = a.sb("g_out", [P, CH])
        b_out = a.sb("b_out", [P, C])
        ones = a.sb("ones", [P, 1])
        rinv = a.sb("rinv", [P, TILES])
        kmax = a.sb("kmax", [P, HID])
        mx = a.sb("mx", [P, PAIRS])
        mxb = a.sb("mxb", [P, PAIRS, P])
        kb = a.sb("kb", [P, HID])
        e = a.sb("e", [P, 4, HID])
        esum = a.sb("esum", [P, HID])
        rs = a.sb("rs", [P, PAIRS])
        gts = a.sb("gts", [P, CH, HID])
        cT = a.sb("cT", [P, PAIRS, P])
        mix = a.sb("mix", [P, PAIRS, C])
        q = a.sb("q", [P, 4, HID])
        qm = a.sb("qm", [P, 4, HEADS])
        qs = a.sb("qs", [P, 4, HEADS])
        qT = a.sb("qT", [P, 2, HID])
        sq = a.sb("sq", [P, C])
        osum = a.sb("osum", [P, TILES])
        oinv = a.sb("oinv", [P, TILES])
        y = a.sb("y", [P, 2, C])
        xo = a.sb("xo", [P, 2, CH, GPIX])
        gn = GroupNorm(a)
        proj = a.ps("proj", [P, 2, HID])
        tp = a.ps("tp", [P, 2, HID])
        gt = a.ps("gt", [P, CH, HID])
        op = a.ps("op", [P, 2, 512])
        averages = op[:, 0, C:C + 2 * CH]
        sums = op[:, 1, C:C + PAIRS]
        sems = {}
        for s in ("w_loaded x_loaded const chain w_ready x_ready x_turned x_squared x_root x_clamped rinv_ready xT_ready "
                  "proj_done k_read kmax_done kmax_turned mx_ready mx_spread kb_ready diff_ready "
                  "e_ready esum_done ctx_used ctx_sum gt_read ctx_done rs_ready cT_ready mix_done mix_ready "
                  "qmax q_read q_exp q_sum q_norm q_turned qT_ready out_done out_ready out_sq oroot oinv_ready y_ready "
                  "y_turned added passed").split():
            sems[s] = a.sem(s)
        S = type("Sems", (), sems)
        stored = [a.sem(f"stored{b}") for b in range(2)]
        res_loaded = [a.sem(f"res_loaded{b}") for b in range(2)]
        U = 2 * GROUP
        RUNS = GROUPS // 2
        CHAIN = CH * GROUPS + CH + 6 + 4

        def laps(eng, lag, steps):
            for c in range(U):
                steps(0, c, lambda k: c >= k)
            with eng.Fori(0, RUNS - 1) as r:
                for c in range(U):
                    steps(r + 1, c, lambda k: True)
            for c in range(lag):
                steps(RUNS, c, lambda k: c < k)

        def written_out(lag, steps):
            for t in range(TILES + lag):
                steps(t // U, t % U, lambda k: k <= t < TILES + k)

        def before(n, lap, c, k):
            at = c + 1 - k
            if isinstance(lap, int):
                return n * TILES + max(lap * U + at, 0)
            return n * TILES + lap * U + at

        with nc.Block() as block:
            @block.sync
            def _(sp):
                for dst, src in ((w, "w_qkv"), (w_out, "w_out"), (g_in, "g_in"), (g_out, "g_out"), (b_out, "b_out")):
                    sp.dma_start(dst[:], D[src]).then_inc(S.w_loaded, 16)
                with sp.Fori(0, IMAGES) as n:
                    with sp.Fori(0, RUNS) as r:
                        for b in range(2):
                            at = bass.ds((2 * r + b) * GPIX, GPIX)
                            sp.wait_ge(stored[b], 16 * (RUNS * n + r))
                            sp.dma_start(xo[:, b], D["x1"][n].rearrange("(h p) q -> p h q", p=P)[:, :, at]).then_inc(res_loaded[b], 16)
                        for b in range(2):
                            at = bass.ds((2 * r + b) * GPIX, GPIX)
                            sp.wait_ge(S.added, CH * (GROUPS * n + 2 * r + b + 1))
                            sp.dma_start(D["x2"][n].rearrange("(h p) q -> p h q", p=P)[:, :, at], xo[:, b]).then_inc(stored[b], 16)
                for b in range(2):
                    sp.wait_ge(stored[b], 16 * IMAGES * RUNS)

            @block.gpsimd
            def _(pool):
                chain = Chain(pool, S.const)
                chain.link(nc.gpsimd.memset(ones[:], 1.0))
                chain.link(nc.gpsimd.memset(cT[:], 0.0))
                with pool.Fori(0, IMAGES) as n:
                    pool.wait_ge(S.proj_done, n * 2 * TILES)
                    pool.sem_inc(S.passed, 1)
                    pool.dma_start(x[:], D["x1"][n].rearrange("(h p) q -> p h q", p=P)).then_inc(S.x_loaded, 16)

                    def esums(lap, c, live):
                        pool.wait_ge(S.e_ready, before(n, lap, c, 0))
                        pool.wait_ge(S.esum_done, before(n, lap, c, 1))
                        pool.sem_inc(S.passed, 1)
                        if isinstance(lap, int) and lap == 0 and c == 0:
                            pool.wait_ge(S.ctx_sum, n)
                            pool.sem_inc(S.passed, 1)
                            nc.gpsimd.tensor_copy(esum[:], e[:, 0, :]).then_inc(S.esum_done, 1)
                        else:
                            nc.gpsimd.tensor_tensor(esum[:], esum[:], e[:, c % 4, :], ALU.add).then_inc(S.esum_done, 1)

                    laps(pool, 0, esums)

            @block.scalar
            def _(act):
                with act.Fori(0, IMAGES) as n:
                    gn.act(nc, act, n)
                    act.wait_ge(gn.ready, n + 1)
                    act.sem_inc(S.passed, 1)
                    for g in range(GROUPS):
                        for h in range(CH):
                            xg = x[:, h, g * GPIX:(g + 1) * GPIX]
                            nc.scalar.activation(xg, xg, ACT.Identity,
                                                 bias=gn.shift[:, h:h + 1], scale=gn.scale[:, h:h + 1]).then_inc(S.x_ready, 1)

                    def pass_a(lap, c, live):
                        if live(0):
                            t = bass.ds(lap * U + c, 1)
                            act.wait_ge(S.x_turned, before(n, lap, c, 0))
                            act.wait_ge(S.x_squared, before(n, lap, c, 1))
                            act.sem_inc(S.passed, 1)
                            nc.scalar.activation(sq[:], tp[:, c % 2, 0:C], ACT.Square, accum_out=rinv[:, t]).then_inc(S.x_squared, 1)
                            act.wait_ge(S.x_squared, before(n, lap, c, 0))
                            act.sem_inc(S.passed, 1)
                            nc.scalar.activation(rinv[:, t], rinv[:, t], ACT.Sqrt).then_inc(S.x_root, 1)
                        if live(1):
                            t = bass.ds(lap * U + c - 1, 1)
                            act.wait_ge(S.proj_done, n * TILES + before(n, lap, c, 1))
                            act.wait_ge(S.rinv_ready, before(n, lap, c, 1))
                            act.sem_inc(S.passed, 1)
                            nc.scalar.activation(keys[:, t, :].rearrange("p t d -> p (t d)"), proj[:, (c - 1) % 2, :], ACT.Copy,
                                                 scale=rinv[:, t]).then_inc(S.k_read, 1)

                    def pass_b(lap, c, live):
                        act.wait_ge(S.diff_ready, before(n, lap, c, 0))
                        nc.scalar.activation(e[:, c % 4, :], e[:, c % 4, :], ACT.Exp).then_inc(S.e_ready, 1)

                    def pass_c(lap, c, live):
                        if live(2):
                            act.wait_ge(S.q_turned, before(n, lap, c, 2))
                            act.wait_ge(S.out_done, before(n, lap, c, 4))
                            nc.scalar.activation(qT[:, c % 2, :], tp[:, c % 2, :], ACT.Copy).then_inc(S.qT_ready, 1)
                        if live(0):
                            act.wait_ge(S.q_read, before(n, lap, c, 0))
                            act.sem_inc(S.passed, 1)
                            nc.scalar.activation(q[:, c % 4, :], q[:, c % 4, :], ACT.Exp,
                                                 scale=rinv[:, bass.ds(lap * U + c, 1)]).then_inc(S.q_exp, 1)
                        if live(4):
                            t = bass.ds(lap * U + c - 4, 1)
                            act.wait_ge(S.out_ready, before(n, lap, c, 4))
                            act.wait_ge(S.out_sq, before(n, lap, c, 5))
                            act.sem_inc(S.passed, 1)
                            nc.scalar.activation(sq[:], outs[:, t, :].rearrange("p t c -> p (t c)"), ACT.Square,
                                                 accum_out=osum[:, t]).then_inc(S.out_sq, 1)

                    laps(act, 1, pass_a)
                    laps(act, 0, pass_b)
                    act.wait_ge(S.ctx_used, (n + 1) * TILES)
                    act.sem_inc(S.passed, 1)
                    nc.scalar.activation(gts[:, 0, :], gt[:, 0, :], ACT.Copy).then_inc(S.gt_read, 1)
                    laps(act, 4, pass_c)
                    act.wait_ge(S.out_sq, (n + 1) * TILES)
                    nc.scalar.activation(oinv[:], osum[:], ACT.Sqrt).then_inc(S.oroot, 1)
                    act.wait_ge(S.oinv_ready, n + 1)
                    act.sem_inc(S.passed, 1)
                    with act.Fori(0, RUNS) as r:
                        for c in range(U):
                            act.wait_ge(S.y_turned, n * TILES + r * U + max(c - 1, 0))
                            act.sem_inc(S.passed, 1)
                            t = bass.ds(r * U + c, 1)
                            nc.scalar.activation(y[:, c % 2, :], outs[:, t, :].rearrange("p t c -> p (t c)"), ACT.Copy,
                                                 scale=oinv[:, t]).then_inc(S.y_ready, 1)

            @block.vector
            def _(dve):
                dve.wait_ge(S.w_loaded, 16 * 5)
                dve.wait_ge(S.const, 2)
                for h in range(CH):
                    nc.vector.tensor_scalar(w[:, h].rearrange("p a b -> p (a b)"), w[:, h].rearrange("p a b -> p (a b)"),
                                            g_in[:, h:h + 1], float(C) ** 0.5, ALU.mult, ALU.mult).then_inc(S.w_ready, 1)
                with dve.Fori(0, IMAGES) as n:
                    chain = Chain(dve, S.chain, n * CHAIN)
                    dve.wait_ge(S.x_loaded, 16 * (n + 1))
                    gn.dve(nc, dve, chain, n, x, averages)

                    def pass_a(lap, c, live):
                        if live(0):
                            t = bass.ds(lap * U + c, 1)
                            dve.wait_ge(S.x_root, before(n, lap, c, 0))
                            dve.sem_inc(S.passed, 1)
                            nc.vector.tensor_scalar(rinv[:, t], rinv[:, t], RMS_EPS, None, ALU.max).then_inc(S.x_clamped, 1)
                            dve.wait_ge(S.x_clamped, before(n, lap, c, 0))
                            dve.sem_inc(S.passed, 1)
                            nc.vector.reciprocal(rinv[:, t], rinv[:, t]).then_inc(S.rinv_ready, 1)
                            dve.wait_ge(S.rinv_ready, before(n, lap, c, 0))
                            dve.sem_inc(S.passed, 1)
                            nc.vector.tensor_scalar(xT[:, t, :].rearrange("p t c -> p (t c)"), tp[:, c % 2, 0:C], rinv[:, t], None,
                                                    ALU.mult).then_inc(S.xT_ready, 1)
                        if live(2):
                            kt = keys[:, bass.ds(lap * U + c - 2, 1), :].rearrange("p t d -> p (t d)")
                            dve.wait_ge(S.k_read, before(n, lap, c, 2))
                            dve.wait_ge(S.kmax_done, before(n, lap, c, 3))
                            dve.sem_inc(S.passed, 1)
                            if isinstance(lap, int) and lap == 0 and c == 2:
                                nc.vector.tensor_copy(kmax[:], kt).then_inc(S.kmax_done, 1)
                            else:
                                nc.vector.tensor_tensor(kmax[:], kmax[:], kt, ALU.max).then_inc(S.kmax_done, 1)

                    def pass_b(lap, c, live):
                        dve.wait_ge(S.ctx_used, before(n, lap, c, 4))
                        dve.wait_ge(S.esum_done, before(n, lap, c, 4))
                        dve.sem_inc(S.passed, 1)
                        nc.vector.tensor_tensor(e[:, c % 4, :], keys[:, bass.ds(lap * U + c, 1), :].rearrange("p t d -> p (t d)"),
                                                kb[:], ALU.subtract).then_inc(S.diff_ready, 1)

                    def pass_c(lap, c, live):
                        if live(4):
                            dve.wait_ge(S.out_done, before(n, lap, c, 4))
                            dve.sem_inc(S.passed, 1)
                            nc.vector.tensor_tensor(outs[:, bass.ds(lap * U + c - 4, 1), :].rearrange("p t c -> p (t c)"), op[:, c % 2, 0:C],
                                                    b_out[:], ALU.add).then_inc(S.out_ready, 1)
                        if live(0):
                            dve.wait_ge(S.proj_done, (n + 1) * TILES + before(n, lap, c, 0))
                            heads = proj[:, c % 2, :].rearrange("p (h d) -> p h d", d=DH)
                            nc.vector.tensor_reduce(qm[:, c % 4, :], heads, AX_X, ALU.max).then_inc(S.qmax, 1)
                            dve.wait_ge(S.qmax, before(n, lap, c, 0))
                            dve.wait_ge(S.q_turned, before(n, lap, c, 4))
                            nc.vector.tensor_tensor(q[:, c % 4, :].rearrange("p (h d) -> p h d", d=DH), heads,
                                                    qm[:, c % 4, :].unsqueeze(2).to_broadcast([P, HEADS, DH]),
                                                    ALU.subtract).then_inc(S.q_read, 1)
                        if live(1):
                            b = (c - 1) % 4
                            qj = q[:, b, :].rearrange("p (h d) -> p h d", d=DH)
                            done = before(n, lap, c, 1)
                            dve.wait_ge(S.q_exp, done)
                            nc.vector.tensor_reduce(qs[:, b, :], qj, AX_X, ALU.add).then_inc(S.q_sum, 1)
                            dve.wait_ge(S.q_sum, 2 * done - 1)
                            nc.vector.reciprocal(qs[:, b, :], qs[:, b, :]).then_inc(S.q_sum, 1)
                            dve.wait_ge(S.q_sum, 2 * done)
                            nc.vector.tensor_tensor(qj, qj, qs[:, b, :].unsqueeze(2).to_broadcast([P, HEADS, DH]),
                                                    ALU.mult).then_inc(S.q_norm, 1)

                    laps(dve, 2, pass_a)
                    dve.wait_ge(S.kmax_turned, n + 1)
                    chain.link(nc.vector.tensor_reduce(mx[:], op[:, 0, :].rearrange("p (j q) -> p j q", q=P), AX_X, ALU.max))
                    nc.vector.tensor_copy(mxb[:], mx[:].unsqueeze(2).to_broadcast([P, PAIRS, P])).then_inc(S.mx_ready, 1)
                    dve.wait_ge(S.mx_spread, n + 1)
                    nc.vector.tensor_copy(kb[:], op[:, 1, :]).then_inc(S.kb_ready, 1)
                    dve.wait_ge(S.kb_ready, n + 1)
                    dve.sem_inc(S.passed, 1)
                    laps(dve, 0, pass_b)
                    dve.wait_ge(S.ctx_used, (n + 1) * TILES)
                    dve.sem_inc(S.passed, 1)
                    nc.vector.tensor_copy(gts[:, 1, :], gt[:, 1, :]).then_inc(S.gt_read, 1)
                    dve.wait_ge(S.ctx_sum, n + 1)
                    chain.link(nc.vector.reciprocal(rs[:], sums))
                    nc.vector.tensor_scalar(rs[:], rs[:], float(DH) ** -0.5, None, ALU.mult).then_inc(S.rs_ready, 1)
                    dve.wait_ge(S.ctx_done, n + 1)
                    for lo in (0, DH):
                        s = slice(lo, lo + DH)
                        nc.vector.tensor_copy(cT[s, :, s], op[s, 0, :].rearrange("p (j d) -> p j d", d=P)[:, :, s]).then_inc(S.cT_ready, 1)
                    dve.wait_ge(S.rs_ready, n + 1)
                    dve.wait_ge(S.mix_done, n + 1)
                    for j in range(PAIRS):
                        nc.vector.tensor_scalar(mix[:, j, :], tp[:, j // 2, (j % 2) * C:(j % 2 + 1) * C], rs[:, j:j + 1], None,
                                                ALU.mult).then_inc(S.mix_ready, 1)
                    laps(dve, 4, pass_c)
                    dve.wait_ge(S.oroot, n + 1)
                    chain.link(nc.vector.tensor_scalar(oinv[:], oinv[:], RMS_EPS, None, ALU.max))
                    chain.link(nc.vector.reciprocal(oinv[:], oinv[:]))
                    nc.vector.tensor_scalar(oinv[:], oinv[:], float(C) ** 0.5, None, ALU.mult).then_inc(S.oinv_ready, 1)
                    with dve.Fori(0, RUNS) as r:
                        for b in range(2):
                            dve.wait_ge(S.y_turned, n * TILES + r * U + (b + 1) * GROUP)
                            dve.wait_ge(res_loaded[b], 16 * (RUNS * n + r + 1))
                            dve.sem_inc(S.passed, 1)
                            for h in range(CH):
                                nc.vector.scalar_tensor_tensor(xo[:, b, h, :], (proj, tp)[b][:, h, :], g_out[:, h:h + 1], xo[:, b, h, :],
                                                               ALU.mult, ALU.add).then_inc(S.added, 1)
                    assert chain.n == CHAIN, chain.n

            @block.tensor
            def _(pe):
                pe.wait_ge(S.w_ready, CH)
                pe.wait_ge(S.const, 2)

                with pe.Fori(0, IMAGES) as n:
                    gn.pe(nc, pe, n, avg, averages)
                    pe.wait_ge(S.added, CH * GROUPS * n)
                    pe.sem_inc(S.passed, 1)

                    def project(lap, c, which):
                        for h in range(CH):
                            mm = nc.tensor.matmul(proj[:, c % 2, :], x[:, h, (lap * U + c) * P:(lap * U + c + 1) * P], w[:, h, which, :],
                                                  start=(h == 0), stop=(h == CH - 1))
                        mm.then_inc(S.proj_done, 1)

                    def pass_a(lap, c, live):
                        if c % GROUP == 0:
                            pe.wait_ge(S.x_ready, CH * (n * GROUPS + lap * 2 + c // GROUP + 1))
                        pe.wait_ge(S.x_squared, before(n, lap, c, 2))
                        pe.wait_ge(S.xT_ready, before(n, lap, c, 2))
                        pe.sem_inc(S.passed, 1)
                        for h in range(CH):
                            mm = nc.tensor.transpose(tp[:, c % 2, h * P:(h + 1) * P], x[:, h, (lap * U + c) * P:(lap * U + c + 1) * P], ident[:])
                        mm.then_inc(S.x_turned, 1)
                        pe.wait_ge(S.k_read, before(n, lap, c, 2))
                        project(lap, c, 1)

                    def pass_b(lap, c, live):
                        pe.wait_ge(S.e_ready, before(n, lap, c, 0))
                        first = isinstance(lap, int) and lap == 0 and c == 0
                        for h in range(CH):
                            mm = nc.tensor.matmul(gt[:, h, :], xT[:, lap * U + c, h * P:(h + 1) * P],
                                                  e[:, c % 4, :], start=first, stop=False, skip_group_check=True)
                        mm.then_inc(S.ctx_used, 1)

                    def pass_c(lap, c, live):
                        if live(0):
                            pe.wait_ge(S.q_read, before(n, lap, c, 2))
                            project(lap, c, 0)
                        if live(2):
                            pe.wait_ge(S.q_norm, before(n, lap, c, 2))
                            pe.wait_ge(S.qT_ready, before(n, lap, c, 4))
                            for p in range(PAIRS):
                                mm = nc.tensor.transpose(tp[:, c % 2, p * P:(p + 1) * P], q[:, (c - 2) % 4, p * P:(p + 1) * P], ident[:])
                            mm.then_inc(S.q_turned, 1)
                        if live(3):
                            pe.wait_ge(S.qT_ready, before(n, lap, c, 3))
                            pe.wait_ge(S.out_ready, before(n, lap, c, 5))
                            b = (c - 3) % 2
                            for p in range(PAIRS):
                                mm = nc.tensor.matmul(op[:, b, 0:C], qT[:, b, p * P:(p + 1) * P], mix[:, p, :],
                                                      start=(p == 0), stop=(p == PAIRS - 1))
                            mm.then_inc(S.out_done, 1)

                    written_out(0, pass_a)
                    pe.wait_ge(S.kmax_done, TILES * (n + 1))
                    for j in range(PAIRS):
                        mm = nc.tensor.transpose(op[:, 0, j * P:(j + 1) * P], kmax[:, j * P:(j + 1) * P], ident[:])
                    mm.then_inc(S.kmax_turned, 1)
                    pe.wait_ge(S.mx_ready, n + 1)
                    for j in range(PAIRS):
                        mm = nc.tensor.matmul(op[:, 1, j * P:(j + 1) * P], mxb[:, j, :], ident[:], start=True, stop=True)
                    mm.then_inc(S.mx_spread, 1)
                    pe.wait_ge(S.xT_ready, TILES * (n + 1))
                    pe.sem_inc(S.passed, 1)
                    written_out(0, pass_b)
                    pe.wait_ge(S.esum_done, TILES * (n + 1))
                    pe.sem_inc(S.passed, 1)
                    for j in range(PAIRS):
                        mm = nc.tensor.matmul(sums[:, j:j + 1], esum[:, j * P:(j + 1) * P], ones[:], start=True, stop=True)
                    mm.then_inc(S.ctx_sum, 1)
                    pe.wait_ge(S.gt_read, 2 * (n + 1))
                    for j in range(PAIRS):
                        s = slice(j * P, (j + 1) * P)
                        for h in range(CH):
                            mm = nc.tensor.matmul(op[:, 0, s], w[:, h, 2, s], gts[:, h, s], start=(h == 0), stop=(h == CH - 1))
                    mm.then_inc(S.ctx_done, 1)
                    pe.wait_ge(S.cT_ready, 2 * (n + 1))
                    for j in range(PAIRS):
                        mm = nc.tensor.matmul(tp[:, j // 2, (j % 2) * C:(j % 2 + 1) * C], cT[:, j, :], w_out[:, j, :], start=True, stop=True)
                    mm.then_inc(S.mix_done, 1)
                    pe.wait_ge(S.k_read, TILES * (n + 1))
                    pe.wait_ge(S.mix_ready, PAIRS * (n + 1))
                    pe.sem_inc(S.passed, 1)
                    written_out(3, pass_c)
                    with pe.Fori(0, RUNS) as r:
                        for b in range(2):
                            pe.wait_ge(S.added, CH * (GROUPS * n + 2 * r + max(b - 1, 0)))
                            for t in range(GROUP):
                                c = b * GROUP + t
                                pe.wait_ge(S.y_ready, n * TILES + r * U + c + 1)
                                for h in range(CH):
                                    mm = nc.tensor.transpose((proj, tp)[b][:, h, t * P:(t + 1) * P], y[:, c % 2, h * P:(h + 1) * P], ident[:])
                                mm.then_inc(S.y_turned, 1)


def stage_involution_filters(nc, D, filts, shift):
    hi, mid, lo_hi = filts
    SIZE = G2 * FLAT
    with ExitStack() as ctx:
        a = Alloc(nc, ctx, "f_")
        w2 = a.sb("w2", [P, G2 * TAPS])
        bn = a.sb("bn", [P, 4, G2 * TAPS])
        flat = a.sb("flat", [P, G2, FLAT])
        rest = a.sb("rest", [P, SIZE])
        flat_shift = a.sb("flat_shift", [1, G2, FLAT])
        one = a.sb("one", [1, 1])
        spread = a.ps("spread", [P, 512])
        loaded = a.sem("loaded")
        chain_sem = a.sem("chain")
        root = a.sem("root")
        shifts_ready = a.sem("shifts_ready")
        spread_done = a.sem("spread_done")

        def taps(v, g, part):
            return v[part, g, LEAD:LEAD + K7 * WX].rearrange("p (a b) -> p a b", b=WX)[:, :, 0:K7]

        def dense(v, g, part):
            return v[part, g * TAPS:(g + 1) * TAPS].rearrange("p (a b) -> p a b", b=K7)

        with nc.Block() as block:
            @block.sync
            def _(sp):
                for half in range(2):
                    sp.dma_start(w2[half * MID:(half + 1) * MID], D["w2"]).then_inc(loaded, 16)
                sp.dma_start(bn[:], D["bn2"]).then_inc(loaded, 16)

            @block.scalar
            def _(act):
                act.wait_ge(chain_sem, 4)
                nc.scalar.activation(bn[:, 3], bn[:, 3], ACT.Sqrt).then_inc(root, 1)

            @block.vector
            def _(dve):
                chain = Chain(dve, chain_sem)
                dve.wait_ge(loaded, 48)
                chain.add(nc.vector.memset(flat[:], 0.0))
                chain.add(nc.vector.memset(flat_shift[:], 0.0))
                chain.add(nc.vector.memset(one[:], 1.0))
                chain.add(nc.vector.tensor_scalar(bn[:, 3], bn[:, 3], BN_EPS, None, ALU.add))
                dve.wait_ge(root, 1)
                chain.link(nc.vector.reciprocal(bn[:, 3], bn[:, 3]))
                chain.link(nc.vector.tensor_tensor(bn[:, 0], bn[:, 0], bn[:, 3], ALU.mult))
                chain.link(nc.vector.tensor_tensor(w2[:], w2[:], bn[:, 0], ALU.mult))
                chain.link(nc.vector.tensor_tensor(bn[:, 2], bn[:, 2], bn[:, 0], ALU.mult))
                chain.link(nc.vector.tensor_tensor(bn[:, 1], bn[:, 1], bn[:, 2], ALU.subtract))
                for g in range(G2):
                    chain.add(nc.vector.tensor_copy(taps(flat, g, slice(0, P)), dense(w2, g, slice(0, P))))
                    ins = nc.vector.tensor_copy(taps(flat_shift, g, slice(0, 1)), dense(bn[:, 1], g, slice(0, 1)))
                    ins.then_inc(shifts_ready, 1)
                dve.wait_ge(chain_sem, chain.value())
                v = flat[:].rearrange("p g f -> p (g f)")
                chain.link(nc.vector.tensor_copy(hi[:], v))
                chain.link(nc.vector.tensor_tensor(rest[:], v, hi[:], ALU.subtract))
                chain.link(nc.vector.tensor_copy(mid[:], rest[:]))
                nc.vector.tensor_tensor(lo_hi[0:MID], rest[0:MID], mid[0:MID], ALU.subtract)
                nc.vector.tensor_copy(lo_hi[MID:P], hi[MID:P])
                dve.wait_ge(spread_done, 1)
                nc.vector.tensor_copy(shift[:], spread[0:WIN, 0:G2 * BPIX])

            @block.tensor
            def _(pe):
                pe.wait_ge(shifts_ready, G2)
                for g in range(G2):
                    for at in range(BPIX):
                        ry, rx = divmod(at, BX)
                        off = ry * WX + rx
                        mm = nc.tensor.matmul(spread[0:WIN, g * BPIX + at:g * BPIX + at + 1], flat_shift[:, g, LEAD - off:FLAT - off],
                                              one[:], start=True, stop=True)
                mm.then_inc(spread_done, 1)


def stage_involution(nc, D, avg, ident, filts, shift):
    GH = G2 // CH
    CHUNKS = 4
    CB = BLOCKS // CHUNKS
    with ExitStack() as ctx:
        a = Alloc(nc, ctx, "i_")
        x = a.sb("x", [P, CH, PIX])
        ym = a.sb("ym", [P, BPIX, 2 * BLOCKS], BF16)
        yl = a.sb("yl", [P, BPIX, 2 * BLOCKS], BF16)
        ym_half = a.sb("ym_half", [P, BPIX, BLOCKS], BF16)
        yl_half = a.sb("yl_half", [P, BPIX, BLOCKS], BF16)
        hi = a.sb("hi", [P, GPIX], BF16)
        mid = a.sb("mid", [P, GPIX], BF16)
        kern = a.sb("kern", [WIN, GH, BPIX, BLOCKS])
        win = a.sb("win", [WIN, 2, CB, P])
        xs = a.sb("xs", [P, 2, CH, GPIX])
        turned = a.sb("turned", [P, 2, GROUP, C])
        w1 = a.sb("w1", [P, CH, P])
        bn1 = a.sb("bn1", [P, 7])
        co = a.sb("co", [P, 8])
        d = a.sb("d", [P, 2, GPIX])
        sg = a.sb("sg", [P, GPIX])
        u = a.sb("u", [P, 2, GPIX])
        quads = a.sb("quads", [P, P // 32])
        own = a.sb("own", [P, 2])
        masked = a.sb("masked", [P, 2, 256])
        inv = a.sb("inv", [P, BLOCKS, BPIX])
        zero = kern[0:PAD2 + 1].rearrange("p g q b -> p (g q b)")[:, 0:(K7 - 1) * C]
        gn = GroupNorm(a)
        tp = a.ps("tp", [P, 2, 2, C])
        kp = a.ps("kp", [P, 4, 4 * BLOCKS])
        sp_ = a.ps("sum", [P, 2, 512])
        small = kp[:, 0, :]
        yp = kp[:, 1, :]
        sems = {}
        for s in ("root1 split kern_read_act patch_ready half_ready w_loaded x_loaded const chain xs_ready yp_done d_ready sg_ready u_ready m_ready y_ready turn_done turn_read "
                  "filled kern_done kern_read sum_done first_read reduced added stored passed").split():
            sems[s] = a.sem(s)
        S = type("Sems", (), sems)
        patched = [a.sem(f"patched{b}") for b in range(2)]
        win_loaded = [a.sem(f"win_loaded{b}") for b in range(2)]
        win_pool = [a.sem(f"win_pool{b}") for b in range(2)]
        WY_SP = 6
        RUNS = GROUPS // 2
        SPLITS = 5
        Y_OPS = 4 * BY
        COEF = 12
        CHAIN = CH * GROUPS + CH + 6
        BANKS = GH * BPIX // 4
        QUAD_CH = 32
        TWO = QUAD_CH // GC
        SB = 16
        SUMS = BLOCKS // SB
        patch = D["patch"]
        EDGE = 3 * PAD2 + 3

        def on_act(k):
            return k % 4 == 3

        ACT_BANKS = sum(on_act(k) for k in range(BANKS))
        DVE_BANKS = BANKS - ACT_BANKS

        def copied(pe, unit, k):
            if k < 4:
                return
            if on_act(k - 4):
                pe.wait_ge(S.kern_read_act, unit * 4 * ACT_BANKS + 4 * sum(on_act(j) for j in range(k - 3)))
            else:
                pe.wait_ge(S.kern_read, unit * DVE_BANKS + sum(not on_act(j) for j in range(k - 3)))

        def load_windows(eng, loaded, n, hf, h, q, wy):
            for by in range(CB // BCOLS):
                row = (hf * HALF_ROWS + q * (HALF_ROWS // CHUNKS) + by * BY + wy) * PAD2
                at = patch[n, bass.ds(row, 1), h * P:(h + 1) * P]
                src = bass.AP(at.tensor, at.offset, [[C, WX], [BX * C, BCOLS], [1, P]])
                dst = win[wy * WX:(wy + 1) * WX, q % 2, by * BCOLS:(by + 1) * BCOLS, :]
                eng.dma_start(dst, src).then_inc(loaded[q % 2], 16)

        with nc.Block() as block:
            @block.sync
            def _(sp):
                sp.dma_start(w1[:], D["w1"]).then_inc(S.w_loaded, 16)
                sp.dma_start(bn1[:], D["bn1"]).then_inc(S.w_loaded, 16)
                sp.wait_ge(S.const, 1)
                with sp.Fori(0, IMAGES) as n:
                    z3 = zero[:, 0:3 * C]
                    for first in (0, PAD2 * PAD2 - EDGE):
                        sp.dma_start(patch[n, bass.ds(first, EDGE), :].rearrange("(p q) c -> p (q c)", q=3), z3[0:EDGE // 3]).then_inc(S.filled, 16)
                    gaps = patch[n, bass.ds(EDGE, (HW - 1) * PAD2), :].rearrange("(r q) c -> r q c", q=PAD2)[:, HW:PAD2, :]
                    sp.dma_start(gaps, zero[0:HW - 1, :].rearrange("p (q c) -> p q c", c=C)).then_inc(S.filled, 16)
                sp.wait_ge(S.filled, 16 * 3 * IMAGES)
                with sp.Fori(0, IMAGES) as n:
                    sp.wait_ge(S.stored, 16 * 4 * n)
                    sp.dma_start(x[:], D["x2"][n].rearrange("(h p) q -> p h q", p=P)).then_inc(S.x_loaded, 16)
                    with sp.Fori(0, RUNS) as r:
                        for b in range(2):
                            sp.wait_ge(S.turn_read, 2 * (GROUPS * n + 2 * r + b + 1))
                            for half in range(2):
                                rows = patch[n, bass.ds((3 + (2 * r + b) * 8) * PAD2, 8 * PAD2), :]
                                dst = rows.rearrange("(t o q) c -> q t o c", o=2, q=PAD2)[3:3 + HW, :, half, :]
                                sp.dma_start(dst, turned[half * HW:(half + 1) * HW, b]).then_inc(patched[b], 16)
                    for b in range(2):
                        sp.wait_ge(patched[b], 32 * RUNS * (n + 1))
                    sp.sem_inc(S.patch_ready, 1)
                    sp.sem_inc(S.passed, 1)
                    with sp.Fori(0, 2) as hf:
                        for h in range(CH):
                            unit = (n * 2 + hf) * CH + h
                            for q in range(CHUNKS):
                                sp.wait_ge(S.sum_done, unit * SUMS + max(q - 1, 0) * SUMS // CHUNKS)
                                for wy in range(WY_SP):
                                    load_windows(sp, win_loaded, n, hf, h, q, wy)
                            sp.wait_ge(S.added, 2 * (unit + 1))
                            dst = D["x3"][n].rearrange("(h p) q -> p h q", p=P)[:, h, bass.ds(hf * (PIX // 2), PIX // 2)]
                            sp.dma_start(dst, x[:, h, bass.ds(hf * (PIX // 2), PIX // 2)]).then_inc(S.stored, 16)
                sp.wait_ge(S.stored, 16 * 4 * IMAGES)

            @block.gpsimd
            def _(pool):
                chain = Chain(pool, S.const)
                chain.link(nc.gpsimd.memset(zero, 0.0))
                chain.link(nc.gpsimd.memset(quads[:], 1.0))
                chain.link(nc.gpsimd.affine_select(out=quads[:], in_=quads[:], compare_op=ALU.is_ge, fill=0.0, base=0,
                                                   pattern=[[-QUAD_CH, P // QUAD_CH]], channel_multiplier=1))
                chain.link(nc.gpsimd.affine_select(out=quads[:], in_=quads[:], compare_op=ALU.is_ge, fill=0.0, base=GC - 1,
                                                   pattern=[[QUAD_CH, P // QUAD_CH]], channel_multiplier=-1))
                with pool.Fori(0, IMAGES) as n:
                    pool.wait_ge(S.patch_ready, n + 1)
                    pool.wait_ge(S.y_ready, Y_OPS * GROUPS * (n + 1))
                    pool.sem_inc(S.passed, 1)
                    with pool.Fori(0, 2) as hf:
                        pool.wait_ge(S.kern_done, (n * 2 + hf) * CH * BANKS)
                        pool.sem_inc(S.passed, 1)
                        for dst, src in ((ym_half, ym), (yl_half, yl)):
                            nc.gpsimd.tensor_copy(dst[:], src[:, :, bass.ds(hf * BLOCKS, BLOCKS)]).then_inc(S.half_ready, 1)
                        for h in range(CH):
                            unit = (n * 2 + hf) * CH + h
                            for q in range(CHUNKS):
                                pool.wait_ge(S.sum_done, unit * SUMS + max(q - 1, 0) * SUMS // CHUNKS)
                                for wy in range(WY_SP, WY):
                                    load_windows(pool, win_pool, n, hf, h, q, wy)
                            pool.wait_ge(S.reduced, (unit + 1) * SUMS)
                            pool.sem_inc(S.passed, 1)
                            half = x[:, h, bass.ds(hf * (PIX // 2), PIX // 2)].rearrange("p (by ry bx rx) -> p by ry bx rx", ry=BY, bx=BCOLS, rx=BX)
                            for ry in range(BY):
                                src = inv[:].rearrange("p (by bx) (ry rx) -> p by bx ry rx", bx=BCOLS, ry=BY)[:, :, :, ry, :]
                                dst = half[:, :, ry, :, :]
                                nc.gpsimd.tensor_tensor(dst, dst, src, ALU.add).then_inc(S.added, 1)

            @block.scalar
            def _(act):
                act.wait_ge(S.chain, 3)
                nc.scalar.activation(co[:, 4:5], co[:, 5:6], ACT.Sqrt).then_inc(S.root1, 1)
                act.wait_ge(S.chain, COEF)
                with act.Fori(0, IMAGES) as n:
                    gn.act(nc, act, n)
                    act.wait_ge(gn.ready, n + 1)
                    act.sem_inc(S.passed, 1)
                    with act.Fori(0, RUNS) as r:
                        for b in range(2):
                            act.wait_ge(S.turn_done, 2 * (GROUPS * n + 2 * r))
                            act.wait_ge(S.yp_done, GROUPS * n + 2 * r)
                            act.sem_inc(S.passed, 1)
                            for h in range(CH):
                                nc.scalar.activation(xs[:, b, h, :], x[:, h, bass.ds((2 * r + b) * GPIX, GPIX)], ACT.Identity,
                                                     bias=gn.shift[:, h:h + 1], scale=gn.scale[:, h:h + 1]).then_inc(S.xs_ready, 1)
                        for b in range(2):
                            act.wait_ge(S.yp_done, GROUPS * n + 2 * r + b + 1)
                            act.wait_ge(S.m_ready, GROUPS * n + 2 * r)
                            act.wait_ge(S.u_ready, GROUPS * n + 2 * r + b)
                            nc.scalar.activation(d[:, b, :], yp, ACT.Identity, bias=co[:, 1:2], scale=co[:, 0:1]).then_inc(S.d_ready, 1)
                            act.wait_ge(S.d_ready, GROUPS * n + 2 * r + b + 1)
                            act.wait_ge(S.m_ready, GROUPS * n + 2 * r + b)
                            act.sem_inc(S.passed, 1)
                            nc.scalar.activation(sg[:], d[:, b, :], ACT.Sigmoid, scale=bn1[:, 6:7]).then_inc(S.sg_ready, 1)
                    act.sem_inc(S.passed, 1)
                    with act.Fori(0, 2) as hf:
                        for h in range(CH):
                            unit = (n * 2 + hf) * CH + h
                            act.wait_ge(S.sum_done, unit * SUMS)
                            for k in range(BANKS):
                                if on_act(k):
                                    act.wait_ge(S.kern_done, unit * BANKS + k + 1)
                                    g, at = divmod(4 * k, BPIX)
                                    for j in range(4):
                                        col = (h * GH + g) * BPIX + at + j
                                        nc.scalar.activation(kern[:, g, at + j, :], kp[0:WIN, k % 4, j * BLOCKS:(j + 1) * BLOCKS],
                                                             ACT.Identity, bias=shift[:, col:col + 1]).then_inc(S.kern_read_act, 1)

            @block.vector
            def _(dve):
                chain = Chain(dve, S.chain)
                dve.wait_ge(S.w_loaded, 32)
                dve.wait_ge(S.const, 4)
                chain.link(nc.vector.tensor_reduce(own[:, 0:1], quads[:], AX_X, ALU.add))
                chain.link(nc.vector.tensor_scalar(own[:, 1:2], own[:, 0:1], -1.0, 1.0, ALU.mult, ALU.add))
                gamma, beta, mean, var, p1, p2 = (bn1[:, k:k + 1] for k in range(6))
                s, t, dp = (co[:, k:k + 1] for k in (4, 5, 6))
                chain.link(nc.vector.tensor_scalar(t, var, BN_EPS, None, ALU.add))
                dve.wait_ge(S.root1, 1)
                chain.link(nc.vector.reciprocal(s, s))
                chain.link(nc.vector.tensor_tensor(s, s, gamma, ALU.mult))
                chain.link(nc.vector.tensor_tensor(t, mean, s, ALU.mult))
                chain.link(nc.vector.tensor_tensor(t, beta, t, ALU.subtract))
                chain.link(nc.vector.tensor_tensor(dp, p1, p2, ALU.subtract))
                chain.link(nc.vector.tensor_tensor(co[:, 0:1], dp, s, ALU.mult))
                chain.link(nc.vector.tensor_tensor(co[:, 1:2], dp, t, ALU.mult))
                chain.link(nc.vector.tensor_tensor(co[:, 2:3], p2, s, ALU.mult))
                chain.link(nc.vector.tensor_tensor(co[:, 3:4], p2, t, ALU.mult))
                assert chain.n == COEF
                with dve.Fori(0, IMAGES) as n:
                    chain = Chain(dve, S.chain, n * CHAIN + COEF)
                    dve.wait_ge(S.x_loaded, 16 * (n + 1))
                    gn.dve(nc, dve, chain, n, x, small[:, 0:2 * CH])
                    assert chain.n == CHAIN, chain.n
                    dve.sem_inc(S.passed, 1)
                    with dve.Fori(0, RUNS) as r:
                        for b in range(2):
                            i = GROUPS * n + 2 * r + b
                            for half in range(2):
                                dve.wait_ge(S.turn_done, 2 * i + half + 1)
                                dve.wait_ge(patched[b], 32 * (RUNS * n + r))
                                nc.vector.tensor_copy(turned[:, b, 2 * half:2 * half + 2, :], tp[:, half]).then_inc(S.turn_read, 1)
                            dve.wait_ge(S.d_ready, i + 1)
                            nc.vector.tensor_scalar(u[:, b, :], yp, co[:, 2:3], co[:, 3:4], ALU.mult, ALU.add).then_inc(S.u_ready, 1)
                            dve.wait_ge(S.sg_ready, i + 1)
                            nc.vector.tensor_tensor(d[:, b, :], d[:, b, :], sg[:], ALU.mult).then_inc(S.m_ready, 1)
                            dve.wait_ge(S.m_ready, i + 1)
                            dve.wait_ge(S.u_ready, i + 1)
                            dve.wait_ge(S.half_ready, 4 * n)
                            dve.sem_inc(S.passed, 1)
                            def split(m, ins):
                                ins.then_inc(S.split, 1)
                                dve.wait_ge(S.split, SPLITS * i + m)

                            def place(dst, src, part):
                                per = GPIX // BPIX
                                for ry in range(BY):
                                    to = dst[part, ry * BX:(ry + 1) * BX, bass.ds((2 * r + b) * per, per)].rearrange("p rx (by bx) -> p by bx rx", bx=BCOLS)
                                    of = src[part].rearrange("p (by ry bx rx) -> p by ry bx rx", ry=BY, bx=BCOLS, rx=BX)[:, :, ry]
                                    nc.vector.tensor_copy(to, of).then_inc(S.y_ready, 1)

                            lower, upper = slice(0, MID), slice(MID, P)
                            split(1, nc.vector.tensor_tensor(u[:, b, :], d[:, b, :], u[:, b, :], ALU.add))
                            split(2, nc.vector.tensor_copy(hi[:], u[:, b, :]))
                            split(3, nc.vector.tensor_tensor(u[:, b, :], u[:, b, :], hi[:], ALU.subtract))
                            split(4, nc.vector.tensor_copy(mid[:], u[:, b, :]))
                            place(ym, hi, lower)
                            place(yl, hi, lower)
                            place(ym, mid, upper)
                            split(5, nc.vector.tensor_tensor(u[:, b, :], u[:, b, :], mid[:], ALU.subtract))
                            place(yl, u[:, b, :], upper)
                            dve.wait_ge(S.y_ready, Y_OPS * (i + 1))
                            dve.sem_inc(S.passed, 1)
                    dve.sem_inc(S.passed, 1)
                    with dve.Fori(0, 2) as hf:
                        for h in range(CH):
                            unit = (n * 2 + hf) * CH + h
                            dve.wait_ge(S.sum_done, unit * SUMS)
                            for k in range(BANKS):
                                if not on_act(k):
                                    dve.wait_ge(S.kern_done, unit * BANKS + k + 1)
                                    g, at = divmod(4 * k, BPIX)
                                    col = (h * GH + g) * BPIX + at
                                    nc.vector.tensor_tensor(kern[:, g, at:at + 4, :], kp[0:WIN, k % 4, :].rearrange("p (a b) -> p a b", a=4),
                                                            shift[:, col:col + 4].unsqueeze(2).to_broadcast([WIN, 4, BLOCKS]),
                                                            ALU.add).then_inc(S.kern_read, 1)
                            for k in range(SUMS):
                                dve.wait_ge(S.sum_done, unit * SUMS + k + 1)
                                dve.wait_ge(S.reduced, unit * SUMS + max(k - 1, 0))
                                both = sp_[:, k % 2, :].rearrange("p (a g q) -> p a g q", a=SB, g=TWO)
                                part = masked[:, k % 2, :].rearrange("p (a q) -> p a q", a=SB)
                                nc.vector.tensor_scalar(part, both[:, :, 0, :], own[:, 0:1], None, ALU.mult).then_inc(S.first_read, 1)
                                if k == 0:
                                    dve.wait_ge(S.added, 2 * unit)
                                dve.wait_ge(S.first_read, unit * SUMS + k + 1)
                                nc.vector.scalar_tensor_tensor(inv[:, SB * k:SB * (k + 1), :], both[:, :, 1, :], own[:, 1:2], part,
                                                               ALU.mult, ALU.add).then_inc(S.reduced, 1)

            @block.tensor
            def _(pe):
                pe.wait_ge(S.w_loaded, 32)
                with pe.Fori(0, IMAGES) as n:
                    gn.pe(nc, pe, n, avg, small[:, 0:2 * CH])
                    pe.sem_inc(S.passed, 1)
                    with pe.Fori(0, RUNS) as r:
                        for b in range(2):
                            i = GROUPS * n + 2 * r + b
                            pe.wait_ge(S.xs_ready, CH * (i + 1))
                            pe.wait_ge(S.u_ready, i)
                            for h in range(CH):
                                mm = nc.tensor.matmul(yp, w1[:, h, :], xs[:, b, h, :], start=(h == 0), stop=(h == CH - 1))
                            mm.then_inc(S.yp_done, 1)
                            for half in range(2):
                                pe.wait_ge(S.turn_read, 2 * i + max(half - 1, 0))
                                for t in range(2):
                                    for h in range(CH):
                                        s = (2 * half + t) * P
                                        mm = nc.tensor.transpose(tp[:, half, t, h * P:(h + 1) * P], xs[:, b, h, s:s + P], ident[:])
                                mm.then_inc(S.turn_done, 1)
                    with pe.Fori(0, 2) as hf:
                        pe.wait_ge(S.half_ready, 2 * (n * 2 + hf + 1))
                        for h in range(CH):
                            unit = (n * 2 + hf) * CH + h
                            for k in range(BANKS):
                                copied(pe, unit, k)
                                for j in range(4):
                                    g, at = divmod(4 * k + j, BPIX)
                                    ry, rx = divmod(at, BX)
                                    col = LEAD - ry * WX - rx
                                    for part, (f, v) in enumerate(zip(filts, (ym_half, ym_half, yl_half))):
                                        at_g = (h * GH + g) * FLAT + col
                                        mm = nc.tensor.matmul(kp[0:WIN, k % 4, j * BLOCKS:(j + 1) * BLOCKS], f[:, at_g:at_g + WIN], v[:, at, :],
                                                              start=(part == 0), stop=(part == 2))
                                mm.then_inc(S.kern_done, 1)
                            pe.wait_ge(S.kern_read, (unit + 1) * DVE_BANKS)
                            pe.wait_ge(S.kern_read_act, (unit + 1) * 4 * ACT_BANKS)
                            for k in range(SUMS):
                                q, first = divmod(SB * k, CB)
                                if first == 0:
                                    turns = unit * (CHUNKS // 2) + q // 2 + 1
                                    pe.wait_ge(win_loaded[q % 2], turns * 16 * WY_SP * (CB // BCOLS))
                                    pe.wait_ge(win_pool[q % 2], turns * 16 * (WY - WY_SP) * (CB // BCOLS))
                                pe.wait_ge(S.reduced, unit * SUMS + max(k - 1, 0))
                                for j in range(SB):
                                    for t in range(P // QUAD_CH):
                                        ch = slice(t * QUAD_CH, (t + 1) * QUAD_CH)
                                        mm = nc.tensor.matmul(sp_[ch, k % 2, j * TWO * BPIX:(j + 1) * TWO * BPIX], win[:, q % 2, first + j, ch],
                                                              kern[:, TWO * t:TWO * (t + 1), :, SB * k + j].rearrange("p g q -> p (g q)"),
                                                              start=True, stop=True)
                                mm.then_inc(S.sum_done, 1)


def stage_filter(nc, D, avg):
    with ExitStack() as ctx:
        a = Alloc(nc, ctx, "u_")
        W1 = HW + 1
        x = a.sb("x", [P, CH, PIX])
        xn = a.sb("xn", [P, CH, W1 * W1])
        f = a.sb("f", [P, CH, 16])
        gn = GroupNorm(a)
        small = a.ps("small", [P, 512])
        loaded = a.sem("loaded")
        x_loaded = a.sem("x_loaded")
        chain_sem = a.sem("chain")
        const = a.sem("const")
        normalised = a.sem("normalised")
        done = a.sem("done")
        stored = a.sem("stored")
        CHAIN = CH * GROUPS + CH + 6 + 6

        with nc.Block() as block:
            @block.sync
            def _(sp):
                sp.dma_start(f[:], D["filt"]).then_inc(loaded, 16)
                with sp.Fori(0, IMAGES) as n:
                    sp.wait_ge(stored, 16 * n)
                    sp.dma_start(x[:], D["x3"][n].rearrange("(h p) q -> p h q", p=P)).then_inc(x_loaded, 16)
                    sp.wait_ge(done, CH * (n + 1))
                    sp.dma_start(D["out"][n].rearrange("(h p) q -> p h q", p=P), x[:]).then_inc(stored, 16)
                sp.wait_ge(stored, 16 * IMAGES)

            @block.gpsimd
            def _(pool):
                nc.gpsimd.memset(xn[:], 0.0).then_inc(const, 1)

            @block.scalar
            def _(act):
                act.wait_ge(const, 1)
                with act.Fori(0, IMAGES) as n:
                    gn.act(nc, act, n)
                    act.wait_ge(gn.ready, n + 1)
                    for h in range(CH):
                        nc.scalar.activation(xn[:, h].rearrange("p (r c) -> p r c", c=W1)[:, 0:HW, 0:HW],
                                             x[:, h].rearrange("p (r c) -> p r c", c=HW), ACT.Identity,
                                             bias=gn.shift[:, h:h + 1], scale=gn.scale[:, h:h + 1]).then_inc(normalised, 1)

            @block.vector
            def _(dve):
                dve.wait_ge(loaded, 16)
                with dve.Fori(0, IMAGES) as n:
                    chain = Chain(dve, chain_sem, n * CHAIN)
                    dve.wait_ge(x_loaded, 16 * (n + 1))
                    gn.dve(nc, dve, chain, n, x, small[:, 0:2 * CH])
                    dve.wait_ge(normalised, CH * (n + 1))
                    taps = [(0, 0), (0, 1), (1, 0), (1, 1)]
                    for dy, dx in taps:
                        for h in range(CH):
                            at = 4 * (2 * dy + 1) + 2 * dx + 1
                            xh = x[:, h].rearrange("p (r c) -> p r c", c=HW)
                            src = xn[:, h].rearrange("p (r c) -> p r c", c=W1)[:, dy:dy + HW, dx:dx + HW]
                            ins = nc.vector.scalar_tensor_tensor(xh, src, f[:, h, at:at + 1], xh, ALU.mult, ALU.add)
                            if (dy, dx) == taps[-1]:
                                ins.then_inc(done, 1)
                            else:
                                chain.add(ins)
                        if (dy, dx) != taps[-1]:
                            dve.wait_ge(chain_sem, chain.value())
                    assert chain.n == CHAIN, chain.n

            @block.tensor
            def _(pe):
                with pe.Fori(0, IMAGES) as n:
                    gn.pe(nc, pe, n, avg, small[:, 0:2 * CH])


def build_program(nc, D, stages=("0", "1", "2", "3")):
    with ExitStack() as ctx:
        a = Alloc(nc, ctx, "g_")
        avg = a.sb("avg", [P, P])
        ident = a.sb("ident", [P, P])
        const = a.sem("const")
        with nc.Block() as block:
            @block.gpsimd
            def _(pool):
                chain = Chain(pool, const)
                group_average_matrix(nc, pool, chain, avg)
                identity_matrix(nc, pool, chain, ident)
        if "0" in stages:
            with ExitStack() as ctx0:
                a0 = Alloc(nc, ctx0, "l0_")
                all_idx = a0.sb("idx", [P, IMAGES, TILES * KK], I32)
                all_wt = a0.sb("wt", [P, IMAGES, 4, TILES * KK])
                stage_offsets(nc, D, avg, ident, all_idx, all_wt)
                stage_deform(nc, D, ident, all_idx[:].bitcast(U32), all_wt)
        if "1" in stages:
            stage_attention(nc, D, avg, ident)
        if "2" in stages:
            with ExitStack() as ctx2:
                a2 = Alloc(nc, ctx2, "l2_")
                filts = [a2.sb(f"filt{k}", [P, G2 * FLAT], BF16) for k in range(3)]
                shift = a2.sb("shift", [WIN, G2 * BPIX])
                stage_involution_filters(nc, D, filts, shift)
                stage_involution(nc, D, avg, ident, filts, shift)
        if "3" in stages:
            stage_filter(nc, D, avg)


def layouts(inp):
    import numpy as np

    def put(a):
        return np.ascontiguousarray(a)

    out = {"x": put(inp["x"].reshape(IMAGES, C, PIX))}
    w = inp["L0_conv_conv_offset_w"].reshape(3 * KK, CH, P, KK)
    b = inp["L0_conv_conv_offset_b"]
    w = np.concatenate([w[0:2 * KK:2], w[1:2 * KK:2], w[2 * KK:]])
    b = np.concatenate([b[0:2 * KK:2], b[1:2 * KK:2], b[2 * KK:]])
    w = np.concatenate([w, np.zeros((OM - 3 * KK,) + w.shape[1:], w.dtype)])
    b = np.concatenate([b, np.zeros(OM - 3 * KK, b.dtype)])
    out["w_off"] = put(w.transpose(2, 1, 3, 0))
    out["b_off"] = put(np.tile(b, P // OM).reshape(P, 1))
    out["w_dcn"] = put(inp["L0_conv_dcn_weight"].reshape(C, CH, P, KK).transpose(2, 1, 3, 0))

    def by_partition(v):
        return put(v.reshape(CH, P).T)

    w = inp["L1_conv_w_qkv"].reshape(3, HID, CH, P)
    out["w_qkv"] = put(w.transpose(3, 2, 0, 1))
    out["w_out"] = put(inp["L1_conv_w_out"].reshape(C, PAIRS, P).transpose(2, 1, 0))
    out["g_in"] = by_partition(inp["L1_conv_g_norm"])
    out["g_out"] = by_partition(inp["L1_conv_g_out"])
    out["b_out"] = put(np.broadcast_to(inp["L1_conv_b_out"], (P, C)))

    w = inp["L2_conv_w1"].reshape(MID, CH, P).transpose(2, 1, 0)
    out["w1"] = put(np.concatenate([w, w], axis=2))
    names = ("bn1_gamma", "bn1_beta", "bn1_mean", "bn1_var", "acon_p1", "acon_p2", "acon_beta")
    out["bn1"] = put(np.tile(np.stack([inp["L2_conv_" + k] for k in names], axis=1), (2, 1)))
    out["w2"] = put(inp["L2_conv_w2"].T)
    bn2 = np.stack([inp["L2_conv_bn2_" + k] for k in ("gamma", "beta", "mean", "var")])
    out["bn2"] = put(np.broadcast_to(bn2, (P,) + bn2.shape))
    out["filt"] = put(inp["L3_conv_filt"].reshape(CH, P, 16).transpose(1, 0, 2))
    return out


SCRATCH = {
    "table": (IMAGES * QROWS, 4 * C),
    "x1": (IMAGES, C, PIX),
    "x2": (IMAGES, C, PIX),
    "patch": (IMAGES, PAD2 * PAD2, C),
    "x3": (IMAGES, C, PIX),
}


def kernel(**inputs):
    import numpy as np
    from concourse import bacc
    from concourse.bass_utils import run_bass_kernel_spmd

    nc = bacc.Bacc("TRN2", target_bir_lowering=False, num_devices=1)
    arrays = layouts(inputs)
    D = {k: nc.dram_tensor("in_" + k, v.shape, F32, kind="ExternalInput").ap() for k, v in arrays.items()}
    for k, shape in SCRATCH.items():
        D[k] = nc.dram_tensor(k, shape, F32, kind="Internal").ap()
    D["out"] = nc.dram_tensor("out", (IMAGES, C, PIX), F32, kind="ExternalOutput").ap()
    build_program(nc, D)
    r = run_bass_kernel_spmd(nc, [{"in_" + k: v for k, v in arrays.items()}], core_ids=[0])
    return r.results[0]["out"].reshape(IMAGES, C, HW, HW)
```

```python
from contextlib import ExitStack

import concourse.bass as bass
from concourse import mybir

ALU = mybir.AluOpType
ACT = mybir.ActivationFunctionType
AX_X = mybir.AxisListType.X
F32 = mybir.dt.float32
I32 = mybir.dt.int32
BF16 = mybir.dt.bfloat16
U32 = mybir.dt.uint32

P = 128
IMAGES = 4
C = 256
CH = C // P
HW = 64
PIX = HW * HW
TILE_ROWS = P // HW
TILES = PIX // P
GROUP = 4
GPIX = GROUP * P
GROUPS = TILES // GROUP
GN_CH = 8
GN_EPS = 1e-5

KK = 9
PADW = HW + 3
POS = PADW * PADW
POS_TILES = -(-POS // (GROUP * P)) * GROUP
POS_PAD = POS_TILES * P
LINE = (0, PADW)
QBASE = PADW
QROWS = POS_PAD + QBASE
STEPS = KK * GROUP
OM = 32

HEADS, DH = 8, 64
HID = HEADS * DH
PAIRS = HID // P
RMS_EPS = 1e-12

MID = 64
K7 = 7
TAPS = K7 * K7
G2 = 16
GC = C // G2
BN_EPS = 1e-3
BY, BX = 2, 8
WY, WX = BY + K7 - 1, BX + K7 - 1
WIN = WY * WX
BPIX = BY * BX
PAD2 = HW + K7 - 1
PITCH = -(-PAD2 // BX) * BX
BLINE = PITCH // BX
PLANE = PAD2 // 2 * PITCH
LEAD = 2 * WX
FLAT = LEAD + WIN
HALF_ROWS = HW // 2
BLOCKS = (HALF_ROWS // BY) * (HW // BX)
BCOLS = HW // BX


class Chain:

    def __init__(self, eng, sem, base=0):
        self.eng, self.sem, self.base, self.n = eng, sem, base, 0

    def value(self):
        return self.base + self.n

    def add(self, ins):
        self.n += 1
        ins.then_inc(self.sem, 1)

    def link(self, ins):
        self.add(ins)
        self.eng.wait_ge(self.sem, self.value())


class Alloc:

    def __init__(self, nc, ctx, tag, passed=None):
        self.nc, self.ctx, self.tag, self.passed = nc, ctx, tag, passed

    def sb(self, name, shape, dt=F32):
        return self.ctx.enter_context(self.nc.sbuf_tensor(self.tag + name, shape, dt))

    def ps(self, name, shape):
        return self.ctx.enter_context(self.nc.psum_tensor(self.tag + name, shape, F32))

    def sem(self, name):
        return self.ctx.enter_context(self.nc.semaphore(self.tag + name))


def group_average_matrix(nc, pool, chain, avg):
    chain.link(nc.gpsimd.memset(avg[:], 1.0 / GN_CH))
    view = avg[:].rearrange("p (g c) -> p g c", c=GN_CH)
    chain.link(nc.gpsimd.affine_select(out=view, in_=view, compare_op=ALU.is_ge, fill=0.0, base=0,
                                       pattern=[[-GN_CH, P // GN_CH], [0, GN_CH]], channel_multiplier=1))
    chain.link(nc.gpsimd.affine_select(out=view, in_=view, compare_op=ALU.is_ge, fill=0.0, base=GN_CH - 1,
                                       pattern=[[GN_CH, P // GN_CH], [0, GN_CH]], channel_multiplier=-1))


def identity_matrix(nc, pool, chain, ident):
    chain.link(nc.gpsimd.memset(ident[:], 0.0))
    chain.link(nc.gpsimd.affine_select(out=ident[:], in_=ident[:], compare_op=ALU.not_equal, fill=1.0, base=0,
                                       pattern=[[-1, P]], channel_multiplier=1))




class GroupNorm:

    def __init__(self, a):
        self.stats = a.sb("gn_stats", [P, CH, GROUPS, 6])
        self.mv = a.sb("gn_mv", [P, CH, 2])
        self.mom = a.sb("gn_mom", [P, CH, 2])
        self.gm = a.sb("gn_gm", [P, CH, 2])
        self.var = a.sb("gn_var", [P, CH])
        self.std = a.sb("gn_std", [P, CH])
        self.scale = a.sb("gn_scale", [P, CH])
        self.shift = a.sb("gn_shift", [P, CH])
        self.passed = a.passed
        self.moments = a.sem("gn_moments")
        self.averaged = a.sem("gn_averaged")
        self.variance = a.sem("gn_variance")
        self.root = a.sem("gn_root")
        self.ready = a.sem("gn_ready")

    def dve(self, nc, dve, chain, n, x, ps, lax=False):
        for h in range(CH):
            for g in range(GROUPS):
                chain.add(nc.vector.bn_stats(self.stats[:, h, g, :], x[:, h, g * GPIX:(g + 1) * GPIX]))
        dve.wait_ge(chain.sem, chain.value())
        dve.sem_inc(self.passed, 1)
        for h in range(CH):
            chain.add(nc.vector.bn_aggr(self.mv[:, h, :], self.stats[:, h, :, :].rearrange("p g s -> p (g s)")))
        dve.wait_ge(chain.sem, chain.value())
        self.dve_rest(nc, dve, chain, n, ps)

    def dve_rest(self, nc, dve, chain, n, ps):
        chain.link(nc.vector.tensor_tensor(self.mom[:, :, 1], self.mv[:, :, 0], self.mv[:, :, 0], ALU.mult))
        nc.vector.tensor_tensor(self.mom[:, :, 1], self.mom[:, :, 1], self.mv[:, :, 1], ALU.add).then_inc(self.moments, 1)
        nc.vector.tensor_copy(self.mom[:, :, 0], self.mv[:, :, 0]).then_inc(self.moments, 1)
        dve.wait_ge(self.averaged, n + 1)
        chain.link(nc.vector.tensor_copy(self.gm[:].rearrange("p h s -> p (h s)"), ps))
        chain.link(nc.vector.tensor_tensor(self.var[:], self.gm[:, :, 0], self.gm[:, :, 0], ALU.mult))
        chain.link(nc.vector.tensor_tensor(self.var[:], self.gm[:, :, 1], self.var[:], ALU.subtract))
        nc.vector.tensor_scalar(self.var[:], self.var[:], GN_EPS, None, ALU.add).then_inc(self.variance, 1)
        dve.wait_ge(self.root, n + 1)
        chain.link(nc.vector.reciprocal(self.scale[:], self.std[:]))
        chain.link(nc.vector.tensor_tensor(self.shift[:], self.gm[:, :, 0], self.scale[:], ALU.mult))
        nc.vector.tensor_scalar(self.shift[:], self.shift[:], -1.0, None, ALU.mult).then_inc(self.ready, 1)
        dve.wait_ge(self.ready, n + 1)

    def pe(self, nc, pe, n, avg, ps):
        pe.wait_ge(self.moments, 2 * (n + 1))
        nc.tensor.matmul(ps, avg[:], self.mom[:].rearrange("p h s -> p (h s)"), start=True, stop=True).then_inc(self.averaged, 1)

    def act(self, nc, act, n):
        act.wait_ge(self.variance, n + 1)
        nc.scalar.activation(self.std[:], self.var[:], ACT.Sqrt).then_inc(self.root, 1)


def stage_offsets(nc, D, passed, avg, ident, all_idx, all_wt):
    with ExitStack() as ctx:
        a = Alloc(nc, ctx, "o_", passed)
        x = a.sb("x", [P, CH, PIX])
        xp = a.sb("xp", [P, CH, POS_PAD])
        w_off = a.sb("w_off", [P, CH, KK, OM])
        b_off = a.sb("b_off", [P, 1])
        quad = a.sb("quad", [P, 2, GROUP, C])
        om_c = a.sb("om_c", [P, 2, GPIX])
        om = a.sb("om", [P, TILES, 3 * KK])
        mask = a.sb("mask", [P, TILES, KK])
        grid = a.sb("grid", [P, 2, TILES * KK])
        pos = a.sb("pos", [P, 2, TILES * KK])
        pos_i = a.sb("pos_i", [P, 2, TILES * KK], I32)
        low = a.sb("low", [P, 2, TILES * KK])
        frac = a.sb("frac", [P, 2, TILES * KK])
        rest = a.sb("rest", [P, 2, TILES * KK])
        over = a.sb("over", [P, 2, TILES * KK])
        row = a.sb("row", [P, TILES * KK])
        base = a.sb("base", [P, 1])
        zero = a.sb("zero", [QBASE, C])
        gn = GroupNorm(a)
        tp = a.ps("tp", [P, 2, 2, 512])
        cv = a.ps("cv", [P, 2, 512])
        ot = a.ps("ot", [P, GROUP, P])
        gp = a.ps("gp", [P, 512])
        w_loaded = a.sem("w_loaded")
        x_loaded = a.sem("x_loaded")
        const = a.sem("const")
        chain_sem = a.sem("chain")
        normalised = a.sem("normalised")
        transposed = a.sem("transposed")
        tp_free = a.sem("tp_free")
        quad_stored = [a.sem(f"quad_stored{b}") for b in range(2)]
        conv_done = a.sem("conv_done")
        om_c_ready = a.sem("om_c_ready")
        om_t = a.sem("om_t")
        om_ready = a.sem("om_ready")
        mask_ready = a.sem("mask_ready")
        passed = a.passed
        filled = a.sem("filled")
        BATCH = POS_TILES // GROUP
        SETS = GROUPS // 4
        AFTER = (1, 4)
        DVE_STEPS = CH * GROUPS + CH + 6 + 12 + 5

        with nc.Block() as block:
            @block.sync
            def _(sp):
                sp.dma_start(w_off[:], D["w_off"]).then_inc(w_loaded, 16)
                sp.dma_start(b_off[:], D["b_off"]).then_inc(w_loaded, 16)
                sp.wait_ge(const, 7)
                with sp.Fori(0, IMAGES) as n:
                    for corner, off in enumerate(LINE):
                        for first, rows in ((0, QBASE - off), (QROWS - off, off)):
                            if rows:
                                sp.dma_start(D["table"][bass.ds(n * QROWS + first, rows), corner * C:(corner + 1) * C],
                                             zero[0:rows]).then_inc(filled, 16)
                    for b in range(BATCH):
                        sp.wait_ge(tp_free, 2 * BATCH * n + 2 * (b + 1))
                        for corner, off in enumerate(LINE):
                            first = QBASE - off + b * GPIX
                            dst = D["table"][bass.ds(n * QROWS + first, GPIX), corner * C:(corner + 1) * C]
                            sp.dma_start(dst.rearrange("(t p) c -> p t c", p=P), quad[:, b % 2]).then_inc(quad_stored[b % 2], 16)
                sp.wait_ge(filled, 16 * 2 * IMAGES)
                sp.wait_ge(quad_stored[0], 32 * IMAGES * -(-BATCH // 2))
                sp.wait_ge(quad_stored[1], 32 * IMAGES * (BATCH // 2))

            @block.gpsimd
            def _(pool):
                def load(n):
                    pool.dma_start(x[:], D["x"][n].rearrange("(h p) q -> p h q", p=P)).then_inc(x_loaded, 16)

                load(0)
                chain = Chain(pool, const)
                chain.link(nc.gpsimd.memset(xp[:], 0.0))
                for half in range(TILE_ROWS):
                    part = slice(half * HW, (half + 1) * HW)
                    for axis in range(2):
                        by = [[2 * GROUP, GROUPS], [1, 3], [0, 3], [2, GROUP]]
                        bx = [[0, GROUPS], [0, 3], [1, 3], [0, GROUP]]
                        chain.link(nc.gpsimd.iota(grid[part, axis, :].rearrange("p (g a b t) -> p g a b t", g=GROUPS, a=3, b=3),
                                       by if axis == 0 else bx, base=half if axis == 0 else 0,
                                       channel_multiplier=0 if axis == 0 else 1,
                                       allow_small_or_imprecise_dtypes=True))
                chain.link(nc.gpsimd.memset(base[:], float(QBASE)))
                chain.link(nc.gpsimd.memset(zero[:], 0.0))
                pool.sem_inc(passed, 1)
                with pool.Fori(0, IMAGES - 1) as n:
                    pool.wait_ge(normalised, CH * (n + 1))
                    pool.sem_inc(passed, 1)
                    load(n + 1)

            @block.vector
            def _(dve):
                dve.wait_ge(const, 7)
                with dve.Fori(0, IMAGES) as n:
                    chain = Chain(dve, chain_sem, n * DVE_STEPS)
                    dve.wait_ge(x_loaded, 16 * (n + 1))
                    gn.dve(nc, dve, chain, n, x, gp[:, 0:2 * CH])
                    dve.wait_ge(transposed, 2 * BATCH * n)
                    dve.wait_ge(conv_done, SETS * n)
                    inner = xp[:, 0, PADW + 1:PADW + 1 + HW * PADW].rearrange("p (r c) -> p r c", c=PADW)[:, :, 0:HW]
                    nc.vector.tensor_scalar(inner, x[:, 0].rearrange("p (r c) -> p r c", c=HW), gn.scale[:, 0:1],
                                            gn.shift[:, 0:1], ALU.mult, ALU.add).then_inc(normalised, 1)
                    for s in range(SETS):
                        dve.wait_ge(om_t, SETS * n + s + 1)
                        src = ot[:].rearrange("p t (g m) -> p g t m", m=OM)[:, :, :, 0:3 * KK]
                        dst = om[:, s * 4 * GROUP:(s + 1) * 4 * GROUP, :].rearrange("p (g t) m -> p g t m", t=GROUP)
                        nc.vector.tensor_copy(dst, src).then_inc(om_ready, 1)
                    dve.wait_ge(om_ready, SETS * (n + 1))
                    for axis in range(2):
                        for g in range(GROUPS):
                            sl = slice(g * STEPS, (g + 1) * STEPS)
                            off = om[:, g * GROUP:(g + 1) * GROUP, axis * KK:(axis + 1) * KK].rearrange("p t k -> p k t")
                            ins = nc.vector.tensor_tensor(pos[:, axis, sl].rearrange("p (k t) -> p k t", t=GROUP),
                                                          grid[:, axis, sl].rearrange("p (k t) -> p k t", t=GROUP), off, ALU.add)
                    chain.link(ins)
                    chain.link(nc.vector.tensor_scalar(pos[:], pos[:], 0.0, HW + 1.0, ALU.max, ALU.min))
                    chain.link(nc.vector.tensor_copy(pos_i[:], pos[:]))
                    chain.link(nc.vector.tensor_copy(low[:], pos_i[:]))
                    chain.link(nc.vector.tensor_tensor(over[:], low[:], pos[:], ALU.is_gt))
                    chain.link(nc.vector.tensor_tensor(low[:], low[:], over[:], ALU.subtract))
                    chain.link(nc.vector.tensor_tensor(frac[:], pos[:], low[:], ALU.subtract))
                    chain.link(nc.vector.tensor_scalar(rest[:], frac[:], -1.0, 1.0, ALU.mult, ALU.add))
                    chain.link(nc.vector.scalar_tensor_tensor(row[:], low[:, 0], float(PADW), low[:, 1], ALU.mult, ALU.add))
                    chain.link(nc.vector.tensor_scalar(row[:], row[:], base[:, 0:1], None, ALU.add))
                    chain.link(nc.vector.tensor_scalar(all_idx[:, n, :], row[:], float(2 * C), None, ALU.mult))
                    chain.link(nc.vector.tensor_scalar(base[:], base[:], float(QROWS), None, ALU.add))
                    dve.wait_ge(mask_ready, n + 1)
                    for g in range(GROUPS):
                        sl = slice(g * STEPS, (g + 1) * STEPS)
                        m = mask[:, g * GROUP:(g + 1) * GROUP, :].rearrange("p t k -> p k t")
                        for src in (frac, rest):
                            v = src[:, 0, sl].rearrange("p (k t) -> p k t", t=GROUP)
                            ins = nc.vector.tensor_tensor(v, v, m, ALU.mult)
                    chain.link(ins)
                    for corner, (wy, wx) in enumerate(((rest, rest), (frac, rest), (rest, frac), (frac, frac))):
                        chain.link(nc.vector.tensor_tensor(all_wt[:, n, corner, :], wy[:, 0], wx[:, 1], ALU.mult))
                    assert chain.n == DVE_STEPS, chain.n

            @block.scalar
            def _(act):
                act.wait_ge(w_loaded, 32)
                with act.Fori(0, IMAGES) as n:
                    gn.act(nc, act, n)
                    act.wait_ge(gn.ready, n + 1)
                    act.wait_ge(transposed, 2 * BATCH * n)
                    act.wait_ge(conv_done, SETS * n)
                    inner = xp[:, 1, PADW + 1:PADW + 1 + HW * PADW].rearrange("p (r c) -> p r c", c=PADW)[:, :, 0:HW]
                    nc.scalar.activation(inner, x[:, 1].rearrange("p (r c) -> p r c", c=HW), ACT.Identity,
                                         bias=gn.shift[:, 1:2], scale=gn.scale[:, 1:2]).then_inc(normalised, 1)

                    def offsets(s):
                        act.wait_ge(conv_done, SETS * n + s + 1)
                        act.wait_ge(om_t, SETS * n)
                        nc.scalar.activation(om_c[:, s, :], cv[:, s, :], ACT.Identity, bias=b_off[:]).then_inc(om_c_ready, 1)

                    for b in range(BATCH):
                        even, odd = -(-BATCH // 2), BATCH // 2
                        act.wait_ge(quad_stored[b % 2], (n * (even, odd)[b % 2] + b // 2) * 32)
                        for half in range(2):
                            act.wait_ge(transposed, 2 * BATCH * n + 2 * b + half + 1)
                            nc.scalar.activation(quad[:, b % 2, 2 * half:2 * half + 2, :],
                                                 tp[:, half, :, 0:C], ACT.Copy).then_inc(tp_free, 1)
                        if b in AFTER:
                            offsets(AFTER.index(b))
                    act.wait_ge(om_ready, SETS * (n + 1))
                    nc.scalar.activation(mask[:], om[:, :, 2 * KK:3 * KK], ACT.Sigmoid).then_inc(mask_ready, 1)

            @block.tensor
            def _(pe):
                pe.wait_ge(w_loaded, 32)
                with pe.Fori(0, IMAGES) as n:
                    gn.pe(nc, pe, n, avg, gp[:, 0:2 * CH])
                    pe.wait_ge(normalised, CH * (n + 1))

                    def conv(s):
                        pe.wait_ge(om_c_ready, SETS * n)
                        for tap in range(KK):
                            ky, kx = divmod(tap, 3)
                            for h in range(CH):
                                for j in range(4):
                                    at = ((4 * s + j) * GPIX // HW + ky) * PADW + kx
                                    rows = xp[:, h, at:at + 8 * PADW].rearrange("p (r c) -> p r c", c=PADW)[:, :, 0:HW]
                                    mm = nc.tensor.matmul(cv[j * OM:(j + 1) * OM, s, :], w_off[:, h, tap, :], rows,
                                                          start=(tap == 0 and h == 0), stop=(tap == KK - 1 and h == CH - 1),
                                                          skip_group_check=True)
                        mm.then_inc(conv_done, 1)

                    def turn(s):
                        pe.wait_ge(om_c_ready, SETS * n + s + 1)
                        pe.wait_ge(om_ready, SETS * n + s)
                        pe.sem_inc(passed, 1)
                        for t in range(GROUP):
                            mm = nc.tensor.transpose(ot[:, t, :], om_c[:, s, t * P:(t + 1) * P], ident[:])
                        mm.then_inc(om_t, 1)

                    for b in range(BATCH):
                        for half in range(2):
                            pe.wait_ge(tp_free, (2 * BATCH * n + 2 * b + half - 1) if b else 2 * BATCH * n)
                            for t in range(2):
                                for h in range(CH):
                                    at = ((2 * b + half) * 2 + t) * P
                                    mm = nc.tensor.transpose(tp[:, half, t, h * P:(h + 1) * P], xp[:, h, at:at + P], ident[:])
                            mm.then_inc(transposed, 1)
                        if b in AFTER:
                            conv(AFTER.index(b))
                        if b - 2 in AFTER:
                            turn(AFTER.index(b - 2))


def stage_deform(nc, D, passed, ident, all_idx, all_wt):
    SLOTS = 9
    with ExitStack() as ctx:
        a = Alloc(nc, ctx, "d_", passed)
        w = a.sb("w", [P, CH, KK, C])
        ring = a.sb("ring", [P, SLOTS, 4 * C])
        idx = a.sb("idx", [P, 2, STEPS], U32)
        wt = a.sb("wt", [P, 2, 4, STEPS])
        val = a.sb("val", [P, 4, C])
        val_c = a.sb("val_c", [P, 2, CH, GPIX])
        xres = a.sb("xres", [P, 2, CH, GPIX])
        tp = a.ps("tp", [P, 2, CH, GPIX])
        acc = a.ps("acc", [P, 2, CH, GPIX])
        w_loaded = a.sem("w_loaded")
        x_loaded = [a.sem(f"x_loaded{b}") for b in range(2)]
        gathered = [a.sem(f"gathered{s}") for s in range(SLOTS)]
        idx_ready = a.sem("idx_ready")
        passed = a.passed
        wt_ready = a.sem("wt_ready")
        first_ready = a.sem("first_ready")
        part = a.sem("part")
        value_ready = a.sem("value_ready")
        val_free = a.sem("val_free")
        val_c_ready = a.sem("val_c_ready")
        tap_done = a.sem("tap_done")
        stored = a.sem("stored")
        added = a.sem("added")
        RUNS = IMAGES * GROUPS // 2

        table = D["table"]
        quads = bass.AP(table.tensor, table.offset, [[1, IMAGES * QROWS * 2 * C], [1, 1]])

        with nc.Block() as block:
            @block.sync
            def _(sp):
                sp.dma_start(w[:], D["w_dcn"]).then_inc(w_loaded, 16)
                with sp.Fori(0, IMAGES) as n:
                    with sp.Fori(0, GROUPS // 2) as gg:
                        for b in range(2):
                            i = (n * (GROUPS // 2) + gg) * 2 + b
                            sp.wait_ge(stored, (n * (GROUPS // 2) + gg) * 32)
                            src = D["x"][n].rearrange("(h p) q -> p h q", p=P)[:, :, bass.ds((gg * 2 + b) * GPIX, GPIX)]
                            sp.dma_start(xres[:, b], src).then_inc(x_loaded[b], 16)
                        for b in range(2):
                            i = (n * (GROUPS // 2) + gg) * 2 + b
                            sp.wait_ge(added, CH * (i + 1))
                            dst = D["x1"][n].rearrange("(h p) q -> p h q", p=P)[:, :, bass.ds((gg * 2 + b) * GPIX, GPIX)]
                            sp.dma_start(dst, xres[:, b]).then_inc(stored, 16)
                sp.wait_ge(stored, 16 * IMAGES * GROUPS)

            @block.gpsimd
            def _(pool):
                pool.sem_inc(value_ready, SLOTS)
                with pool.Fori(0, IMAGES) as n:
                    with pool.Fori(0, GROUPS // 2) as gg:
                        for b in range(2):
                            i = (n * (GROUPS // 2) + gg) * 2 + b
                            nc.gpsimd.tensor_copy(idx[:, b], all_idx[:, n, bass.ds((gg * 2 + b) * STEPS, STEPS)]).then_inc(idx_ready, 1)
                            pool.wait_ge(idx_ready, i + 1)
                            for s in range(STEPS):
                                pool.wait_ge(value_ready, i * STEPS + s + 1)
                                pool.sem_inc(passed, 1)
                                pool.indirect_dma_start(out=ring[:, s % SLOTS, :], out_offset=None, in_=quads,
                                                        in_offset=bass.IndirectOffsetOnAxis(ap=idx[:, b, s:s + 1], axis=0)
                                                        ).then_inc(gathered[s % SLOTS], 16)

            @block.scalar
            def _(act):
                with act.Fori(0, IMAGES) as n:
                    with act.Fori(0, GROUPS // 2) as gg:
                        for b in range(2):
                            i = (n * (GROUPS // 2) + gg) * 2 + b
                            act.wait_ge(wt_ready, i + 1)
                            for tap in range(KK + 1):
                                if tap < KK:
                                    for t in range(GROUP):
                                        s = tap * GROUP + t
                                        act.wait_ge(gathered[s % SLOTS], (i * (STEPS // SLOTS) + s // SLOTS + 1) * 16)
                                        act.wait_ge(val_free, (i * STEPS + s - 3) if s > 3 else i * STEPS)
                                        nc.scalar.activation(val[:, s % 4, :], ring[:, s % SLOTS, 0:C], ACT.Copy,
                                                             scale=wt[:, b, 0, s:s + 1]).then_inc(first_ready, 1)
                                if tap:
                                    k = tap - 1
                                    act.wait_ge(val_free, i * STEPS + (k + 1) * GROUP)
                                    act.wait_ge(tap_done, (i * KK + k - 1) if k > 1 else i * KK)
                                    nc.scalar.activation(val_c[:, (b * KK + k) % 2, :, :], tp[:, (b * KK + k) % 2, :, :], ACT.Copy).then_inc(val_c_ready, 1)

            @block.vector
            def _(dve):
                with dve.Fori(0, IMAGES) as n:
                    with dve.Fori(0, GROUPS // 2) as gg:
                        for b in range(2):
                            i = (n * (GROUPS // 2) + gg) * 2 + b
                            nc.vector.tensor_copy(wt[:, b], all_wt[:, n, :, bass.ds((gg * 2 + b) * STEPS, STEPS)]).then_inc(wt_ready, 1)
                            dve.wait_ge(wt_ready, i + 1)
                            for pair in range(STEPS // 2):
                                for corner in range(1, 4):
                                    for j in range(2):
                                        s = 2 * pair + j
                                        if corner == 1:
                                            dve.wait_ge(first_ready, i * STEPS + s + 1)
                                        else:
                                            dve.wait_ge(part, i * STEPS * 2 + pair * 4 + (corner - 2) * 2 + j + 1)
                                        ins = nc.vector.scalar_tensor_tensor(
                                            val[:, s % 4, :], ring[:, s % SLOTS, corner * C:(corner + 1) * C],
                                            wt[:, b, corner, s:s + 1], val[:, s % 4, :], ALU.mult, ALU.add)
                                        ins.then_inc(part if corner < 3 else value_ready, 1)
                            dve.wait_ge(tap_done, KK * (i + 1))
                            dve.wait_ge(x_loaded[b], (n * (GROUPS // 2) + gg + 1) * 16)
                            for h in range(CH):
                                nc.vector.tensor_tensor(xres[:, b, h, :], xres[:, b, h, :], acc[:, b, h, :], ALU.add).then_inc(added, 1)

            @block.tensor
            def _(pe):
                pe.wait_ge(w_loaded, 16)
                with pe.Fori(0, IMAGES) as n:
                    with pe.Fori(0, GROUPS // 2) as gg:
                        for b in range(2):
                            i = (n * (GROUPS // 2) + gg) * 2 + b
                            pe.wait_ge(added, (n * (GROUPS // 2) + gg) * 4)
                            for tap in range(KK + 1):
                                if tap < KK:
                                    pe.wait_ge(val_c_ready, (i * KK + tap - 1) if tap > 1 else i * KK)
                                    for t in range(GROUP):
                                        s = tap * GROUP + t
                                        pe.wait_ge(value_ready, i * STEPS + s + 1 + SLOTS)
                                        for h in range(CH):
                                            mm = nc.tensor.transpose(tp[:, (b * KK + tap) % 2, h, t * P:(t + 1) * P],
                                                                     val[:, s % 4, h * P:(h + 1) * P], ident[:])
                                        mm.then_inc(val_free, 1)
                                if tap:
                                    k = tap - 1
                                    pe.wait_ge(val_c_ready, i * KK + k + 1)
                                    for o in range(CH):
                                        for h in range(CH):
                                            mm = nc.tensor.matmul(acc[:, b, o, :], w[:, h, k, o * P:(o + 1) * P], val_c[:, (b * KK + k) % 2, h, :],
                                                                  start=(k == 0 and h == 0), stop=(k == KK - 1 and h == CH - 1),
                                                                  skip_group_check=True)
                                    mm.then_inc(tap_done, 1)


def stage_attention(nc, D, passed, avg, ident):
    with ExitStack() as ctx:
        a = Alloc(nc, ctx, "a_", passed)
        x = a.sb("x", [P, CH, PIX])
        xT = a.sb("xT", [P, TILES, C])
        keys = a.sb("keys", [P, TILES, HID])
        outs = keys[:].rearrange("p t d -> p (t d)")[:, 0:TILES * C].rearrange("p (t c) -> p t c", c=C)
        xo = keys[:].rearrange("p t d -> p (t d)")[:, TILES * C:].rearrange("p (h q) -> p h q", h=CH)
        w = a.sb("w", [P, CH, 3, HID])
        w_out = a.sb("w_out", [P, PAIRS, C])
        g_in = a.sb("g_in", [P, CH])
        g_out = a.sb("g_out", [P, CH])
        b_out = a.sb("b_out", [P, C])
        ones = a.sb("ones", [P, 1])
        rinv = a.sb("rinv", [P, TILES])
        kmax = a.sb("kmax", [P, HID])
        mx = a.sb("mx", [P, PAIRS])
        mxb = a.sb("mxb", [P, PAIRS, P])
        kb = a.sb("kb", [P, HID])
        e = a.sb("e", [P, 4, HID])
        esum = a.sb("esum", [P, HID])
        rs = a.sb("rs", [P, PAIRS])
        gts = a.sb("gts", [P, CH, HID])
        cT = a.sb("cT", [P, PAIRS, P])
        mix = a.sb("mix", [P, PAIRS, C])
        q = a.sb("q", [P, 4, HID])
        qm = a.sb("qm", [P, 4, HEADS])
        qs = a.sb("qs", [P, 4, HEADS])
        qT = a.sb("qT", [P, 2, HID])
        sq = a.sb("sq", [P, C])
        osum = a.sb("osum", [P, TILES])
        oinv = a.sb("oinv", [P, TILES])
        y = a.sb("y", [P, 4, C])
        gn = GroupNorm(a)
        proj = a.ps("proj", [P, 2, HID])
        tp = a.ps("tp", [P, 2, HID])
        gt = a.ps("gt", [P, CH, HID])
        op = a.ps("op", [P, 2, 512])
        averages = op[:, 0, C:C + 2 * CH]
        sums = op[:, 1, C:C + PAIRS]
        sems = {}
        for s in ("w_loaded x_loaded const chain w_ready x_ready x_turned x_squared x_root x_clamped rinv_ready xT_ready "
                  "proj_done k_read kmax_done kmax_turned mx_ready mx_spread kb_ready diff_ready "
                  "e_ready esum_done ctx_used ctx_sum gt_read ctx_done rs_ready cT_ready mix_done mix_ready "
                  "qmax q_read q_exp q_sum q_norm q_turned qT_ready out_done out_ready out_sq oroot oinv_ready y_ready "
                  "y_turned added").split():
            sems[s] = a.sem(s)
        sems["passed"] = a.passed
        S = type("Sems", (), sems)
        stored = a.sem("stored")
        res_loaded = a.sem("res_loaded")
        U = 2 * GROUP
        RUNS = GROUPS // 2
        CHAIN = CH * GROUPS + CH + 6 + 4

        def laps(eng, lag, steps):
            for c in range(U):
                steps(0, c, lambda k: c >= k)
            with eng.Fori(0, RUNS - 1) as r:
                for c in range(U):
                    steps(r + 1, c, lambda k: True)
            for c in range(lag):
                steps(RUNS, c, lambda k: c < k)

        def written_out(lag, steps):
            for t in range(TILES + lag):
                steps(t // U, t % U, lambda k: k <= t < TILES + k)

        def before(n, lap, c, k):
            at = c + 1 - k
            if isinstance(lap, int):
                return n * TILES + max(lap * U + at, 0)
            return n * TILES + lap * U + at

        with nc.Block() as block:
            @block.sync
            def _(sp):
                for dst, src in ((w, "w_qkv"), (w_out, "w_out"), (g_in, "g_in"), (g_out, "g_out"), (b_out, "b_out")):
                    sp.dma_start(dst[:], D[src]).then_inc(S.w_loaded, 16)
                with sp.Fori(0, IMAGES) as n:
                    sp.wait_ge(S.diff_ready, (n + 1) * TILES)
                    sp.dma_start(xo, D["x1"][n].rearrange("(h p) q -> p h q", p=P)).then_inc(res_loaded, 16)
                    with sp.Fori(0, RUNS) as r:
                        for b in range(2):
                            at = bass.ds((2 * r + b) * GPIX, GPIX)
                            sp.wait_ge(S.added, CH * (GROUPS * n + 2 * r + b + 1))
                            sp.dma_start(D["x2"][n].rearrange("(h p) q -> p h q", p=P)[:, :, at], xo[:, :, at]).then_inc(stored, 16)
                sp.wait_ge(stored, 16 * IMAGES * GROUPS)

            @block.gpsimd
            def _(pool):
                chain = Chain(pool, S.const)
                chain.link(nc.gpsimd.memset(ones[:], 1.0))
                chain.link(nc.gpsimd.memset(cT[:], 0.0))
                with pool.Fori(0, IMAGES) as n:
                    pool.wait_ge(S.proj_done, n * 2 * TILES)
                    pool.sem_inc(S.passed, 1)
                    pool.dma_start(x[:], D["x1"][n].rearrange("(h p) q -> p h q", p=P)).then_inc(S.x_loaded, 16)

                    def esums(lap, c, live):
                        pool.wait_ge(S.e_ready, before(n, lap, c, 0))
                        pool.wait_ge(S.esum_done, before(n, lap, c, 1))
                        pool.sem_inc(S.passed, 1)
                        if isinstance(lap, int) and lap == 0 and c == 0:
                            pool.wait_ge(S.ctx_sum, n)
                            pool.sem_inc(S.passed, 1)
                            nc.gpsimd.tensor_copy(esum[:], e[:, 0, :]).then_inc(S.esum_done, 1)
                        else:
                            nc.gpsimd.tensor_tensor(esum[:], esum[:], e[:, c % 4, :], ALU.add).then_inc(S.esum_done, 1)

                    laps(pool, 0, esums)

            @block.scalar
            def _(act):
                with act.Fori(0, IMAGES) as n:
                    gn.act(nc, act, n)
                    act.wait_ge(gn.ready, n + 1)
                    act.sem_inc(S.passed, 1)

                    def normalise(g):
                        for h in range(CH):
                            xg = x[:, h, g * GPIX:(g + 1) * GPIX]
                            nc.scalar.activation(xg, xg, ACT.Identity,
                                                 bias=gn.shift[:, h:h + 1], scale=gn.scale[:, h:h + 1]).then_inc(S.x_ready, 1)

                    normalise(0)

                    def pass_a(lap, c, live):
                        if live(0):
                            t = bass.ds(lap * U + c, 1)
                            act.wait_ge(S.x_turned, before(n, lap, c, 0))
                            act.wait_ge(S.x_squared, before(n, lap, c, 1))
                            act.sem_inc(S.passed, 1)
                            nc.scalar.activation(sq[:], tp[:, c % 2, 0:C], ACT.Square, accum_out=rinv[:, t]).then_inc(S.x_squared, 1)
                            act.wait_ge(S.x_squared, before(n, lap, c, 0))
                            act.sem_inc(S.passed, 1)
                            nc.scalar.activation(rinv[:, t], rinv[:, t], ACT.Sqrt).then_inc(S.x_root, 1)
                            if isinstance(lap, int) and lap == 0 and c + 1 < GROUPS:
                                normalise(c + 1)
                        if live(1):
                            t = bass.ds(lap * U + c - 1, 1)
                            act.wait_ge(S.proj_done, n * TILES + before(n, lap, c, 1))
                            act.wait_ge(S.rinv_ready, before(n, lap, c, 1))
                            if isinstance(lap, int) and lap == 0 and c == 1:
                                act.wait_ge(stored, 16 * GROUPS * n)
                            act.sem_inc(S.passed, 1)
                            nc.scalar.activation(keys[:, t, :].rearrange("p t d -> p (t d)"), proj[:, (c - 1) % 2, :], ACT.Copy,
                                                 scale=rinv[:, t]).then_inc(S.k_read, 1)

                    def pass_b(lap, c, live):
                        act.wait_ge(S.diff_ready, before(n, lap, c, 0))
                        nc.scalar.activation(e[:, c % 4, :], e[:, c % 4, :], ACT.Exp).then_inc(S.e_ready, 1)

                    def pass_c(lap, c, live):
                        if live(2):
                            act.wait_ge(S.q_turned, before(n, lap, c, 2))
                            act.wait_ge(S.out_done, before(n, lap, c, 4))
                            nc.scalar.activation(qT[:, c % 2, :], tp[:, c % 2, :], ACT.Copy).then_inc(S.qT_ready, 1)
                        if live(0):
                            act.wait_ge(S.q_read, before(n, lap, c, 0))
                            act.sem_inc(S.passed, 1)
                            nc.scalar.activation(q[:, c % 4, :], q[:, c % 4, :], ACT.Exp,
                                                 scale=rinv[:, bass.ds(lap * U + c, 1)]).then_inc(S.q_exp, 1)
                        if live(4):
                            t = bass.ds(lap * U + c - 4, 1)
                            act.wait_ge(S.out_ready, before(n, lap, c, 4))
                            act.wait_ge(S.out_sq, before(n, lap, c, 5))
                            act.sem_inc(S.passed, 1)
                            nc.scalar.activation(sq[:], outs[:, t, :].rearrange("p t c -> p (t c)"), ACT.Square,
                                                 accum_out=osum[:, t]).then_inc(S.out_sq, 1)

                    laps(act, 1, pass_a)
                    laps(act, 0, pass_b)
                    act.wait_ge(S.ctx_used, (n + 1) * TILES)
                    act.sem_inc(S.passed, 1)
                    nc.scalar.activation(gts[:, 0, :], gt[:, 0, :], ACT.Copy).then_inc(S.gt_read, 1)
                    laps(act, 4, pass_c)
                    act.wait_ge(S.out_sq, (n + 1) * TILES)
                    nc.scalar.activation(oinv[:], osum[:], ACT.Sqrt).then_inc(S.oroot, 1)
                    act.wait_ge(S.oinv_ready, n + 1)
                    act.sem_inc(S.passed, 1)
                    with act.Fori(0, RUNS) as r:
                        for c in range(U):
                            act.wait_ge(S.y_turned, n * TILES + r * U + max(c - 3, 0))
                            act.sem_inc(S.passed, 1)
                            t = bass.ds(r * U + c, 1)
                            nc.scalar.activation(y[:, c % 4, :], outs[:, t, :].rearrange("p t c -> p (t c)"), ACT.Copy,
                                                 scale=oinv[:, t]).then_inc(S.y_ready, 1)

            @block.vector
            def _(dve):
                dve.wait_ge(S.w_loaded, 16 * 5)
                dve.wait_ge(S.const, 2)
                for h in range(CH):
                    nc.vector.tensor_scalar(w[:, h].rearrange("p a b -> p (a b)"), w[:, h].rearrange("p a b -> p (a b)"),
                                            g_in[:, h:h + 1], float(C) ** 0.5, ALU.mult, ALU.mult).then_inc(S.w_ready, 1)
                with dve.Fori(0, IMAGES) as n:
                    chain = Chain(dve, S.chain, n * CHAIN)
                    dve.wait_ge(S.x_loaded, 16 * (n + 1))
                    gn.dve(nc, dve, chain, n, x, averages)

                    def pass_a(lap, c, live):
                        if live(0):
                            t = bass.ds(lap * U + c, 1)
                            dve.wait_ge(S.x_root, before(n, lap, c, 0))
                            dve.sem_inc(S.passed, 1)
                            nc.vector.tensor_scalar(rinv[:, t], rinv[:, t], RMS_EPS, None, ALU.max).then_inc(S.x_clamped, 1)
                            dve.wait_ge(S.x_clamped, before(n, lap, c, 0))
                            dve.sem_inc(S.passed, 1)
                            nc.vector.reciprocal(rinv[:, t], rinv[:, t]).then_inc(S.rinv_ready, 1)
                            dve.wait_ge(S.rinv_ready, before(n, lap, c, 0))
                            dve.sem_inc(S.passed, 1)
                            nc.vector.tensor_scalar(xT[:, t, :].rearrange("p t c -> p (t c)"), tp[:, c % 2, 0:C], rinv[:, t], None,
                                                    ALU.mult).then_inc(S.xT_ready, 1)
                        if live(2):
                            kt = keys[:, bass.ds(lap * U + c - 2, 1), :].rearrange("p t d -> p (t d)")
                            dve.wait_ge(S.k_read, before(n, lap, c, 2))
                            dve.wait_ge(S.kmax_done, before(n, lap, c, 3))
                            dve.sem_inc(S.passed, 1)
                            if isinstance(lap, int) and lap == 0 and c == 2:
                                nc.vector.tensor_copy(kmax[:], kt).then_inc(S.kmax_done, 1)
                            else:
                                nc.vector.tensor_tensor(kmax[:], kmax[:], kt, ALU.max).then_inc(S.kmax_done, 1)

                    def pass_b(lap, c, live):
                        dve.wait_ge(S.ctx_used, before(n, lap, c, 4))
                        dve.wait_ge(S.esum_done, before(n, lap, c, 4))
                        dve.sem_inc(S.passed, 1)
                        nc.vector.tensor_tensor(e[:, c % 4, :], keys[:, bass.ds(lap * U + c, 1), :].rearrange("p t d -> p (t d)"),
                                                kb[:], ALU.subtract).then_inc(S.diff_ready, 1)

                    def pass_c(lap, c, live):
                        if live(4):
                            dve.wait_ge(S.out_done, before(n, lap, c, 4))
                            dve.sem_inc(S.passed, 1)
                            nc.vector.tensor_tensor(outs[:, bass.ds(lap * U + c - 4, 1), :].rearrange("p t c -> p (t c)"), op[:, c % 2, 0:C],
                                                    b_out[:], ALU.add).then_inc(S.out_ready, 1)
                        if live(0):
                            dve.wait_ge(S.proj_done, (n + 1) * TILES + before(n, lap, c, 0))
                            heads = proj[:, c % 2, :].rearrange("p (h d) -> p h d", d=DH)
                            nc.vector.tensor_reduce(qm[:, c % 4, :], heads, AX_X, ALU.max).then_inc(S.qmax, 1)
                            dve.wait_ge(S.qmax, before(n, lap, c, 0))
                            dve.wait_ge(S.q_turned, before(n, lap, c, 4))
                            nc.vector.tensor_tensor(q[:, c % 4, :].rearrange("p (h d) -> p h d", d=DH), heads,
                                                    qm[:, c % 4, :].unsqueeze(2).to_broadcast([P, HEADS, DH]),
                                                    ALU.subtract).then_inc(S.q_read, 1)
                        if live(1):
                            b = (c - 1) % 4
                            qj = q[:, b, :].rearrange("p (h d) -> p h d", d=DH)
                            done = before(n, lap, c, 1)
                            dve.wait_ge(S.q_exp, done)
                            nc.vector.tensor_reduce(qs[:, b, :], qj, AX_X, ALU.add).then_inc(S.q_sum, 1)
                            dve.wait_ge(S.q_sum, 2 * done - 1)
                            nc.vector.reciprocal(qs[:, b, :], qs[:, b, :]).then_inc(S.q_sum, 1)
                            dve.wait_ge(S.q_sum, 2 * done)
                            nc.vector.tensor_tensor(qj, qj, qs[:, b, :].unsqueeze(2).to_broadcast([P, HEADS, DH]),
                                                    ALU.mult).then_inc(S.q_norm, 1)

                    laps(dve, 2, pass_a)
                    dve.wait_ge(S.kmax_turned, n + 1)
                    chain.link(nc.vector.tensor_reduce(mx[:], op[:, 0, :].rearrange("p (j q) -> p j q", q=P), AX_X, ALU.max))
                    nc.vector.tensor_copy(mxb[:], mx[:].unsqueeze(2).to_broadcast([P, PAIRS, P])).then_inc(S.mx_ready, 1)
                    dve.wait_ge(S.mx_spread, n + 1)
                    nc.vector.tensor_copy(kb[:], op[:, 1, :]).then_inc(S.kb_ready, 1)
                    dve.wait_ge(S.kb_ready, n + 1)
                    dve.sem_inc(S.passed, 1)
                    laps(dve, 0, pass_b)
                    dve.wait_ge(S.ctx_used, (n + 1) * TILES)
                    dve.sem_inc(S.passed, 1)
                    nc.vector.tensor_copy(gts[:, 1, :], gt[:, 1, :]).then_inc(S.gt_read, 1)
                    dve.wait_ge(S.ctx_sum, n + 1)
                    chain.link(nc.vector.reciprocal(rs[:], sums))
                    nc.vector.tensor_scalar(rs[:], rs[:], float(DH) ** -0.5, None, ALU.mult).then_inc(S.rs_ready, 1)
                    dve.wait_ge(S.ctx_done, n + 1)
                    for lo in (0, DH):
                        s = slice(lo, lo + DH)
                        nc.vector.tensor_copy(cT[s, :, s], op[s, 0, :].rearrange("p (j d) -> p j d", d=P)[:, :, s]).then_inc(S.cT_ready, 1)
                    dve.wait_ge(S.rs_ready, n + 1)
                    dve.wait_ge(S.mix_done, n + 1)
                    for j in range(PAIRS):
                        nc.vector.tensor_scalar(mix[:, j, :], tp[:, j // 2, (j % 2) * C:(j % 2 + 1) * C], rs[:, j:j + 1], None,
                                                ALU.mult).then_inc(S.mix_ready, 1)
                    laps(dve, 4, pass_c)
                    dve.wait_ge(S.oroot, n + 1)
                    chain.link(nc.vector.tensor_scalar(oinv[:], oinv[:], RMS_EPS, None, ALU.max))
                    chain.link(nc.vector.reciprocal(oinv[:], oinv[:]))
                    nc.vector.tensor_scalar(oinv[:], oinv[:], float(C) ** 0.5, None, ALU.mult).then_inc(S.oinv_ready, 1)
                    with dve.Fori(0, RUNS) as r:
                        for b in range(2):
                            dve.wait_ge(S.y_turned, n * TILES + r * U + (b + 1) * GROUP)
                            dve.wait_ge(res_loaded, 16 * (n + 1))
                            dve.sem_inc(S.passed, 1)
                            at = bass.ds((2 * r + b) * GPIX, GPIX)
                            for h in range(CH):
                                nc.vector.scalar_tensor_tensor(xo[:, h, at], (proj, tp)[b][:, h, :], g_out[:, h:h + 1], xo[:, h, at],
                                                               ALU.mult, ALU.add).then_inc(S.added, 1)
                    assert chain.n == CHAIN, chain.n

            @block.tensor
            def _(pe):
                pe.wait_ge(S.w_ready, CH)
                pe.wait_ge(S.const, 2)

                with pe.Fori(0, IMAGES) as n:
                    gn.pe(nc, pe, n, avg, averages)
                    pe.wait_ge(S.added, CH * GROUPS * n)
                    pe.sem_inc(S.passed, 1)

                    def project(lap, c, which):
                        for h in range(CH):
                            mm = nc.tensor.matmul(proj[:, c % 2, :], x[:, h, (lap * U + c) * P:(lap * U + c + 1) * P], w[:, h, which, :],
                                                  start=(h == 0), stop=(h == CH - 1))
                        mm.then_inc(S.proj_done, 1)

                    def pass_a(lap, c, live):
                        if c % GROUP == 0:
                            pe.wait_ge(S.x_ready, CH * (n * GROUPS + lap * 2 + c // GROUP + 1))
                        pe.wait_ge(S.x_squared, before(n, lap, c, 2))
                        pe.wait_ge(S.xT_ready, before(n, lap, c, 2))
                        pe.sem_inc(S.passed, 1)
                        for h in range(CH):
                            mm = nc.tensor.transpose(tp[:, c % 2, h * P:(h + 1) * P], x[:, h, (lap * U + c) * P:(lap * U + c + 1) * P], ident[:])
                        mm.then_inc(S.x_turned, 1)
                        pe.wait_ge(S.k_read, before(n, lap, c, 2))
                        project(lap, c, 1)

                    def pass_b(lap, c, live):
                        pe.wait_ge(S.e_ready, before(n, lap, c, 0))
                        first = isinstance(lap, int) and lap == 0 and c == 0
                        for h in range(CH):
                            mm = nc.tensor.matmul(gt[:, h, :], xT[:, lap * U + c, h * P:(h + 1) * P],
                                                  e[:, c % 4, :], start=first, stop=False, skip_group_check=True)
                        mm.then_inc(S.ctx_used, 1)

                    def pass_c(lap, c, live):
                        if live(0):
                            pe.wait_ge(S.q_read, before(n, lap, c, 2))
                            project(lap, c, 0)
                        if live(2):
                            pe.wait_ge(S.q_norm, before(n, lap, c, 2))
                            pe.wait_ge(S.qT_ready, before(n, lap, c, 4))
                            for p in range(PAIRS):
                                mm = nc.tensor.transpose(tp[:, c % 2, p * P:(p + 1) * P], q[:, (c - 2) % 4, p * P:(p + 1) * P], ident[:])
                            mm.then_inc(S.q_turned, 1)
                        if live(3):
                            pe.wait_ge(S.qT_ready, before(n, lap, c, 3))
                            pe.wait_ge(S.out_ready, before(n, lap, c, 5))
                            b = (c - 3) % 2
                            for p in range(PAIRS):
                                mm = nc.tensor.matmul(op[:, b, 0:C], qT[:, b, p * P:(p + 1) * P], mix[:, p, :],
                                                      start=(p == 0), stop=(p == PAIRS - 1))
                            mm.then_inc(S.out_done, 1)

                    written_out(0, pass_a)
                    pe.wait_ge(S.kmax_done, TILES * (n + 1))
                    for j in range(PAIRS):
                        mm = nc.tensor.transpose(op[:, 0, j * P:(j + 1) * P], kmax[:, j * P:(j + 1) * P], ident[:])
                    mm.then_inc(S.kmax_turned, 1)
                    pe.wait_ge(S.mx_ready, n + 1)
                    for j in range(PAIRS):
                        mm = nc.tensor.matmul(op[:, 1, j * P:(j + 1) * P], mxb[:, j, :], ident[:], start=True, stop=True)
                    mm.then_inc(S.mx_spread, 1)
                    pe.wait_ge(S.xT_ready, TILES * (n + 1))
                    pe.sem_inc(S.passed, 1)
                    written_out(0, pass_b)
                    pe.wait_ge(S.esum_done, TILES * (n + 1))
                    pe.sem_inc(S.passed, 1)
                    for j in range(PAIRS):
                        mm = nc.tensor.matmul(sums[:, j:j + 1], esum[:, j * P:(j + 1) * P], ones[:], start=True, stop=True)
                    mm.then_inc(S.ctx_sum, 1)
                    pe.wait_ge(S.gt_read, 2 * (n + 1))
                    for j in range(PAIRS):
                        s = slice(j * P, (j + 1) * P)
                        for h in range(CH):
                            mm = nc.tensor.matmul(op[:, 0, s], w[:, h, 2, s], gts[:, h, s], start=(h == 0), stop=(h == CH - 1))
                    mm.then_inc(S.ctx_done, 1)
                    pe.wait_ge(S.cT_ready, 2 * (n + 1))
                    for j in range(PAIRS):
                        mm = nc.tensor.matmul(tp[:, j // 2, (j % 2) * C:(j % 2 + 1) * C], cT[:, j, :], w_out[:, j, :], start=True, stop=True)
                    mm.then_inc(S.mix_done, 1)
                    pe.wait_ge(S.k_read, TILES * (n + 1))
                    pe.wait_ge(S.mix_ready, PAIRS * (n + 1))
                    pe.sem_inc(S.passed, 1)
                    written_out(3, pass_c)
                    with pe.Fori(0, RUNS) as r:
                        for b in range(2):
                            pe.wait_ge(S.added, CH * (GROUPS * n + 2 * r + max(b - 1, 0)))
                            for t in range(GROUP):
                                c = b * GROUP + t
                                pe.wait_ge(S.y_ready, n * TILES + r * U + c + 1)
                                for h in range(CH):
                                    mm = nc.tensor.transpose((proj, tp)[b][:, h, t * P:(t + 1) * P], y[:, c % 4, h * P:(h + 1) * P], ident[:])
                                mm.then_inc(S.y_turned, 1)


def stage_involution_filters(nc, D, passed, ident, filts, shift):
    hi, mid, lo_hi = filts
    SIZE = G2 * FLAT
    with ExitStack() as ctx:
        a = Alloc(nc, ctx, "f_", passed)
        w2 = a.sb("w2", [P, G2 * TAPS])
        bn = a.sb("bn", [P, 4, G2 * TAPS])
        flat = a.sb("flat", [P, G2, FLAT])
        rest = a.sb("rest", [P, SIZE])
        flat_shift = a.sb("flat_shift", [G2, G2, FLAT])
        shift_row = a.sb("shift_row", [G2, FLAT])
        spread = a.ps("spread", [P, 512])
        loaded = a.sem("loaded")
        chain_sem = a.sem("chain")
        root = a.sem("root")
        shifts_ready = a.sem("shifts_ready")
        spread_done = a.sem("spread_done")

        def taps(v, g, part):
            return v[part, g, LEAD:LEAD + K7 * WX].rearrange("p (a b) -> p a b", b=WX)[:, :, 0:K7]

        def dense(v, g, part):
            return v[part, g * TAPS:(g + 1) * TAPS].rearrange("p (a b) -> p a b", b=K7)

        with nc.Block() as block:
            @block.sync
            def _(sp):
                for half in range(2):
                    sp.dma_start(w2[half * MID:(half + 1) * MID], D["w2"]).then_inc(loaded, 16)
                sp.dma_start(bn[:], D["bn2"]).then_inc(loaded, 16)

            @block.scalar
            def _(act):
                act.wait_ge(chain_sem, 4)
                nc.scalar.activation(bn[:, 3], bn[:, 3], ACT.Sqrt).then_inc(root, 1)

            @block.vector
            def _(dve):
                chain = Chain(dve, chain_sem)
                dve.wait_ge(loaded, 48)
                chain.add(nc.vector.memset(flat[:], 0.0))
                chain.add(nc.vector.memset(flat_shift[:], 0.0))
                chain.add(nc.vector.memset(shift_row[:], 0.0))
                chain.add(nc.vector.tensor_scalar(bn[:, 3], bn[:, 3], BN_EPS, None, ALU.add))
                dve.wait_ge(root, 1)
                chain.link(nc.vector.reciprocal(bn[:, 3], bn[:, 3]))
                chain.link(nc.vector.tensor_tensor(bn[:, 0], bn[:, 0], bn[:, 3], ALU.mult))
                chain.link(nc.vector.tensor_tensor(w2[:], w2[:], bn[:, 0], ALU.mult))
                chain.link(nc.vector.tensor_tensor(bn[:, 2], bn[:, 2], bn[:, 0], ALU.mult))
                chain.link(nc.vector.tensor_tensor(bn[:, 1], bn[:, 1], bn[:, 2], ALU.subtract))
                for g in range(G2):
                    chain.add(nc.vector.tensor_copy(taps(flat, g, slice(0, P)), dense(w2, g, slice(0, P))))
                    chain.add(nc.vector.tensor_copy(taps(flat_shift, g, slice(0, G2)), dense(bn[:, 1], g, slice(0, G2))))
                dve.wait_ge(chain_sem, chain.value())
                for g in range(G2):
                    ins = nc.vector.scalar_tensor_tensor(shift_row[:], flat_shift[:, g, :], ident[0:G2, g:g + 1], shift_row[:], ALU.mult, ALU.add)
                    ins.then_inc(shifts_ready, 1)
                    dve.wait_ge(shifts_ready, g + 1)
                v = flat[:].rearrange("p g f -> p (g f)")
                chain.link(nc.vector.tensor_copy(hi[:], v))
                chain.link(nc.vector.tensor_tensor(rest[:], v, hi[:], ALU.subtract))
                chain.link(nc.vector.tensor_copy(mid[:], rest[:]))
                nc.vector.tensor_tensor(lo_hi[0:MID], rest[0:MID], mid[0:MID], ALU.subtract)
                nc.vector.tensor_copy(lo_hi[MID:P], hi[MID:P])
                dve.wait_ge(spread_done, 1)
                nc.vector.tensor_copy(shift[:], spread[0:WIN, 0:G2 * BPIX])

            @block.tensor
            def _(pe):
                pe.wait_ge(shifts_ready, G2)
                for at in range(BPIX):
                    ry, rx = divmod(at, BX)
                    off = ry * WX + rx
                    mm = nc.tensor.matmul(spread[0:WIN, at:at + (G2 - 1) * BPIX + 1:BPIX], shift_row[:, LEAD - off:FLAT - off],
                                          ident[0:G2, 0:G2], start=True, stop=True)
                mm.then_inc(spread_done, 1)


def stage_involution(nc, D, passed, avg, ident, filts, shift):
    GH = G2 // CH
    CHUNKS = 4
    CB = BLOCKS // CHUNKS
    CL = CB // BCOLS * BLINE
    with ExitStack() as ctx:
        a = Alloc(nc, ctx, "i_", passed)
        x = a.sb("x", [P, CH, PIX])
        ym = a.sb("ym", [P, BPIX, 2 * BLOCKS], BF16)
        yl = a.sb("yl", [P, BPIX, 2 * BLOCKS], BF16)
        ym_half = a.sb("ym_half", [P, BPIX, BLOCKS], BF16)
        yl_half = a.sb("yl_half", [P, BPIX, BLOCKS], BF16)
        hi = a.sb("hi", [P, 2, GPIX], BF16)
        mid = a.sb("mid", [P, 2, GPIX], BF16)
        kern = a.sb("kern", [WIN, GH, BPIX, BLOCKS])
        win = a.sb("win", [WIN, 2, CL, P])
        xs = a.sb("xs", [P, 2, CH, GPIX])
        turned = a.sb("turned", [P, 2, GROUP, C])
        w1 = a.sb("w1", [P, CH, P])
        bn1 = a.sb("bn1", [P, 7])
        co = a.sb("co", [P, 8])
        sg = a.sb("sg", [P, 2, GPIX])
        quads = a.sb("quads", [P, P // 32])
        own = a.sb("own", [P, 2])
        masked = a.sb("masked", [P, 2, 256])
        inv = a.sb("inv", [P, BLOCKS, BPIX])
        d, u = (inv[:].rearrange("p b q -> p (b q)")[:, k * 2 * GPIX:(k + 1) * 2 * GPIX].rearrange("p (b q) -> p b q", b=2)
                for k in range(2))
        zero = kern[:].rearrange("p g q b -> p (g q b)")[:, 0:BX * C]
        gn = GroupNorm(a)
        tp = a.ps("tp", [P, 2, 2, C])
        kp = a.ps("kp", [P, 4, 4 * BLOCKS])
        sp_ = a.ps("sum", [P, 2, 512])
        small = kp[:, 0, :]
        yp = kp[:, 1:3, :]

        def turn_bank(b, half):
            return tp[:, half] if b == 0 else sp_[:, half, :].rearrange("p (t c) -> p t c", c=C)

        sems = {}
        for s in ("root1 split kern_read_act half_ready w_loaded x_loaded const chain xs_ready yp_done d_ready sg_ready u_ready m_ready turn_done turn_read "
                  "placed_pool placed_act placed_dve filled kern_done kern_read sum_done first_read reduced added").split():
            sems[s] = a.sem(s)
        sems["passed"] = a.passed
        S = type("Sems", (), sems)
        patched = [a.sem(f"patched{b}") for b in range(2)]
        stored = [a.sem(f"stored{h}") for h in range(CH)]
        win_loaded = [a.sem(f"win_loaded{b}") for b in range(2)]
        RUNS = GROUPS // 2
        SPLITS = 5
        COEF = 12
        CHAIN = CH * GROUPS + CH + 6
        BANKS = GH * BPIX // 4
        QUAD_CH = 32
        TWO = QUAD_CH // GC
        SB = 16
        SUMS = BLOCKS // SB
        patch = D["patch"]

        def place(copy, dst, src, part, r, b, done):
            per = GPIX // BPIX
            for ry in range(BY):
                to = dst[part, ry * BX:(ry + 1) * BX, bass.ds((2 * r + b) * per, per)].rearrange("p rx (by bx) -> p by bx rx", bx=BCOLS)
                of = src[part, b].rearrange("p (by ry bx rx) -> p by ry bx rx", ry=BY, bx=BCOLS, rx=BX)[:, :, ry]
                copy(to, of).then_inc(done, 1)

        def copy_act(to, of):
            return nc.scalar.activation(to, of, ACT.Copy)

        lower, upper = slice(0, MID), slice(MID, P)

        def on_act(k):
            return k % 4 == 3

        ACT_BANKS = sum(on_act(k) for k in range(BANKS))
        DVE_BANKS = BANKS - ACT_BANKS

        def copied(pe, unit, k):
            if k < 4:
                return
            if on_act(k - 4):
                pe.wait_ge(S.kern_read_act, unit * 4 * ACT_BANKS + 4 * sum(on_act(j) for j in range(k - 3)))
            else:
                pe.wait_ge(S.kern_read, unit * DVE_BANKS + sum(not on_act(j) for j in range(k - 3)))

        def load_windows(eng, n, hf, h, q):
            for wy in range(WY):
                row = (wy % 2) * (PAD2 // 2) + (wy // 2) + hf * (HALF_ROWS // 2) + q * (CB // BCOLS)
                at = patch[n, bass.ds(row * PITCH, 1), h * P:(h + 1) * P]
                src = bass.AP(at.tensor, at.offset, [[C, WX], [BX * C, CL - 1], [1, P]])
                eng.dma_start(win[wy * WX:(wy + 1) * WX, q % 2, 0:CL - 1, :], src).then_inc(win_loaded[q % 2], 16)

        with nc.Block() as block:
            @block.sync
            def _(sp):
                sp.dma_start(w1[:], D["w1"]).then_inc(S.w_loaded, 16)
                sp.dma_start(bn1[:], D["bn1"]).then_inc(S.w_loaded, 16)
                sp.wait_ge(S.const, 1)
                with sp.Fori(0, IMAGES) as n:
                    for plane in range(2):
                        edge = (K7 // 2 + 1 - plane) // 2 * PITCH + K7 // 2
                        gap = edge + HW
                        tail = gap + (HALF_ROWS - 1) * PITCH
                        odd = (PLANE - tail) % 3

                        def fill(first, count, rows):
                            dst = patch[n, bass.ds(plane * PLANE + first, count), :].rearrange("(p q) c -> p (q c)", p=rows)
                            sp.dma_start(dst, zero[0:rows, 0:count // rows * C]).then_inc(S.filled, 16)

                        fill(0, edge, edge // 3)
                        fill(tail, PLANE - tail - odd, (PLANE - tail) // 3)
                        fill(PLANE - odd, odd, odd)
                        dst = patch[n, bass.ds(plane * PLANE + gap, (HALF_ROWS - 1) * PITCH), :].rearrange("(r q) c -> r (q c)", q=PITCH)
                        sp.dma_start(dst[:, 0:(PITCH - HW) * C], zero[0:HALF_ROWS - 1]).then_inc(S.filled, 16)
                sp.wait_ge(S.filled, 16 * 8 * IMAGES)
                with sp.Fori(0, IMAGES) as n:
                    with sp.Fori(0, RUNS) as r:
                        for b in range(2):
                            sp.wait_ge(S.turn_read, 2 * (GROUPS * n + 2 * r + b + 1))
                            for half in range(2):
                                first = ((K7 // 2 + half) % 2) * PLANE + (K7 // 2 + half) // 2 * PITCH
                                rows = patch[n, bass.ds(first + (2 * r + b) * GROUP * PITCH, GROUP * PITCH), :]
                                dst = rows.rearrange("(t q) c -> q t c", q=PITCH)[3:3 + HW]
                                sp.dma_start(dst, turned[half * HW:(half + 1) * HW, b]).then_inc(patched[b], 16)
                    for b in range(2):
                        sp.wait_ge(patched[b], 32 * RUNS * (n + 1))
                    sp.sem_inc(S.passed, 1)
                    with sp.Fori(0, 2) as hf:
                        for h in range(CH):
                            unit = (n * 2 + hf) * CH + h
                            for q in range(CHUNKS):
                                sp.wait_ge(S.sum_done, unit * SUMS + max(q - 1, 0) * SUMS // CHUNKS)
                                load_windows(sp, n, hf, h, q)
                            sp.wait_ge(S.added, SUMS * (unit + 1))
                            dst = D["x3"][n].rearrange("(h p) q -> p h q", p=P)[:, h, bass.ds(hf * (PIX // 2), PIX // 2)]
                            sp.dma_start(dst, x[:, h, bass.ds(hf * (PIX // 2), PIX // 2)]).then_inc(stored[h], 16)
                for h in range(CH):
                    sp.wait_ge(stored[h], 16 * 2 * IMAGES)

            @block.gpsimd
            def _(pool):
                chain = Chain(pool, S.const)
                chain.link(nc.gpsimd.memset(zero, 0.0))
                chain.link(nc.gpsimd.memset(quads[:], 1.0))
                chain.link(nc.gpsimd.affine_select(out=quads[:], in_=quads[:], compare_op=ALU.is_ge, fill=0.0, base=0,
                                                   pattern=[[-QUAD_CH, P // QUAD_CH]], channel_multiplier=1))
                chain.link(nc.gpsimd.affine_select(out=quads[:], in_=quads[:], compare_op=ALU.is_ge, fill=0.0, base=GC - 1,
                                                   pattern=[[QUAD_CH, P // QUAD_CH]], channel_multiplier=-1))
                with pool.Fori(0, IMAGES) as n:
                    for h in range(CH):
                        pool.wait_ge(stored[h], 16 * 2 * n)
                        pool.sem_inc(S.passed, 1)
                        pool.dma_start(x[:, h], D["x2"][n].rearrange("(h p) q -> p h q", p=P)[:, h]).then_inc(S.x_loaded, 16)
                    pool.wait_ge(S.half_ready, 4 * n)
                    pool.sem_inc(S.passed, 1)
                    with pool.Fori(0, RUNS) as r:
                        for src, part, step in ((hi, lower, 2), (u, upper, 5)):
                            for b in range(2):
                                pool.wait_ge(S.split, SPLITS * (GROUPS * n + 2 * r) + 2 * (step - 1) + b + 1)
                                pool.sem_inc(S.passed, 1)
                                place(nc.gpsimd.tensor_copy, yl, src, part, r, b, S.placed_pool)

            @block.scalar
            def _(act):
                act.wait_ge(S.chain, 3)
                nc.scalar.activation(co[:, 4:5], co[:, 5:6], ACT.Sqrt).then_inc(S.root1, 1)
                act.wait_ge(S.chain, COEF)
                with act.Fori(0, IMAGES) as n:
                    gn.act(nc, act, n)
                    act.wait_ge(gn.ready, n + 1)
                    act.sem_inc(S.passed, 1)

                    def normalise(r):
                        act.wait_ge(S.turn_done, 2 * (GROUPS * n + 2 * r))
                        act.wait_ge(S.yp_done, GROUPS * n + 2 * r)
                        act.sem_inc(S.passed, 1)
                        for b in range(2):
                            for h in range(CH):
                                nc.scalar.activation(xs[:, b, h, :], x[:, h, bass.ds((2 * r + b) * GPIX, GPIX)], ACT.Identity,
                                                     bias=gn.shift[:, h:h + 1], scale=gn.scale[:, h:h + 1]).then_inc(S.xs_ready, 1)

                    def pair(r, last):
                        for b in range(2):
                            act.wait_ge(S.yp_done, GROUPS * n + 2 * r + b + 1)
                            act.wait_ge(S.split, SPLITS * (GROUPS * n + 2 * r))
                            act.sem_inc(S.passed, 1)
                            nc.scalar.activation(d[:, b, :], yp[:, b], ACT.Identity, bias=co[:, 1:2], scale=co[:, 0:1]).then_inc(S.d_ready, 1)
                        for b in range(2):
                            act.wait_ge(S.d_ready, GROUPS * n + 2 * r + b + 1)
                            nc.scalar.activation(sg[:, b, :], d[:, b, :], ACT.Sigmoid, scale=bn1[:, 6:7]).then_inc(S.sg_ready, 1)
                        if not last:
                            normalise(r + 1)
                        for b in range(2):
                            act.wait_ge(S.split, SPLITS * (GROUPS * n + 2 * r) + 2 + b + 1)
                            act.sem_inc(S.passed, 1)
                            place(copy_act, ym, hi, lower, r, b, S.placed_act)

                    normalise(0)
                    with act.Fori(0, RUNS - 1) as r:
                        pair(r, False)
                    pair(RUNS - 1, True)
                    act.sem_inc(S.passed, 1)
                    with act.Fori(0, 2) as hf:
                        act.wait_ge(S.placed_pool, 2 * BY * GROUPS * (n + 1))
                        act.wait_ge(S.kern_done, (n * 2 + hf) * CH * BANKS)
                        act.sem_inc(S.passed, 1)
                        nc.scalar.activation(yl_half[:], yl[:, :, bass.ds(hf * BLOCKS, BLOCKS)], ACT.Copy).then_inc(S.half_ready, 1)
                        for h in range(CH):
                            unit = (n * 2 + hf) * CH + h
                            act.wait_ge(S.sum_done, unit * SUMS)
                            for k in range(BANKS):
                                if on_act(k):
                                    act.wait_ge(S.kern_done, unit * BANKS + k + 1)
                                    g, at = divmod(4 * k, BPIX)
                                    for j in range(4):
                                        col = (h * GH + g) * BPIX + at + j
                                        nc.scalar.activation(kern[:, g, at + j, :], kp[0:WIN, k % 4, j * BLOCKS:(j + 1) * BLOCKS],
                                                             ACT.Identity, bias=shift[:, col:col + 1]).then_inc(S.kern_read_act, 1)

            @block.vector
            def _(dve):
                chain = Chain(dve, S.chain)
                dve.wait_ge(S.w_loaded, 32)
                dve.wait_ge(S.const, 4)
                chain.link(nc.vector.tensor_reduce(own[:, 0:1], quads[:], AX_X, ALU.add))
                chain.link(nc.vector.tensor_scalar(own[:, 1:2], own[:, 0:1], -1.0, 1.0, ALU.mult, ALU.add))
                gamma, beta, mean, var, p1, p2 = (bn1[:, k:k + 1] for k in range(6))
                s, t, dp = (co[:, k:k + 1] for k in (4, 5, 6))
                chain.link(nc.vector.tensor_scalar(t, var, BN_EPS, None, ALU.add))
                dve.wait_ge(S.root1, 1)
                chain.link(nc.vector.reciprocal(s, s))
                chain.link(nc.vector.tensor_tensor(s, s, gamma, ALU.mult))
                chain.link(nc.vector.tensor_tensor(t, mean, s, ALU.mult))
                chain.link(nc.vector.tensor_tensor(t, beta, t, ALU.subtract))
                chain.link(nc.vector.tensor_tensor(dp, p1, p2, ALU.subtract))
                chain.link(nc.vector.tensor_tensor(co[:, 0:1], dp, s, ALU.mult))
                chain.link(nc.vector.tensor_tensor(co[:, 1:2], dp, t, ALU.mult))
                chain.link(nc.vector.tensor_tensor(co[:, 2:3], p2, s, ALU.mult))
                chain.link(nc.vector.tensor_tensor(co[:, 3:4], p2, t, ALU.mult))
                assert chain.n == COEF
                with dve.Fori(0, IMAGES) as n:
                    chain = Chain(dve, S.chain, n * CHAIN + COEF)
                    dve.wait_ge(S.x_loaded, 16 * CH * (n + 1))
                    gn.dve(nc, dve, chain, n, x, small[:, 0:2 * CH])
                    assert chain.n == CHAIN, chain.n
                    dve.sem_inc(S.passed, 1)
                    with dve.Fori(0, RUNS) as r:
                        done = GROUPS * n + 2 * r
                        for b in range(2):
                            for half in range(2):
                                dve.wait_ge(S.turn_done, 2 * (done + b) + half + 1)
                                dve.wait_ge(patched[b], 32 * (RUNS * n + r))
                                nc.vector.tensor_copy(turned[:, b, 2 * half:2 * half + 2, :], turn_bank(b, half)).then_inc(S.turn_read, 1)
                        for b in range(2):
                            dve.wait_ge(S.d_ready, done + b + 1)
                            dve.wait_ge(S.placed_pool, 2 * BY * done)
                            dve.wait_ge(S.placed_act, BY * done)
                            dve.wait_ge(S.placed_dve, BY * done)
                            dve.sem_inc(S.passed, 1)
                            nc.vector.tensor_scalar(u[:, b, :], yp[:, b], co[:, 2:3], co[:, 3:4], ALU.mult, ALU.add).then_inc(S.u_ready, 1)
                        for b in range(2):
                            dve.wait_ge(S.sg_ready, done + b + 1)
                            nc.vector.tensor_tensor(d[:, b, :], d[:, b, :], sg[:, b, :], ALU.mult).then_inc(S.m_ready, 1)

                        def after(m, b):
                            dve.wait_ge(S.split, SPLITS * done + 2 * (m - 1) + b + 1)

                        for b in range(2):
                            dve.wait_ge(S.m_ready, done + b + 1)
                            dve.wait_ge(S.u_ready, done + b + 1)
                            dve.sem_inc(S.passed, 1)
                            nc.vector.tensor_tensor(u[:, b, :], d[:, b, :], u[:, b, :], ALU.add).then_inc(S.split, 1)
                        for b in range(2):
                            after(1, b)
                            nc.vector.tensor_copy(hi[:, b, :], u[:, b, :]).then_inc(S.split, 1)
                        for b in range(2):
                            after(2, b)
                            nc.vector.tensor_tensor(u[:, b, :], u[:, b, :], hi[:, b, :], ALU.subtract).then_inc(S.split, 1)
                        for b in range(2):
                            after(3, b)
                            nc.vector.tensor_copy(mid[:, b, :], u[:, b, :]).then_inc(S.split, 1)
                        for b in range(2):
                            after(4, b)
                            nc.vector.tensor_tensor(u[:, b, :], u[:, b, :], mid[:, b, :], ALU.subtract).then_inc(S.split, 1)
                        for b in range(2):
                            place(nc.vector.tensor_copy, ym, mid, upper, r, b, S.placed_dve)
                    dve.sem_inc(S.passed, 1)
                    with dve.Fori(0, 2) as hf:
                        dve.wait_ge(S.placed_dve, BY * GROUPS * (n + 1))
                        dve.wait_ge(S.placed_act, BY * GROUPS * (n + 1))
                        dve.wait_ge(S.kern_done, (n * 2 + hf) * CH * BANKS)
                        dve.sem_inc(S.passed, 1)
                        nc.vector.tensor_copy(ym_half[:], ym[:, :, bass.ds(hf * BLOCKS, BLOCKS)]).then_inc(S.half_ready, 1)
                        for h in range(CH):
                            unit = (n * 2 + hf) * CH + h
                            dve.wait_ge(S.sum_done, unit * SUMS)
                            for k in range(BANKS):
                                if not on_act(k):
                                    dve.wait_ge(S.kern_done, unit * BANKS + k + 1)
                                    g, at = divmod(4 * k, BPIX)
                                    col = (h * GH + g) * BPIX + at
                                    nc.vector.tensor_tensor(kern[:, g, at:at + 4, :], kp[0:WIN, k % 4, :].rearrange("p (a b) -> p a b", a=4),
                                                            shift[:, col:col + 4].unsqueeze(2).to_broadcast([WIN, 4, BLOCKS]),
                                                            ALU.add).then_inc(S.kern_read, 1)
                            for k in range(SUMS):
                                dve.wait_ge(S.sum_done, unit * SUMS + k + 1)
                                dve.wait_ge(S.reduced, unit * SUMS + max(k - 1, 0))
                                both = sp_[:, k % 2, :].rearrange("p (a g q) -> p a g q", a=SB, g=TWO)
                                part = masked[:, k % 2, :].rearrange("p (a q) -> p a q", a=SB)
                                nc.vector.tensor_scalar(part, both[:, :, 0, :], own[:, 0:1], None, ALU.mult).then_inc(S.first_read, 1)
                                if k == 0:
                                    dve.wait_ge(S.added, SUMS * unit)
                                dve.wait_ge(S.first_read, unit * SUMS + k + 1)
                                nc.vector.scalar_tensor_tensor(inv[:, SB * k:SB * (k + 1), :], both[:, :, 1, :], own[:, 1:2], part,
                                                               ALU.mult, ALU.add).then_inc(S.reduced, 1)
                                dve.wait_ge(S.reduced, unit * SUMS + k + 1)
                                dve.sem_inc(S.passed, 1)
                                lines = SB // BCOLS * BY * HW
                                half = x[:, h, bass.ds(hf * (PIX // 2) + k * lines, lines)].rearrange("p (a bx rx) -> p a bx rx", bx=BCOLS, rx=BX)
                                src = inv[:, SB * k:SB * (k + 1), :].rearrange("p (by bx) (ry rx) -> p by ry bx rx", bx=BCOLS, ry=BY)
                                for by in range(SB // BCOLS):
                                    dst = half[:, by * BY:(by + 1) * BY]
                                    ins = nc.vector.tensor_tensor(dst, dst, src[:, by], ALU.add)
                                ins.then_inc(S.added, 1)

            @block.tensor
            def _(pe):
                pe.wait_ge(S.w_loaded, 32)
                with pe.Fori(0, IMAGES) as n:
                    gn.pe(nc, pe, n, avg, small[:, 0:2 * CH])
                    pe.sem_inc(S.passed, 1)
                    with pe.Fori(0, RUNS) as r:
                        for b in range(2):
                            pe.wait_ge(S.xs_ready, CH * (GROUPS * n + 2 * r + b + 1))
                            pe.wait_ge(S.u_ready, GROUPS * n + 2 * r)
                            pe.wait_ge(S.d_ready, GROUPS * n + 2 * r)
                            for h in range(CH):
                                mm = nc.tensor.matmul(yp[:, b], w1[:, h, :], xs[:, b, h, :], start=(h == 0), stop=(h == CH - 1))
                            mm.then_inc(S.yp_done, 1)
                        for b in range(2):
                            for half in range(2):
                                pe.wait_ge(S.turn_read, 2 * (GROUPS * n + 2 * r))
                                for t in range(2):
                                    for h in range(CH):
                                        at = (2 * half + t) * P
                                        mm = nc.tensor.transpose(turn_bank(b, half)[:, t, h * P:(h + 1) * P], xs[:, b, h, at:at + P], ident[:])
                                mm.then_inc(S.turn_done, 1)
                    with pe.Fori(0, 2) as hf:
                        pe.wait_ge(S.half_ready, 2 * (n * 2 + hf + 1))
                        for h in range(CH):
                            unit = (n * 2 + hf) * CH + h
                            for k in range(BANKS):
                                copied(pe, unit, k)
                                for j in range(4):
                                    g, at = divmod(4 * k + j, BPIX)
                                    ry, rx = divmod(at, BX)
                                    col = LEAD - ry * WX - rx
                                    for part, (f, v) in enumerate(zip(filts, (ym_half, ym_half, yl_half))):
                                        at_g = (h * GH + g) * FLAT + col
                                        mm = nc.tensor.matmul(kp[0:WIN, k % 4, j * BLOCKS:(j + 1) * BLOCKS], f[:, at_g:at_g + WIN], v[:, at, :],
                                                              start=(part == 0), stop=(part == 2))
                                mm.then_inc(S.kern_done, 1)
                            pe.wait_ge(S.kern_read, (unit + 1) * DVE_BANKS)
                            pe.wait_ge(S.kern_read_act, (unit + 1) * 4 * ACT_BANKS)
                            for k in range(SUMS):
                                q, first = divmod(SB * k, CB)
                                if first == 0:
                                    turns = unit * (CHUNKS // 2) + q // 2 + 1
                                    pe.wait_ge(win_loaded[q % 2], turns * 16 * WY)
                                pe.wait_ge(S.reduced, unit * SUMS + max(k - 1, 0))
                                for j in range(SB):
                                    at = (first + j) // BCOLS * BLINE + (first + j) % BCOLS
                                    for t in range(P // QUAD_CH):
                                        ch = slice(t * QUAD_CH, (t + 1) * QUAD_CH)
                                        mm = nc.tensor.matmul(sp_[ch, k % 2, j * TWO * BPIX:(j + 1) * TWO * BPIX], win[:, q % 2, at, ch],
                                                              kern[:, TWO * t:TWO * (t + 1), :, SB * k + j].rearrange("p g q -> p (g q)"),
                                                              start=True, stop=True)
                                mm.then_inc(S.sum_done, 1)


def stage_filter(nc, D, passed, avg, ident):
    with ExitStack() as ctx:
        a = Alloc(nc, ctx, "u_", passed)
        W1 = HW + 1
        x = a.sb("x", [P, 2, CH, PIX])
        xn = a.sb("xn", [P, 2, CH, W1 * W1])
        f = a.sb("f", [P, CH, 16])
        diag = a.sb("diag", [P, 4, P])
        sums = a.ps("sums", [P, 4, GPIX])
        gn = GroupNorm(a)
        small = a.ps("small", [P, 512])
        loaded = a.sem("loaded")
        x_loaded = [a.sem(f"x_loaded{b}") for b in range(2)]
        stored = [a.sem(f"stored{b}") for b in range(2)]
        chain_sem = a.sem("chain")
        const = a.sem("const")
        normalised = a.sem("normalised")
        tapped = a.sem("tapped")
        done = a.sem("done")
        summed = a.sem("summed")
        sum_added = a.sem("sum_added")
        TAPS4 = [(0, 0), (0, 1), (1, 0), (1, 1)]
        PAIRS_OF_IMAGES = IMAGES // 2

        with nc.Block() as block:
            @block.sync
            def _(sp):
                sp.dma_start(f[:], D["filt"]).then_inc(loaded, 16)
                with sp.Fori(0, PAIRS_OF_IMAGES) as m:
                    for b in range(2):
                        for h in range(CH):
                            sp.wait_ge((done, sum_added)[h], (1, GROUPS)[h] * (2 * m + b + 1))
                            sp.dma_start(D["out"][2 * m + b].rearrange("(h p) q -> p h q", p=P)[:, h], x[:, b, h]).then_inc(stored[b], 16)
                for b in range(2):
                    sp.wait_ge(stored[b], 16 * CH * PAIRS_OF_IMAGES)

            @block.gpsimd
            def _(pool):
                def load(m, b):
                    pool.dma_start(x[:, b], D["x3"][2 * m + b].rearrange("(h p) q -> p h q", p=P)).then_inc(x_loaded[b], 16)

                for b in range(2):
                    load(0, b)
                for b in range(2):
                    nc.gpsimd.memset(xn[:, b], 0.0).then_inc(const, 1)
                with pool.Fori(0, PAIRS_OF_IMAGES - 1) as m:
                    for b in range(2):
                        pool.wait_ge(stored[b], 16 * CH * (m + 1))
                        pool.sem_inc(gn.passed, 1)
                        load(m + 1, b)

            @block.scalar
            def _(act):
                act.wait_ge(const, 2 + len(TAPS4))
                with act.Fori(0, PAIRS_OF_IMAGES) as m:
                    for b in range(2):
                        n = 2 * m + b
                        gn.act(nc, act, n)
                        act.wait_ge(gn.ready, n + 1)
                        act.wait_ge(done, 2 * m)
                        act.wait_ge(sum_added, 2 * GROUPS * m)
                        act.sem_inc(gn.passed, 1)
                        for h in reversed(range(CH)):
                            nc.scalar.activation(xn[:, b, h].rearrange("p (r c) -> p r c", c=W1)[:, 0:HW, 0:HW],
                                                 x[:, b, h].rearrange("p (r c) -> p r c", c=HW), ACT.Identity,
                                                 bias=gn.shift[:, h:h + 1], scale=gn.scale[:, h:h + 1]).then_inc(normalised, 1)

            @block.vector
            def _(dve):
                dve.wait_ge(loaded, 16)
                for k, (dy, dx) in enumerate(TAPS4):
                    at = 4 * (2 * dy + 1) + 2 * dx + 1
                    nc.vector.tensor_scalar(diag[:, k, :], ident[:], f[:, 1, at:at + 1], None, ALU.mult).then_inc(const, 1)
                with dve.Fori(0, PAIRS_OF_IMAGES) as m:
                    for b in range(2):
                        n = 2 * m + b
                        chain = Chain(dve, chain_sem, n * (CH * GROUPS + CH + 6))
                        dve.wait_ge(x_loaded[b], 16 * (m + 1))
                        gn.dve(nc, dve, chain, n, x[:, b], small[:, 0:2 * CH])
                        assert chain.n == CH * GROUPS + CH + 6, chain.n
                    for b in range(2):
                        n = 2 * m + b
                        dve.wait_ge(normalised, CH * (n + 1))
                        xh = x[:, b, 0].rearrange("p (r c) -> p r c", c=HW)
                        for k, (dy, dx) in enumerate(TAPS4):
                            at = 4 * (2 * dy + 1) + 2 * dx + 1
                            src = xn[:, b, 0].rearrange("p (r c) -> p r c", c=W1)[:, dy:dy + HW, dx:dx + HW]
                            ins = nc.vector.scalar_tensor_tensor(xh, src, f[:, 0, at:at + 1], xh, ALU.mult, ALU.add)
                            if k == len(TAPS4) - 1:
                                ins.then_inc(done, 1)
                            else:
                                ins.then_inc(tapped, 1)
                                dve.wait_ge(tapped, n * (len(TAPS4) - 1) + k + 1)
                            for g in (2 * k, 2 * k + 1):
                                dve.wait_ge(summed, n * GROUPS + g + 1)
                                xg = x[:, b, 1, g * GPIX:(g + 1) * GPIX]
                                ins = nc.vector.tensor_tensor(xg, xg, sums[:, g % 4, :], ALU.add)
                                ins.then_inc(sum_added, 1)

            @block.tensor
            def _(pe):
                pe.wait_ge(const, 2 + len(TAPS4))
                with pe.Fori(0, PAIRS_OF_IMAGES) as m:
                    for b in range(2):
                        gn.pe(nc, pe, 2 * m + b, avg, small[:, 0:2 * CH])
                    for b in range(2):
                        n = 2 * m + b
                        pe.wait_ge(normalised, CH * (n + 1))
                        pe.sem_inc(gn.passed, 1)
                        for g in range(GROUPS):
                            if b == 0 and g < 4:
                                pe.wait_ge(sum_added, 2 * m * GROUPS)
                            else:
                                pe.wait_ge(sum_added, n * GROUPS + g - 3)
                            for k, (dy, dx) in enumerate(TAPS4):
                                rows = xn[:, b, 1].rearrange("p (r c) -> p r c", c=W1)[:, g * 8 + dy:g * 8 + dy + 8, dx:dx + HW]
                                mm = nc.tensor.matmul(sums[:, g % 4, :], diag[:, k, :], rows, start=(k == 0), stop=(k == len(TAPS4) - 1))
                            mm.then_inc(summed, 1)


def build_program(nc, D, stages=("0", "1", "2", "3")):
    with ExitStack() as ctx:
        a = Alloc(nc, ctx, "g_")
        avg = a.sb("avg", [P, P])
        ident = a.sb("ident", [P, P])
        passed = a.sem("passed")
        const = a.sem("const")
        with nc.Block() as block:
            @block.gpsimd
            def _(pool):
                chain = Chain(pool, const)
                group_average_matrix(nc, pool, chain, avg)
                identity_matrix(nc, pool, chain, ident)
        if "0" in stages:
            with ExitStack() as ctx0:
                a0 = Alloc(nc, ctx0, "l0_")
                all_idx = a0.sb("idx", [P, IMAGES, TILES * KK], I32)
                all_wt = a0.sb("wt", [P, IMAGES, 4, TILES * KK])
                stage_offsets(nc, D, passed, avg, ident, all_idx, all_wt)
                stage_deform(nc, D, passed, ident, all_idx[:].bitcast(U32), all_wt)
        if "1" in stages:
            stage_attention(nc, D, passed, avg, ident)
        if "2" in stages:
            with ExitStack() as ctx2:
                a2 = Alloc(nc, ctx2, "l2_")
                filts = [a2.sb(f"filt{k}", [P, G2 * FLAT], BF16) for k in range(3)]
                shift = a2.sb("shift", [WIN, G2 * BPIX])
                stage_involution_filters(nc, D, passed, ident, filts, shift)
                stage_involution(nc, D, passed, avg, ident, filts, shift)
        if "3" in stages:
            stage_filter(nc, D, passed, avg, ident)


def layouts(inp):
    import numpy as np

    def put(a):
        return np.ascontiguousarray(a)

    out = {"x": put(inp["x"].reshape(IMAGES, C, PIX))}
    w = inp["L0_conv_conv_offset_w"].reshape(3 * KK, CH, P, KK)
    b = inp["L0_conv_conv_offset_b"]
    w = np.concatenate([w[0:2 * KK:2], w[1:2 * KK:2], w[2 * KK:]])
    b = np.concatenate([b[0:2 * KK:2], b[1:2 * KK:2], b[2 * KK:]])
    w = np.concatenate([w, np.zeros((OM - 3 * KK,) + w.shape[1:], w.dtype)])
    b = np.concatenate([b, np.zeros(OM - 3 * KK, b.dtype)])
    out["w_off"] = put(w.transpose(2, 1, 3, 0))
    out["b_off"] = put(np.tile(b, P // OM).reshape(P, 1))
    out["w_dcn"] = put(inp["L0_conv_dcn_weight"].reshape(C, CH, P, KK).transpose(2, 1, 3, 0))

    def by_partition(v):
        return put(v.reshape(CH, P).T)

    w = inp["L1_conv_w_qkv"].reshape(3, HID, CH, P)
    out["w_qkv"] = put(w.transpose(3, 2, 0, 1))
    out["w_out"] = put(inp["L1_conv_w_out"].reshape(C, PAIRS, P).transpose(2, 1, 0))
    out["g_in"] = by_partition(inp["L1_conv_g_norm"])
    out["g_out"] = by_partition(inp["L1_conv_g_out"])
    out["b_out"] = put(np.broadcast_to(inp["L1_conv_b_out"], (P, C)))

    w = inp["L2_conv_w1"].reshape(MID, CH, P).transpose(2, 1, 0)
    out["w1"] = put(np.concatenate([w, w], axis=2))
    names = ("bn1_gamma", "bn1_beta", "bn1_mean", "bn1_var", "acon_p1", "acon_p2", "acon_beta")
    out["bn1"] = put(np.tile(np.stack([inp["L2_conv_" + k] for k in names], axis=1), (2, 1)))
    out["w2"] = put(inp["L2_conv_w2"].T)
    bn2 = np.stack([inp["L2_conv_bn2_" + k] for k in ("gamma", "beta", "mean", "var")])
    out["bn2"] = put(np.broadcast_to(bn2, (P,) + bn2.shape))
    out["filt"] = put(inp["L3_conv_filt"].reshape(CH, P, 16).transpose(1, 0, 2))
    return out


SCRATCH = {
    "table": (IMAGES * QROWS, 2 * C),
    "x1": (IMAGES, C, PIX),
    "x2": (IMAGES, C, PIX),
    "patch": (IMAGES, 2 * PLANE, C),
    "x3": (IMAGES, C, PIX),
}


def kernel(**inputs):
    import numpy as np
    from concourse import bacc
    from concourse.bass_utils import run_bass_kernel_spmd

    nc = bacc.Bacc("TRN2", target_bir_lowering=False, num_devices=1)
    arrays = layouts(inputs)
    D = {k: nc.dram_tensor("in_" + k, v.shape, F32, kind="ExternalInput").ap() for k, v in arrays.items()}
    for k, shape in SCRATCH.items():
        D[k] = nc.dram_tensor(k, shape, F32, kind="Internal").ap()
    D["out"] = nc.dram_tensor("out", (IMAGES, C, PIX), F32, kind="ExternalOutput").ap()
    build_program(nc, D)
    r = run_bass_kernel_spmd(nc, [{"in_" + k: v for k, v in arrays.items()}], core_ids=[0])
    return r.results[0]["out"].reshape(IMAGES, C, HW, HW)
```
